# Optimizing a Trainium2 kernel written in Bass

```python
import numpy as np
import jax
import jax.numpy as jnp

def _softmax(x, axis=-1):
    return jax.nn.softmax(x, axis=axis)

def _gelu(x):
    return jax.nn.gelu(x, approximate=True)

def _silu(x):
    return jax.nn.silu(x)

def _sigmoid(x):
    return jax.nn.sigmoid(x)

def _layernorm(x, axis=-1, eps=1e-05):
    m = jnp.mean(x, axis=axis, keepdims=True)
    v = jnp.var(x, axis=axis, keepdims=True)
    return (x - m) / jnp.sqrt(v + eps)

def _scatter_add(tgt, idx, src, axis=0):
    return tgt.at[idx].add(src)

def _segment_sum(src, seg, n):
    return jax.ops.segment_sum(src, seg, n)
kernel_name = 'mk_vit_tower_d1_tok_img256_r4_15f1fb'

def setup_inputs(seed: int=0):
    np.random.seed(seed)
    _w = jnp.asarray

    def _rec_inputs():
        import jax
        import jax.numpy as jnp
        _rk = jax.random.key(seed)
        x = -0.00040386 + 0.999972 * jax.random.normal(jax.random.fold_in(_rk, 1), (128, 128, 64, 3), jnp.float32)
        return x
    x = _rec_inputs()

    def _L0_tok_setup():
        import jax, jax.numpy as jnp
        import numpy as np
        B, T, J, LAT = (128, 128, 64, 64)
        EPS = 1e-05

        def layernorm(x, g, b):
            m = jnp.mean(x, axis=-1, keepdims=True)
            v = jnp.var(x, axis=-1, keepdims=True)
            return (x - m) * jax.lax.rsqrt(v + EPS) * g + b

        def conv2d(x, w, b, pad):
            y = jax.lax.conv_general_dilated(x, w, window_strides=(1, 1), padding=pad, dimension_numbers=('NCHW', 'OIHW', 'NCHW'))
            return y + b[None, :, None, None]
        key = jax.random.key(seed)
        ks = jax.random.split(key, 10)
        s = 0.02
        return {'x': jax.random.normal(ks[0], (B, T, J, 3), dtype=jnp.float32), 'ln0_g': jnp.ones((J * 3,), jnp.float32), 'ln0_b': jnp.zeros((J * 3,), jnp.float32), 'ln1_g': jnp.ones((J * 2,), jnp.float32), 'ln1_b': jnp.zeros((J * 2,), jnp.float32), 'conv1_w': jax.random.normal(ks[1], (T, T, 5, 3), jnp.float32) * s, 'conv1_b': jnp.zeros((T,), jnp.float32), 'conv2_w': jax.random.normal(ks[2], (T, T, 5, 2), jnp.float32) * s, 'conv2_b': jnp.zeros((T,), jnp.float32), 'conv3_w': jax.random.normal(ks[3], (2 * T, T, 5, 2), jnp.float32) * s, 'conv3_b': jnp.zeros((2 * T,), jnp.float32), 'out_w': jax.random.normal(ks[4], (2 * J, LAT), jnp.float32) * s, 'out_b': jnp.zeros((LAT,), jnp.float32)}
    _L0_tok_all = _L0_tok_setup()
    _L0_tok_in = {k: v for k, v in _L0_tok_all.items() if k in ('ln0_g', 'ln0_b', 'ln1_g', 'ln1_b', 'conv1_w', 'conv1_b', 'conv2_w', 'conv2_b', 'conv3_w', 'conv3_b', 'out_w', 'out_b')}
    del _L0_tok_all

    def _L0_attn_setup():
        import jax, jax.numpy as jnp
        import numpy as np
        B, N, DIM = (8, 2048, 64)
        HEADS, LOCAL_HEADS, WINDOW = (8, 1, 64)
        HD = DIM // HEADS
        MLP_HIDDEN = 256
        EPS = 1e-05

        def layer_norm(x, g, b):
            mu = jnp.mean(x, axis=-1, keepdims=True)
            var = jnp.var(x, axis=-1, keepdims=True)
            return (x - mu) * jax.lax.rsqrt(var + EPS) * g + b

        def look_around(t, pad_value=0.0):
            nw = t.shape[1]
            pads = [(0, 0), (1, 1)] + [(0, 0)] * (t.ndim - 2)
            p = jnp.pad(t, pads, constant_values=pad_value)
            return jnp.concatenate([p[:, i:i + nw] for i in range(3)], axis=2)

        def local_attn(q, k, v):
            b, n, d = q.shape
            nw = n // WINDOW
            scale = d ** (-0.5)
            bq = q.reshape(b, nw, WINDOW, d) * scale
            bk = look_around(k.reshape(b, nw, WINDOW, d))
            bv = look_around(v.reshape(b, nw, WINDOW, d))
            ticker = jnp.arange(n).reshape(1, nw, WINDOW)
            bq_k = look_around(ticker, pad_value=-1)
            pad_mask = (bq_k == -1)[:, :, None, :]
            dots = jnp.einsum('bnie,bnje->bnij', bq, bk)
            dots = jnp.where(pad_mask, -1000000000.0, dots)
            attn = jax.nn.softmax(dots, axis=-1)
            out = jnp.einsum('bnij,bnje->bnie', attn, bv)
            return out.reshape(b, n, d)

        def linear_attn(q, k, v):
            d = q.shape[-1]
            qs = jax.nn.softmax(q, axis=-1) * d ** (-0.5)
            ks = jax.nn.softmax(k, axis=-2)
            ctx = jnp.einsum('bhnd,bhne->bhde', ks, v)
            return jnp.einsum('bhnd,bhde->bhne', qs, ctx)
        key = jax.random.key(seed)
        ks = jax.random.split(key, 8)
        s = 0.02
        return {'x': jax.random.normal(ks[0], (B, N, DIM), jnp.float32), 'norm1_g': jnp.ones((DIM,), jnp.float32), 'norm1_b': jnp.zeros((DIM,), jnp.float32), 'Wq': jax.random.normal(ks[1], (DIM, DIM), jnp.float32) * s, 'Wkv': jax.random.normal(ks[2], (DIM, DIM), jnp.float32) * s, 'Wproj': jax.random.normal(ks[3], (DIM, DIM), jnp.float32) * s, 'bproj': jnp.zeros((DIM,), jnp.float32), 'norm2_g': jnp.ones((DIM,), jnp.float32), 'norm2_b': jnp.zeros((DIM,), jnp.float32), 'W1': jax.random.normal(ks[4], (MLP_HIDDEN, DIM), jnp.float32) * s, 'b1': jnp.zeros((MLP_HIDDEN,), jnp.float32), 'W2': jax.random.normal(ks[5], (DIM, MLP_HIDDEN), jnp.float32) * s, 'b2': jnp.zeros((DIM,), jnp.float32)}
    _L0_attn_all = _L0_attn_setup()
    _L0_attn_in = {k: v for k, v in _L0_attn_all.items() if k in ('norm1_g', 'norm1_b', 'Wq', 'Wkv', 'Wproj', 'bproj', 'norm2_g', 'norm2_b', 'W1', 'b1', 'W2', 'b2')}
    del _L0_attn_all

    def _L0_ffn_setup():
        import jax, jax.numpy as jnp
        import numpy as np
        B, N, D = (16, 1024, 64)
        NUM_EXPERTS, TOP_K, HEADS = (4, 2, 4)
        N_EDGES = 262144
        LN_EPS = 1e-05

        def _layernorm(x, g, b):
            mu = x.mean(-1, keepdims=True)
            var = ((x - mu) ** 2).mean(-1, keepdims=True)
            return (x - mu) * jax.lax.rsqrt(var + LN_EPS) * g + b

        def _forward(x, edge_index, W_gat, att_src, att_dst, b_gat, ln_gamma, ln_beta, W1, b1, W2, b2):
            Bc, Nc, Dc = x.shape
            M = Bc * Nc
            x_flat = x.reshape(M, Dc)
            h = (x_flat @ W_gat).reshape(M, HEADS, NUM_EXPERTS)
            loops = jnp.arange(M, dtype=edge_index.dtype)
            src = jnp.concatenate([edge_index[0], loops])
            dst = jnp.concatenate([edge_index[1], loops])
            a_src = (h * att_src).sum(-1)
            a_dst = (h * att_dst).sum(-1)
            e = jax.nn.leaky_relu(a_src[src] + a_dst[dst], negative_slope=0.2)
            e_max = jax.ops.segment_max(e, dst, num_segments=M)
            ee = jnp.exp(e - e_max[dst])
            denom = jax.ops.segment_sum(ee, dst, num_segments=M)
            alpha = ee / (denom[dst] + 1e-16)
            msg = h[src] * alpha[:, :, None]
            agg = jax.ops.segment_sum(msg, dst, num_segments=M).reshape(M, HEADS * NUM_EXPERTS) + b_gat
            scores = _layernorm(agg, ln_gamma, ln_beta).reshape(M, HEADS, NUM_EXPERTS).mean(1)
            scores = scores.reshape(Bc, Nc, NUM_EXPERTS)
            topk_s, topk_i = jax.lax.top_k(scores, TOP_K)
            w = jax.nn.softmax(topk_s, axis=-1)
            out = jnp.zeros_like(x)
            for ei in range(NUM_EXPERTS):
                g = jnp.where(topk_i == ei, w, 0.0).sum(-1)
                hh = jax.nn.gelu(x @ W1[ei] + b1[ei], approximate=False)
                out = out + g[..., None] * (hh @ W2[ei] + b2[ei])
            return out
        key = jax.random.key(seed)
        ks = jax.random.split(key, 8)
        s = 0.05
        return {'x': jax.random.normal(ks[0], (B, N, D), jnp.float32), 'W_gat': jax.random.normal(ks[1], (D, HEADS * NUM_EXPERTS), jnp.float32) * s, 'att_src': jax.random.normal(ks[2], (HEADS, NUM_EXPERTS), jnp.float32) * s, 'att_dst': jax.random.normal(ks[3], (HEADS, NUM_EXPERTS), jnp.float32) * s, 'b_gat': jnp.zeros((HEADS * NUM_EXPERTS,), jnp.float32), 'ln_gamma': jnp.ones((HEADS * NUM_EXPERTS,), jnp.float32), 'ln_beta': jnp.zeros((HEADS * NUM_EXPERTS,), jnp.float32), 'W1': jax.random.normal(ks[4], (NUM_EXPERTS, D, 2 * D), jnp.float32) * s, 'b1': jnp.zeros((NUM_EXPERTS, 2 * D), jnp.float32), 'W2': jax.random.normal(ks[5], (NUM_EXPERTS, 2 * D, D), jnp.float32) * s, 'b2': jnp.zeros((NUM_EXPERTS, D), jnp.float32), 'edge_index': jax.random.randint(ks[6], (2, N_EDGES), 0, B * N, jnp.int32)}
    _L0_ffn_all = _L0_ffn_setup()
    _L0_ffn_in = {k: v for k, v in _L0_ffn_all.items() if k in ('W_gat', 'att_src', 'att_dst', 'b_gat', 'ln_gamma', 'ln_beta', 'W1', 'b1', 'W2', 'b2', 'edge_index')}
    del _L0_ffn_all
    return {'x': x, 'L0_tok_ln0_g': _L0_tok_in['ln0_g'], 'L0_tok_ln0_b': _L0_tok_in['ln0_b'], 'L0_tok_ln1_g': _L0_tok_in['ln1_g'], 'L0_tok_ln1_b': _L0_tok_in['ln1_b'], 'L0_tok_conv1_w': _L0_tok_in['conv1_w'], 'L0_tok_conv1_b': _L0_tok_in['conv1_b'], 'L0_tok_conv2_w': _L0_tok_in['conv2_w'], 'L0_tok_conv2_b': _L0_tok_in['conv2_b'], 'L0_tok_conv3_w': _L0_tok_in['conv3_w'], 'L0_tok_conv3_b': _L0_tok_in['conv3_b'], 'L0_tok_out_w': _L0_tok_in['out_w'], 'L0_tok_out_b': _L0_tok_in['out_b'], 'L0_attn_norm1_g': _L0_attn_in['norm1_g'], 'L0_attn_norm1_b': _L0_attn_in['norm1_b'], 'L0_attn_Wq': _L0_attn_in['Wq'], 'L0_attn_Wkv': _L0_attn_in['Wkv'], 'L0_attn_Wproj': _L0_attn_in['Wproj'], 'L0_attn_bproj': _L0_attn_in['bproj'], 'L0_attn_norm2_g': _L0_attn_in['norm2_g'], 'L0_attn_norm2_b': _L0_attn_in['norm2_b'], 'L0_attn_W1': _L0_attn_in['W1'], 'L0_attn_b1': _L0_attn_in['b1'], 'L0_attn_W2': _L0_attn_in['W2'], 'L0_attn_b2': _L0_attn_in['b2'], 'L0_ffn_W_gat': _L0_ffn_in['W_gat'], 'L0_ffn_att_src': _L0_ffn_in['att_src'], 'L0_ffn_att_dst': _L0_ffn_in['att_dst'], 'L0_ffn_b_gat': _L0_ffn_in['b_gat'], 'L0_ffn_ln_gamma': _L0_ffn_in['ln_gamma'], 'L0_ffn_ln_beta': _L0_ffn_in['ln_beta'], 'L0_ffn_W1': _L0_ffn_in['W1'], 'L0_ffn_b1': _L0_ffn_in['b1'], 'L0_ffn_W2': _L0_ffn_in['W2'], 'L0_ffn_b2': _L0_ffn_in['b2'], 'L0_ffn_edge_index': _L0_ffn_in['edge_index']}

def reference(x, L0_tok_ln0_g, L0_tok_ln0_b, L0_tok_ln1_g, L0_tok_ln1_b, L0_tok_conv1_w, L0_tok_conv1_b, L0_tok_conv2_w, L0_tok_conv2_b, L0_tok_conv3_w, L0_tok_conv3_b, L0_tok_out_w, L0_tok_out_b, L0_attn_norm1_g, L0_attn_norm1_b, L0_attn_Wq, L0_attn_Wkv, L0_attn_Wproj, L0_attn_bproj, L0_attn_norm2_g, L0_attn_norm2_b, L0_attn_W1, L0_attn_b1, L0_attn_W2, L0_attn_b2, L0_ffn_W_gat, L0_ffn_att_src, L0_ffn_att_dst, L0_ffn_b_gat, L0_ffn_ln_gamma, L0_ffn_ln_beta, L0_ffn_W1, L0_ffn_b1, L0_ffn_W2, L0_ffn_b2, L0_ffn_edge_index):
    import jax
    import jax.numpy as jnp

    def _L0_tok_ref(x, ln0_g, ln0_b, ln1_g, ln1_b, conv1_w, conv1_b, conv2_w, conv2_b, conv3_w, conv3_b, out_w, out_b):
        import jax, jax.numpy as jnp
        import numpy as np
        B, T, J, LAT = (128, 128, 64, 64)
        EPS = 1e-05

        def layernorm(x, g, b):
            m = jnp.mean(x, axis=-1, keepdims=True)
            v = jnp.var(x, axis=-1, keepdims=True)
            return (x - m) * jax.lax.rsqrt(v + EPS) * g + b

        def conv2d(x, w, b, pad):
            y = jax.lax.conv_general_dilated(x, w, window_strides=(1, 1), padding=pad, dimension_numbers=('NCHW', 'OIHW', 'NCHW'))
            return y + b[None, :, None, None]
        b, t, j, d = x.shape
        h = layernorm(x.reshape(b, t, j * 3), ln0_g, ln0_b).reshape(b, t, j, 3)
        h = jax.nn.relu(conv2d(h, conv1_w, conv1_b, ((2, 2), (1, 1))))
        h = layernorm(h.reshape(b, t, j * 3), ln0_g, ln0_b).reshape(b, t, j, 3)
        h = jax.nn.relu(conv2d(h, conv2_w, conv2_b, ((2, 2), (0, 0))))
        h = layernorm(h.reshape(b, t, j * 2), ln1_g, ln1_b).reshape(b, t, j, 2)
        h = jax.nn.relu(conv2d(h, conv3_w, conv3_b, ((2, 2), (0, 0))))
        h = h.reshape(b, 2 * t, j)
        res = jnp.concatenate([h[:, :t, :], h[:, t:, :]], axis=2)
        res = layernorm(res, ln1_g, ln1_b)
        return res @ out_w + out_b

    def _L0_attn_ref(x, norm1_g, norm1_b, Wq, Wkv, Wproj, bproj, norm2_g, norm2_b, W1, b1, W2, b2):
        import jax, jax.numpy as jnp
        import numpy as np
        B, N, DIM = (8, 2048, 64)
        HEADS, LOCAL_HEADS, WINDOW = (8, 1, 64)
        HD = DIM // HEADS
        MLP_HIDDEN = 256
        EPS = 1e-05

        def layer_norm(x, g, b):
            mu = jnp.mean(x, axis=-1, keepdims=True)
            var = jnp.var(x, axis=-1, keepdims=True)
            return (x - mu) * jax.lax.rsqrt(var + EPS) * g + b

        def look_around(t, pad_value=0.0):
            nw = t.shape[1]
            pads = [(0, 0), (1, 1)] + [(0, 0)] * (t.ndim - 2)
            p = jnp.pad(t, pads, constant_values=pad_value)
            return jnp.concatenate([p[:, i:i + nw] for i in range(3)], axis=2)

        def local_attn(q, k, v):
            b, n, d = q.shape
            nw = n // WINDOW
            scale = d ** (-0.5)
            bq = q.reshape(b, nw, WINDOW, d) * scale
            bk = look_around(k.reshape(b, nw, WINDOW, d))
            bv = look_around(v.reshape(b, nw, WINDOW, d))
            ticker = jnp.arange(n).reshape(1, nw, WINDOW)
            bq_k = look_around(ticker, pad_value=-1)
            pad_mask = (bq_k == -1)[:, :, None, :]
            dots = jnp.einsum('bnie,bnje->bnij', bq, bk)
            dots = jnp.where(pad_mask, -1000000000.0, dots)
            attn = jax.nn.softmax(dots, axis=-1)
            out = jnp.einsum('bnij,bnje->bnie', attn, bv)
            return out.reshape(b, n, d)

        def linear_attn(q, k, v):
            d = q.shape[-1]
            qs = jax.nn.softmax(q, axis=-1) * d ** (-0.5)
            ks = jax.nn.softmax(k, axis=-2)
            ctx = jnp.einsum('bhnd,bhne->bhde', ks, v)
            return jnp.einsum('bhnd,bhde->bhne', qs, ctx)
        b, n, c = x.shape
        h = layer_norm(x, norm1_g, norm1_b)
        q = h @ Wq.T
        kv = h @ Wkv.T
        split_heads = lambda t: t.reshape(b, n, HEADS, HD).transpose(0, 2, 1, 3)
        q, k, v = (split_heads(q), split_heads(kv), split_heads(kv))
        lq, gq = (q[:, :LOCAL_HEADS], q[:, LOCAL_HEADS:])
        lk, gk = (k[:, :LOCAL_HEADS], k[:, LOCAL_HEADS:])
        lv, gv = (v[:, :LOCAL_HEADS], v[:, LOCAL_HEADS:])
        lout = local_attn(lq.reshape(b * LOCAL_HEADS, n, HD), lk.reshape(b * LOCAL_HEADS, n, HD), lv.reshape(b * LOCAL_HEADS, n, HD)).reshape(b, LOCAL_HEADS, n, HD)
        gout = linear_attn(gq, gk, gv)
        attn = jnp.concatenate([lout, gout], axis=1)
        y = attn.transpose(0, 2, 1, 3).reshape(b, n, c) @ Wproj.T + bproj
        x = x + y
        h2 = layer_norm(x, norm2_g, norm2_b)
        m = jax.nn.gelu(h2 @ W1.T + b1, approximate=False) @ W2.T + b2
        return x + m

    def _L0_ffn_ref(x, W_gat, att_src, att_dst, b_gat, ln_gamma, ln_beta, W1, b1, W2, b2, edge_index):
        import jax, jax.numpy as jnp
        import numpy as np
        B, N, D = (16, 1024, 64)
        NUM_EXPERTS, TOP_K, HEADS = (4, 2, 4)
        N_EDGES = 262144
        LN_EPS = 1e-05

        def _layernorm(x, g, b):
            mu = x.mean(-1, keepdims=True)
            var = ((x - mu) ** 2).mean(-1, keepdims=True)
            return (x - mu) * jax.lax.rsqrt(var + LN_EPS) * g + b

        def _forward(x, edge_index, W_gat, att_src, att_dst, b_gat, ln_gamma, ln_beta, W1, b1, W2, b2):
            Bc, Nc, Dc = x.shape
            M = Bc * Nc
            x_flat = x.reshape(M, Dc)
            h = (x_flat @ W_gat).reshape(M, HEADS, NUM_EXPERTS)
            loops = jnp.arange(M, dtype=edge_index.dtype)
            src = jnp.concatenate([edge_index[0], loops])
            dst = jnp.concatenate([edge_index[1], loops])
            a_src = (h * att_src).sum(-1)
            a_dst = (h * att_dst).sum(-1)
            e = jax.nn.leaky_relu(a_src[src] + a_dst[dst], negative_slope=0.2)
            e_max = jax.ops.segment_max(e, dst, num_segments=M)
            ee = jnp.exp(e - e_max[dst])
            denom = jax.ops.segment_sum(ee, dst, num_segments=M)
            alpha = ee / (denom[dst] + 1e-16)
            msg = h[src] * alpha[:, :, None]
            agg = jax.ops.segment_sum(msg, dst, num_segments=M).reshape(M, HEADS * NUM_EXPERTS) + b_gat
            scores = _layernorm(agg, ln_gamma, ln_beta).reshape(M, HEADS, NUM_EXPERTS).mean(1)
            scores = scores.reshape(Bc, Nc, NUM_EXPERTS)
            topk_s, topk_i = jax.lax.top_k(scores, TOP_K)
            w = jax.nn.softmax(topk_s, axis=-1)
            out = jnp.zeros_like(x)
            for ei in range(NUM_EXPERTS):
                g = jnp.where(topk_i == ei, w, 0.0).sum(-1)
                hh = jax.nn.gelu(x @ W1[ei] + b1[ei], approximate=False)
                out = out + g[..., None] * (hh @ W2[ei] + b2[ei])
            return out
        return _forward(x, edge_index, W_gat, att_src, att_dst, b_gat, ln_gamma, ln_beta, W1, b1, W2, b2)
    h = _L0_tok_ref(x, L0_tok_ln0_g, L0_tok_ln0_b, L0_tok_ln1_g, L0_tok_ln1_b, L0_tok_conv1_w, L0_tok_conv1_b, L0_tok_conv2_w, L0_tok_conv2_b, L0_tok_conv3_w, L0_tok_conv3_b, L0_tok_out_w, L0_tok_out_b)
    h = h + _L0_attn_ref(_layernorm(h, axis=-1), L0_attn_norm1_g, L0_attn_norm1_b, L0_attn_Wq, L0_attn_Wkv, L0_attn_Wproj, L0_attn_bproj, L0_attn_norm2_g, L0_attn_norm2_b, L0_attn_W1, L0_attn_b1, L0_attn_W2, L0_attn_b2)
    h = h + _L0_ffn_ref(_layernorm(h, axis=-1), L0_ffn_W_gat, L0_ffn_att_src, L0_ffn_att_dst, L0_ffn_b_gat, L0_ffn_ln_gamma, L0_ffn_ln_beta, L0_ffn_W1, L0_ffn_b1, L0_ffn_W2, L0_ffn_b2, L0_ffn_edge_index)
    return h

_drawn_inputs = setup_inputs


def setup_inputs(seed=0):
    import zlib

    import numpy as np

    out = dict(_drawn_inputs(seed))
    spreads = {'L0_tok_ln0_g': (1.0, 0.2),
     'L0_tok_ln0_b': (0.0, 0.1),
     'L0_tok_ln1_g': (1.0, 0.2),
     'L0_tok_ln1_b': (0.0, 0.1),
     'L0_tok_conv1_b': (0.0, 0.1),
     'L0_tok_conv2_b': (0.0, 0.1),
     'L0_tok_conv3_b': (0.0, 0.1),
     'L0_tok_out_b': (0.0, 0.1),
     'L0_attn_norm1_g': (1.0, 0.6),
     'L0_attn_norm1_b': (0.0, 0.8),
     'L0_attn_bproj': (0.0, 0.1),
     'L0_attn_norm2_g': (1.0, 0.6),
     'L0_attn_norm2_b': (0.0, 2.0),
     'L0_attn_b1': (0.0, 0.496),
     'L0_attn_b2': (0.0, 0.1),
     'L0_ffn_b_gat': (0.0, 0.295),
     'L0_ffn_ln_gamma': (1.0, 0.6),
     'L0_ffn_ln_beta': (0.0, 1.826),
     'L0_ffn_b1': (0.0, 0.421),
     'L0_ffn_b2': (0.0, 0.1)}
    factors = {'L0_attn_Wq': 8.0,
     'L0_attn_Wkv': 8.0,
     'L0_attn_Wproj': 8.0,
     'L0_ffn_att_src': 200.0,
     'L0_ffn_att_dst': 200.0,
     'L0_ffn_W_gat': 3.941}
    for name, (base, spread) in spreads.items():
        noise = np.random.default_rng([zlib.crc32(name.encode()), seed]).standard_normal(out[name].shape)
        drawn = base * np.exp(spread * noise) if base else spread * noise
        out[name] = jnp.asarray(drawn.astype(out[name].dtype))
    for name, factor in factors.items():
        out[name] = (out[name] * factor).astype(out[name].dtype)
    return out
```

```python
import numpy as np
import concourse.bass as bass
from concourse import mybir
from contextlib import ExitStack

F32 = mybir.dt.float32
I32 = mybir.dt.int32
U32 = mybir.dt.uint32
BF16 = mybir.dt.bfloat16
ALU = mybir.AluOpType
ACT = mybir.ActivationFunctionType
AX = mybir.AxisListType

B, T, J, D = 128, 128, 64, 3
LAT = 64
NODES = B * T
EDGES = 262144
KH = 5
JP = J + KH - 1
GB = 8
G = B // GB
EP = EDGES // 128
EPS = 1e-5
NEG = -1.0e30
LOG_EP = EP.bit_length() - 1
LOG_E = EDGES.bit_length() - 1
NODE_BITS = NODES.bit_length() - 1
KEY_TOP = 1 << (2 * NODE_BITS)


class Names:

    def __init__(self, nc, ctx, stage):
        self.nc, self.ctx, self.stage, self.sems = nc, ctx, stage, {}

    def sem(self, name):
        if name not in self.sems:
            self.sems[name] = self.nc.alloc_semaphore(f"{self.stage}_{name}")
        return self.sems[name]

    def release(self):
        self.nc.all_engine_barrier()
        self.nc.clear_and_free_semaphores(list(self.sems.values()))
        self.nc.all_engine_barrier()

    def sb(self, name, shape, dtype=F32):
        return self.ctx.enter_context(self.nc.sbuf_tensor(name, shape, dtype))

    def ps(self, name, shape, dtype=F32):
        return self.ctx.enter_context(self.nc.psum_tensor(name, shape, dtype))


def after(engine, sem, value):
    if not isinstance(value, int) or value > 0:
        engine.wait_ge(sem, value)


def sign_of_level(k):
    p = np.arange(128)
    if k < LOG_EP or k == LOG_E:
        return np.ones(128)
    return 1.0 - 2.0 * ((p >> (k - LOG_EP)) & 1)


def constants():
    p = np.arange(128)
    head = (p % LAT) // 8
    same = (p[:, None] // LAT == p[None, :] // LAT) & (head[:, None] == head[None, :]) & (head[:, None] > 0)
    return {
        "c_ident": np.eye(128, dtype=np.float32),
        "c_sign": np.stack([sign_of_level(k - 1) * sign_of_level(k) for k in range(LOG_EP, LOG_E + 1)], 1).astype(np.float32),
        "c_headmask": same.astype(np.float32),
        "c_upto": (p[:, None] <= p[None, :]).astype(np.float32),
        "c_rowpos": (p * EP).astype(np.float32)[:, None],
        "c_ones": np.ones((128, 128), np.float32),
        "c_ramp": np.tile(p.astype(np.float32), (128, 1)),
    }


def tokenizer_and_sort(nc, d, keys, res):
    ctx = ExitStack()
    with ctx:
        n = Names(nc, ctx, "tok")
        S = n.sem
        w1 = n.sb("w_conv1", [128, KH, 3, 128])
        w2 = n.sb("w_conv2", [128, KH, 2, 128])
        w3 = n.sb("w_conv3", [128, KH, 2, 2, 128])
        cb = n.sb("conv_bias", [128, 4])
        g0 = n.sb("ln0_gain", [128, D * J])
        b0 = n.sb("ln0_shift", [128, D * J])
        g1 = n.sb("ln1_gain", [128, 2, 2 * J])
        b1 = n.sb("ln1_shift", [128, 2, 2 * J])
        sgn = n.sb("sort_signs", [128, LOG_E - LOG_EP + 1])
        xraw = [n.sb(f"x_raw{i}", [128, GB, D * J]) for i in range(2)]
        y0 = [n.sb(f"conv1_in{i}", [128, GB, D, JP]) for i in range(2)]
        y1 = [n.sb(f"conv2_in{i}", [128, GB, D, JP]) for i in range(2)]
        y2 = [n.sb(f"conv3_in{i}", [128, GB, 2, JP]) for i in range(2)]
        r = [xraw, n.sb("relu1", [128, GB, D * J]), n.sb("relu2", [128, GB, 2 * J]), n.sb("relu3", [128, GB, 2 * J])]
        dump = [n.sb(f"act_dump{k}", [128, GB, w], BF16) for k, w in enumerate((D * J, D * J, 2 * J, 2 * J))]
        dump_x = n.sb("act_dump_x", [128, GB, D * J], BF16)
        stat = [n.sb(f"stat{k}", [128, 6, GB]) for k in range(4)]
        sum3 = n.sb("sum3_half", [128, GB])
        half = n.sb("minus_half", [128, GB])
        eps = n.sb("eps", [128, GB])
        inv = n.sb("inverse_width", [128, 4, GB])
        minus_inv = n.sb("minus_inverse_width", [128, 4, GB])
        c1 = n.ps("conv1_out", [128, D, GB * J])
        c2 = n.ps("conv2_out", [128, 2, GB * J])
        c3 = n.ps("conv3_out", [128, 2, GB * J])
        block = ctx.enter_context(nc.Block())

        widths = (D * J, D * J, 2 * J, 2 * J)

        exchanges = []
        count = [0]
        cur = [0]

        @block.vector
        def _(dve):
            def did(i):
                i.then_inc(S("sort"), 1)
                count[0] += 1

            def stage(level, j):
                dve.wait_ge(S("sort"), count[0])
                A, Bk = keys[cur[0]], keys[1 - cur[0]]
                if level < LOG_EP:
                    pat, kw = "p (g r m h d) -> p r h g m d", dict(r=2, m=2 ** (level - 1 - j), h=2, d=2 ** j)
                    a, b = A[:, :].rearrange(pat, **kw), Bk[:, :].rearrange(pat, **kw)
                    for up in range(2):
                        for h in range(2):
                            did(nc.vector.tensor_tensor(b[:, up, h], a[:, up, 0], a[:, up, 1], ALU.min if up == h else ALU.max))
                else:
                    pat, kw = "p (m h d) -> p h m d", dict(h=2, d=2 ** j)
                    a, b = A[:, :].rearrange(pat, **kw), Bk[:, :].rearrange(pat, **kw)
                    for h in range(2):
                        did(nc.vector.tensor_tensor(b[:, h], a[:, 0], a[:, 1], ALU.max if h else ALU.min))
                cur[0] ^= 1

            def transpose():
                dve.wait_ge(S("sort"), count[0])
                did(nc.vector.transpose(keys[1 - cur[0]][:, :], keys[cur[0]][:, :]))
                cur[0] ^= 1

            def turn(col):
                dve.wait_ge(S("sort"), count[0])
                did(nc.vector.tensor_scalar(keys[1 - cur[0]][:, :], keys[cur[0]][:, :], sgn[:, col:col + 1], None, ALU.mult))
                cur[0] ^= 1

            def exchange(bits):
                exchanges.append((count[0], cur[0], bits))
                dve.wait_ge(S("exchanged"), 16 * sum((4 >> b) << (2 * b) for _, _, b in exchanges))
                cur[0] ^= 1

            dve.wait_ge(S("keys_in"), 48)
            dst, src = keys[0][:, :].bitcast(I32), keys[1][:, :].bitcast(I32)
            did(nc.vector.tensor_scalar(dst, dst, NODE_BITS, None, ALU.logical_shift_left))
            dve.wait_ge(S("sort"), count[0])
            did(nc.vector.tensor_tensor(src, dst, src, ALU.bitwise_or))
            dve.wait_ge(S("sort"), count[0])
            did(nc.vector.tensor_scalar(src, src, KEY_TOP, None, ALU.bitwise_or))
            cur[0] = 1
            for level in range(1, LOG_E + 1):
                if level >= LOG_EP:
                    turn(level - LOG_EP)
                quadrant_bits = max(0, level - 16)
                if quadrant_bits:
                    exchange(quadrant_bits)
                    for j in range(quadrant_bits - 1, -1, -1):
                        stage(level + LOG_EP, LOG_EP - quadrant_bits + j)
                if level > LOG_EP:
                    transpose()
                    for j in range(min(level, 16) - LOG_EP - 1, -1, -1):
                        stage(level + LOG_EP, j)
                    transpose()
                if quadrant_bits:
                    exchange(quadrant_bits)
                for j in range(min(level, LOG_EP) - 1, -1, -1):
                    stage(level, j)

        @block.sync
        def _(sp):
            sp.dma_start(keys[0][:, :].bitcast(I32), d["edges"][1].rearrange("(p f) -> p f", p=128)).then_inc(S("keys_in"), 16)
            sp.dma_start(keys[1][:, :].bitcast(I32), d["edges"][0].rearrange("(p f) -> p f", p=128)).then_inc(S("keys_in"), 16)
            sp.dma_start(sgn[:, :], d["c_sign"]).then_inc(S("keys_in"), 16)
            sp.dma_start(w1[:, :, :, :], d["conv1_w"]).then_inc(S("w_in"), 16)
            sp.dma_start(w2[:, :, :, :], d["conv2_w"]).then_inc(S("w_in"), 16)
            sp.dma_start(w3[:, :, :, :, :], d["conv3_w"]).then_inc(S("w_in"), 16)
            for count, src, bits in exchanges:
                sp.wait_ge(S("sort"), count)
                A, Bk = keys[src], keys[1 - src]
                w = EP >> bits
                for top in range(4 >> bits):
                    for f in range(1 << bits):
                        for p in range(1 << bits):
                            to, at = 32 * ((top << bits) + f), 32 * ((top << bits) + p)
                            sp.dma_start(Bk[to:to + 32, p * w:(p + 1) * w], A[at:at + 32, f * w:(f + 1) * w]).then_inc(S("exchanged"), 16)

        FIRST, LOOP0, PAIRS, LAST0, END = -1, 4, (G - 6) // 2, G - 2, G + 2

        @block.tensor
        def _(pe):
            pe.wait_ge(S("w_in"), 48)

            def conv(k, g, par, src, w, out, taps):
                pe.wait_ge(S(f"y{k}_ready"), g + 1)
                after(pe, S(f"sum{k + 1}"), g)
                for bank, cols in taps:
                    for i, (dd, kh, wt) in enumerate(cols):
                        m = nc.tensor.matmul(out[:, bank, :].rearrange("p (b j) -> p b j", j=J), wt,
                                             src[par][:, :, dd, kh:kh + J], start=(i == 0), stop=(i == len(cols) - 1))
                m.then_inc(S(f"conv{k}_done"), 1)

            taps0 = [(o, [(o + kw - 1, kh, w1[:, kh, kw, :]) for kw in range(3) if 0 <= o + kw - 1 < D for kh in range(KH)]) for o in range(D)]
            taps1 = [(o, [(o + kw, kh, w2[:, kh, kw, :]) for kw in range(2) for kh in range(KH)]) for o in range(2)]
            taps2 = [(h, [(kw, kh, w3[:, kh, kw, h, :]) for kw in range(2) for kh in range(KH)]) for h in range(2)]

            def step(s, par, a, b, c):
                if a:
                    conv(0, s, par, y0, w1, c1, taps0)
                if b:
                    conv(1, s - 1, 1 - par, y1, w2, c2, taps1)
                if c:
                    conv(2, s - 2, par, y2, w3, c3, taps2)

            for s in range(0, LOOP0):
                step(s, s % 2, True, s >= 1, s >= 2)
            with pe.Fori(0, PAIRS) as i:
                for par in range(2):
                    step(2 * i + (LOOP0 + par), par, True, True, True)
            for s in range(LAST0, END):
                step(s, s % 2, s < G, s - 1 < G, True)

        @block.scalar
        def _(act):
            act.dma_start(cb[:, :], d["conv_b"]).then_inc(S("act_w_in"), 16)

            def load(g, par):
                act.dma_start(xraw[par][:, :, :], d["x"][:, bass.ds(g * GB, GB), :]).then_inc(S(f"x_in{par}"), 16)

            def sums(k, g, par):
                after(act, S("res_ready" if k == 3 else f"y{k}_ready"), g)
                if k == 0:
                    act.wait_ge(S(f"x_in{par}"), 8 * (g - par) + 16)
                else:
                    act.wait_ge(S(f"conv{k - 1}_done"), g + 1)
                for b in range(GB):
                    if k == 0:
                        o = act.activation(dump_x[:, b, :], xraw[par][:, b, :], ACT.Identity, accum_out=stat[0][:, 0, b:b + 1])
                    elif k < 3:
                        c = (None, c1, c2)[k]
                        w = widths[k] // J
                        o = act.activation(r[k][:, b, :].rearrange("p (d j) -> p d j", j=J), c[:, 0:w, b * J:(b + 1) * J],
                                           ACT.Relu, bias=cb[:, k - 1:k], accum_out=stat[k][:, 0, b:b + 1])
                    else:
                        for h in range(2):
                            o = act.activation(r[3][:, b, h * J:(h + 1) * J], c3[:, h, b * J:(b + 1) * J], ACT.Relu,
                                               bias=cb[:, 2 + h:3 + h], accum_out=(sum3 if h else stat[3][:, 0])[:, b:b + 1])
                o.then_inc(S(f"sum{k}"), 1)

            def squares(k, g, par):
                act.wait_ge(S(f"mean{k}"), g + 1)
                src = r[0][par] if k == 0 else r[k]
                for b in range(GB):
                    o = act.activation(dump[k][:, b, :], src[:, b, :], ACT.Square, bias=stat[k][:, 1, b:b + 1],
                                       accum_out=stat[k][:, 2, b:b + 1])
                o.then_inc(S(f"sq{k}"), 1)

            def normalise(k, g, par):
                act.wait_ge(S(f"scaled_mean{k}"), g + 1)
                src = r[0][par] if k == 0 else r[k]
                for b in range(GB):
                    o = act.activation(src[:, b, :], src[:, b, :], ACT.Identity, scale=stat[k][:, 4, b:b + 1], bias=stat[k][:, 5, b:b + 1])
                o.then_inc(S(f"norm{k}"), 1)

            def step(s, par, n0, n1, n2, n3):
                if n0:
                    sums(0, s + 1, 1 - par)
                    squares(0, s + 1, 1 - par)
                    normalise(0, s + 1, 1 - par)
                if n1:
                    sums(1, s, par)
                    squares(1, s, par)
                    normalise(1, s, par)
                if n2:
                    sums(2, s - 1, 1 - par)
                    squares(2, s - 1, 1 - par)
                    normalise(2, s - 1, 1 - par)
                if n3:
                    sums(3, s - 2, par)
                    squares(3, s - 2, par)
                    normalise(3, s - 2, par)

            load(0, 0)
            load(1, 1)
            act.wait_ge(S("act_w_in"), 16)

            def load_ahead(s, par):
                act.wait_ge(S("y0_ready"), s + 2)
                load(s + 3, 1 - par)

            for s in range(FIRST, LOOP0):
                step(s, s % 2, True, s >= 0, s >= 1, s >= 2)
                load_ahead(s, s % 2)
            with act.Fori(0, PAIRS - 1) as i:
                for par in range(2):
                    step(2 * i + (LOOP0 + par), par, True, True, True, True)
                    load_ahead(2 * i + (LOOP0 + par), par)
            for s in range(LAST0 - 2, END):
                step(s, s % 2, s + 1 < G, s < G, s - 1 < G, True)
                if s + 3 < G:
                    load_ahead(s, s % 2)

        @block.gpsimd
        def _(pool):
            pool.dma_start(g0[:, :], d["ln0_g"].partition_broadcast(128)).then_inc(S("pool_in"), 16)
            pool.dma_start(b0[:, :], d["ln0_b"].partition_broadcast(128)).then_inc(S("pool_in"), 16)
            for v in range(2):
                pool.dma_start(g1[:, v, :], d[f"ln1_g{v}"].partition_broadcast(128)).then_inc(S("pool_in"), 16)
                pool.dma_start(b1[:, v, :], d[f"ln1_b{v}"].partition_broadcast(128)).then_inc(S("pool_in"), 16)
            for y in (*y0, *y1, *y2):
                pool.memset(y[:, :, :, :].rearrange("p b d j -> p (b d j)"), 0.0).then_inc(S("zeroed"), 1)
            pool.memset(half[:, :], -0.5).then_inc(S("zeroed"), 1)
            pool.memset(eps[:, :], EPS).then_inc(S("zeroed"), 1)
            for k in range(4):
                pool.memset(inv[:, k, :], 1.0 / widths[k]).then_inc(S("zeroed"), 1)
                pool.memset(minus_inv[:, k, :], -1.0 / widths[k]).then_inc(S("zeroed"), 1)
            pool.wait_ge(S("zeroed"), 16)
            pool.wait_ge(S("pool_in"), 96)

            def mean(k, g):
                pool.wait_ge(S(f"sum{k}"), g + 1)
                total = stat[k][:, 0, :]
                if k == 3:
                    nc.gpsimd.tensor_tensor(stat[3][:, 3, :], total, sum3[:, :], ALU.add).then_inc(S("sum3_both"), 1)
                    pool.wait_ge(S("sum3_both"), g + 1)
                    total = stat[3][:, 3, :]
                nc.gpsimd.tensor_tensor(stat[k][:, 1, :], total, minus_inv[:, k, :], ALU.mult).then_inc(S(f"mean{k}"), 1)

            def deviation(k, g):
                pool.wait_ge(S(f"sq{k}"), g + 1)
                st = stat[k]
                nc.gpsimd.tensor_tensor(st[:, 3, :], st[:, 2, :], inv[:, k, :], ALU.mult).then_inc(S(f"var{k}"), 1)
                pool.wait_ge(S(f"var{k}"), g + 1)
                nc.gpsimd.tensor_tensor(st[:, 3, :], st[:, 3, :], eps[:, :], ALU.add).then_inc(S(f"vareps{k}"), 1)
                pool.wait_ge(S(f"vareps{k}"), g + 1)
                nc.gpsimd.tensor_tensor(st[:, 4, :], st[:, 3, :], half[:, :], ALU.pow).then_inc(S(f"std{k}"), 1)
                pool.wait_ge(S(f"std{k}"), g + 1)
                nc.gpsimd.tensor_tensor(st[:, 5, :], st[:, 1, :], st[:, 4, :], ALU.mult).then_inc(S(f"scaled_mean{k}"), 1)

            def affine(k, g, par, gain):
                pool.wait_ge(S(f"norm{k}"), g + 1)
                src = r[0][par] if k == 0 else r[k]
                nc.gpsimd.tensor_tensor(src[:, :, :], src[:, :, :], wide(k, gain), ALU.mult).then_inc(S(f"gain{k}"), 1)
                pool.wait_ge(S(f"gain{k}"), g + 1)
                return src

            def wide(k, v):
                return v.unsqueeze(1).broadcast_to([128, GB, widths[k]])

            def layer(k, g, par, gain, shift, out):
                mean(k, g)
                deviation(k, g)
                src, sh = affine(k, g, par, gain), wide(k, shift)
                if k < 3:
                    after(pool, S(f"conv{k}_done"), g - 1)
                    for dd in range(widths[k] // J):
                        o = nc.gpsimd.tensor_tensor(out[par][:, :, dd, KH // 2:KH // 2 + J], src[:, :, dd * J:(dd + 1) * J],
                                            sh[:, :, dd * J:(dd + 1) * J], ALU.add)
                    o.then_inc(S(f"y{k}_ready"), 1)
                else:
                    nc.gpsimd.tensor_tensor(res[:, bass.ds(g * GB, GB), :], src[:, :, :], sh, ALU.add).then_inc(S("res_ready"), 1)

            def step(s, par, n0, n1, n2, n3):
                if n0:
                    layer(0, s + 1, 1 - par, g0[:, :], b0[:, :], y0)
                if n1:
                    layer(1, s, par, g0[:, :], b0[:, :], y1)
                if n2:
                    layer(2, s - 1, 1 - par, g1[:, 0, :], b1[:, 0, :], y2)
                if n3:
                    layer(3, s - 2, par, g1[:, 1, :], b1[:, 1, :], None)

            for s in range(FIRST, LOOP0):
                step(s, s % 2, True, s >= 0, s >= 1, s >= 2)
            with pool.Fori(0, PAIRS) as i:
                for par in range(2):
                    step(2 * i + (LOOP0 + par), par, True, True, True, True)
            for s in range(LAST0, END):
                step(s, s % 2, s + 1 < G, s < G, s - 1 < G, True)
    n.release()
    return cur[0]


def attention(nc, d, res):
    ctx = ExitStack()
    with ctx:
        n = Names(nc, ctx, "attn")
        S = n.sem
        P2, PC = GB // 2, GB // 2 * 128
        ident = n.sb("ident", [128, 128])
        headmask = n.sb("headmask", [128, 128])
        w_out = n.sb("w_out", [128, LAT])
        w_qkv = n.sb("w_qkv", [128, 2, 128])
        w_qkv_g = n.sb("w_qkv_g", [128, 2, 128])
        w_proj = n.sb("w_proj", [128, 128])
        w_1 = n.sb("w_mlp1", [128, 256])
        w_1g = n.sb("w_mlp1_g", [128, 256])
        w_2 = n.sb("w_mlp2", [128, 2, LAT])
        w_gat = n.sb("w_gat", [128, 16])
        w_att = n.sb("w_att", [128, 2, 16])
        w_node = n.sb("w_node", [128, 2, 24])
        att_tmp = n.sb("att_tmp", [128, 2, 16])
        cols = n.sb("norm_cols", [128, 6])
        out_b = n.sb("out_b", [128, LAT])
        proj_b = n.sb("proj_b", [128, LAT])
        mlp_b = n.sb("mlp_b", [128, LAT])
        qkv_b = n.sb("qkv_bias", [128, 2, 128])
        qk_bc = n.sb("qk_bias_cols", [128, 2])
        hid_b = n.sb("hidden_bias", [128, 2])
        shift1 = n.sb("shift1_wide", [128, 128])
        con = n.sb("minus_one_half", [128, 1, GB])
        resg = [n.sb(f"res_group{i}", [128, GB, 128]) for i in range(2)]
        resT = n.sb("resT", [128, GB * 128])
        cenA = n.sb("cenA", [128, GB, LAT])
        sqA = n.sb("sqA", [128, GB, LAT])
        nA = n.sb("nA", [128, GB, LAT])
        ub = [n.sb(f"u_plus_bias{i}", [128, GB, LAT]) for i in range(2)]
        nT = [n.sb(f"nT{i}", [128, PC]) for i in range(2)]
        stA = n.sb("statA", [128, 6, GB])
        qkv = n.sb("qkv", [128, 2, GB, LAT])
        kvT = n.sb("kvT", [128, PC])
        qT = n.sb("qT", [128, PC])
        nkmax = n.sb("minus_kmax", [128, P2])
        ET = n.sb("expkT", [128, PC])
        ksum = n.sb("ksum", [128, P2])
        rks = n.sb("one_over_ksum", [128, P2])
        E = n.sb("expk", [128, PC])
        ctx2 = n.sb("context", [128, P2, 128])
        qmax = n.sb("qmax", [128, GB, 7])
        qexp = n.sb("qexp", [128, GB, 7, 8])
        qsum = n.sb("qsum", [128, GB, 7])
        qs = n.sb("qsoft", [128, GB, LAT])
        qsT = n.sb("qsoftT", [128, PC])
        ndmax = n.sb("minus_dots_max", [128, 2, GB])
        prob = n.sb("prob", [128, GB, 128])
        psm = n.sb("prob_sum", [128, 2, GB])
        probT = n.sb("probT", [128, GB * 128])
        O = n.sb("attn_out", [128, GB, LAT])
        OT = n.sb("attn_outT", [128, PC])
        x1 = [n.sb(f"x1_{i}", [128, GB, LAT]) for i in range(2)]
        cenC = n.sb("cenC", [128, GB, LAT])
        sqC = n.sb("sqC", [128, GB, LAT])
        n2T = n.sb("n2T", [128, PC])
        stC = n.sb("statC", [128, 5, GB])
        hx = n.sb("h_plus_x1", [128, GB, LAT])
        h = [n.sb(f"h_{i}", [128, GB, LAT]) for i in range(2)]
        hnew = [n.sb(f"h_new{i}", [128, GB, LAT]) for i in range(2)]
        hid = n.sb("hidden", [128, 2, 2, PC])
        zTg = n.sb("zT_group", [128, PC])
        tabg = [n.sb(f"table_group{i}", [128, GB, 24]) for i in range(2)]

        B01 = n.ps("bank01", [128, 1024])
        B2 = n.ps("bank2", [128, 512])
        B34 = n.ps("bank34", [128, 1024])
        B5 = n.ps("bank5", [128, 512])
        B6 = n.ps("bank6", [128, 512])
        B7 = n.ps("bank7", [128, 512])
        block = ctx.enter_context(nc.Block())
        SCALE = 8 ** -0.5

        def group(ap):
            return ap.rearrange("p (b c) -> p b c", c=LAT)

        def wide(stat):
            return stat.unsqueeze(2).broadcast_to([128, GB, LAT])

        def over(row):
            return row.unsqueeze(1).broadcast_to([128, GB, LAT])

        def rows(ap, g):
            return ap[:, bass.ds(g * GB, GB), :]

        FIRST, LOOP0, PAIRS, LAST0, END = 0, 4, (G - 4) // 2, G, G + 2

        def run(engine, step):
            for s in range(FIRST, LOOP0):
                step(s, s % 2, True, s >= 1, s >= 2)
            with engine.Fori(0, PAIRS) as i:
                for par in range(2):
                    step(2 * i + (LOOP0 + par), par, True, True, True)
            for s in range(LAST0, END):
                step(s, s % 2, False, s - 1 < G, True)

        @block.sync
        def _(sp):
            for t, name in ((ident, "c_ident"), (headmask, "c_headmask"), (w_out, "out_w"), (w_proj, "w_proj"),
                            (w_1, "w_mlp1"), (w_gat, "w_gat"), (cols, "norm_cols")):
                sp.dma_start(t[:, :], d[name]).then_inc(S("w_in"), 16)
            sp.dma_start(w_2[:, :, :], d["w_mlp2"]).then_inc(S("w_in"), 16)
            sp.dma_start(w_qkv[:, :, :], d["w_qkv"]).then_inc(S("w_in"), 16)
            for t, name in ((out_b, "out_b"), (proj_b, "proj_b"), (mlp_b, "mlp_b")):
                sp.dma_start(t[:, :], d[name].partition_broadcast(128)).then_inc(S("w_in"), 16)
            for k in range(2):
                sp.dma_start(w_att[:, k, :], d[f"att{k}"].partition_broadcast(128)).then_inc(S("w_in"), 16)

            def fetch(g, par):
                sp.dma_start(resg[par][:, :, :], rows(res, g)).then_inc(S(f"res_in{par}"), 16)

            fetch(0, 0)
            fetch(1, 1)

            def step(s, par, a, b, c):
                if a:
                    sp.wait_ge(S("resT_ps"), s + 1)
                    if not isinstance(s, int) or s + 2 < G:
                        fetch(s + 2, par)
                if c:
                    g = s - 2
                    sp.wait_ge(S("hnew"), g + 1)
                    sp.dma_start(d["h2"][:, bass.ds(g * GB * LAT, GB * LAT)], hnew[par][:, :, :].rearrange("p b c -> p (b c)")).then_inc(S(f"h_out{par}"), 16)
                    sp.wait_ge(S("zT"), g + 1)
                    sp.dma_start(d["zT"][:, bass.ds(g * PC, PC)], zTg[:, :]).then_inc(S("zT_out"), 16)
                    sp.wait_ge(S("table"), g + 1)
                    for name, cut in (("node_src", slice(0, 20)), ("node_dst", slice(20, 24))):
                        sp.dma_start(d[name].rearrange("(b t) c -> t b c", t=128)[:, bass.ds(g * GB, GB), :], tabg[par][:, :, cut])\
                          .then_inc(S(f"table_out{par}"), 16)

            for s in range(FIRST, LOOP0):
                step(s, s % 2, True, s >= 1, s >= 2)
            with sp.Fori(0, PAIRS - 1) as i:
                for par in range(2):
                    step(2 * i + (LOOP0 + par), par, True, True, True)
            for s in range(LAST0 - 2, END):
                step(s, s % 2, s < G, s - 1 < G, True)
            sp.wait_ge(S("zT_out"), 16 * G)
            for par in range(2):
                sp.wait_ge(S(f"table_out{par}"), 32 * (G // 2))
                sp.wait_ge(S(f"h_out{par}"), 16 * (G // 2))

        @block.tensor
        def _(pe):
            mm, tr = nc.tensor.matmul, nc.tensor.transpose
            one = dict(start=True, stop=True)
            pe.wait_ge(S("w_in"), 16 * 14)
            pe.wait_ge(S("w_ready"), 1)
            for k in range(2):
                mm(B7[:, 128 * k:128 * k + 128], shift1[:, :], w_qkv[:, k, :], **one)
                mm(B7[:, 256 + k:257 + k], w_qkv[:, k, :], cols[:, 1:2], **one)
            for m in range(2):
                last = mm(B6[:, m:m + 1], w_1[0:LAT, 128 * m:128 * (m + 1)], cols[0:LAT, 3:4], **one)
            last.then_inc(S("bias_ps"), 1)
            pe.wait_ge(S("bias_sb"), 1)

            def sample(b):
                return slice(LAT * (b % 2), LAT * (b % 2) + LAT), slice(128 * (b // 2), 128 * (b // 2) + 128)

            def slot(b):
                k = GB // 2 * (b % 2) + b // 2
                return slice(128 * k, 128 * k + 128)

            def pair_columns(p):
                return slice(128 * p, 128 * p + 128)

            def hidden_layer(k):
                m, i = k // 2, k % 2
                half = slice(LAT * i, LAT * (i + 1))
                return mm(B01[:, 512 * i:512 * i + 512], w_1g[half, 128 * m:128 * m + 128], n2T[half, :], **one)

            def step(s, par, a, b_, c):
                A, B, C = s, s - 1, s - 2
                if b_:
                    pe.wait_ge(S("nT"), B + 1)
                    after(pe, S("x1"), B)
                    mm(B5[:, :], w_qkv_g[:, 1, :], nT[1 - par][:, :], **one).then_inc(S("kvT_ps"), 1)
                if a:
                    pe.wait_ge(S(f"res_in{par}"), 8 * (A - par) + 16)
                    after(pe, S("gelu"), A - 2)
                    after(pe, S("resT_sb"), A)
                    for b in range(GB):
                        m = tr(B01[:, 128 * b:128 * b + 128], resg[par][:, b, :], ident[:, :])
                    m.then_inc(S("resT_ps"), 1)
                if b_:
                    pe.wait_ge(S("nT"), B + 1)
                    after(pe, S("probT_sb"), B)
                    for k in range(2):
                        for p in range(P2):
                            m = mm(B34[:, 512 * k + 128 * p:512 * k + 128 * p + 128], nT[1 - par][:, pair_columns(p)], w_qkv_g[:, k, :], **one)
                    m.then_inc(S("qkv_ps"), 1)
                    after(pe, S("OT_sb"), B)
                    mm(B6[:, :], w_qkv_g[:, 0, :], nT[1 - par][:, :], **one).then_inc(S("qT_ps"), 1)
                if a:
                    pe.wait_ge(S("resT_sb"), A + 1)
                    after(pe, S("nT"), A)
                    for b in range(GB):
                        m = mm(B2[:, LAT * b:LAT * b + LAT], resT[:, 128 * b:128 * b + 128], w_out[:, :], **one)
                    m.then_inc(S("h_ps"), 1)
                if c:
                    pe.wait_ge(S("n2"), C + 1)
                    after(pe, S("table"), C)
                    for p in range(P2):
                        m = tr(B7[:, pair_columns(p)], cenC[:, 2 * p:2 * p + 2, :].rearrange("t b c -> t (b c)"), ident[:, :])
                    m.then_inc(S("n2T_ps"), 1)
                if b_:
                    pe.wait_ge(S("ET"), B + 1)
                    for p in range(P2):
                        m = tr(B5[:, pair_columns(p)], ET[:, pair_columns(p)], ident[:, :])
                    m.then_inc(S("E_ps"), 1)
                if c:
                    pe.wait_ge(S("n2T_sb"), C + 1)
                    after(pe, S("resT_sb"), A + 1 if a else 0)
                    hidden_layer(0).then_inc(S("hid_ps0"), 1)
                    pe.wait_ge(S("n2T_sb"), C + 1)
                    after(pe, S("resT_sb"), A + 1 if a else 0)
                    hidden_layer(1).then_inc(S("hid_ps1"), 1)
                if b_:
                    pe.wait_ge(S("qT_sb"), B + 1)
                    pe.wait_ge(S("kvT_sb"), B + 1)
                    pe.wait_ge(S("qkv_sb"), B + 1)
                    for b in range(GB):
                        half, pc = sample(b)
                        head0 = slice(half.start, half.start + 8)
                        m = mm(B34[:, slot(b)], qT[head0, pc], kvT[head0, pc], **one)
                    m.then_inc(S("dots"), 1)
                if c:
                    pe.wait_ge(S("gelu_chunk0"), C + 1)
                    hidden_layer(2).then_inc(S("hid_ps2"), 1)
                    pe.wait_ge(S("gelu_chunk1"), C + 1)
                    hidden_layer(3).then_inc(S("hid_ps3"), 1)
                if b_:
                    pe.wait_ge(S("E_sb"), B + 1)
                    pe.wait_ge(S("qkv_sb"), B + 1)
                    for p in range(P2):
                        m = mm(B5[:, pair_columns(p)].rearrange("p (i c) -> p i c", i=2), E[:, pair_columns(p)], qkv[:, 1, 2 * p:2 * p + 2, :], **one)
                    m.then_inc(S("ctx_ps"), 1)
                if c:
                    for k in (2, 3):
                        pe.wait_ge(S("gelu" if k == 3 else f"gelu_chunk{k}"), C + 1)
                    for b in range(GB):
                        _, pc = sample(b)
                        for m_ in range(2):
                            m = mm(B7[:, LAT * b:LAT * b + LAT], hid[:, m_, b % 2, pc], w_2[:, m_, :], start=m_ == 0, stop=m_ == 1)
                    m.then_inc(S("mlp_ps"), 1)
                if b_:
                    pe.wait_ge(S("qs"), B + 1)
                    pe.wait_ge(S("ctx_sb"), B + 1)
                    for p in range(P2):
                        m = tr(B5[:, pair_columns(p)], qs[:, 2 * p:2 * p + 2, :].rearrange("t b c -> t (b c)"), ident[:, :])
                    m.then_inc(S("qsT_ps"), 1)
                    pe.wait_ge(S("prob"), B + 1)
                    for b in range(GB):
                        m = tr(B34[:, slot(b)], prob[:, slot(b).start // 128, :], ident[:, :])
                    m.then_inc(S("probT_ps"), 1)
                    pe.wait_ge(S("qsT_sb"), B + 1)
                    for p in range(P2):
                        m = mm(B5[:, pair_columns(p)], qsT[:, pair_columns(p)], ctx2[:, p, :], **one)
                    m.then_inc(S("global_ps"), 1)
                if a:
                    pe.wait_ge(S("nA"), A + 1)
                    for p in range(P2):
                        m = tr(B2[:, pair_columns(p)], nA[:, 2 * p:2 * p + 2, :].rearrange("t b c -> t (b c)"), ident[:, :])
                    m.then_inc(S("nT_ps"), 1)
                if b_:
                    pe.wait_ge(S("probT_sb"), B + 1)
                    for b in range(GB):
                        k = slot(b).start // 128
                        m = mm(B6[:, 8 * k:8 * k + 8], probT[:, slot(b)], qkv[:, 1, b, 0:8], **one)
                    m.then_inc(S("local_ps"), 1)
                    pe.wait_ge(S("O"), B + 1)
                    for p in range(P2):
                        m = tr(B6[:, pair_columns(p)], O[:, 2 * p:2 * p + 2, :].rearrange("t b c -> t (b c)"), ident[:, :])
                    m.then_inc(S("OT_ps"), 1)
                if c:
                    pe.wait_ge(S("z"), C + 1)
                    for p in range(P2):
                        m = tr(B7[:, pair_columns(p)], cenC[:, 2 * p:2 * p + 2, :].rearrange("t b c -> t (b c)"), ident[:, :])
                    m.then_inc(S("zT_ps"), 1)
                if b_:
                    pe.wait_ge(S("OT_sb"), B + 1)
                    for p in range(P2):
                        m = mm(B5[:, pair_columns(p)], OT[:, pair_columns(p)], w_proj[:, :], **one)
                    m.then_inc(S("proj_ps"), 1)
                if c:
                    pe.wait_ge(S("zT"), C + 1)
                    for p in range(P2):
                        m = mm(B7[:, 48 * p:48 * p + 48], zTg[:, pair_columns(p)], w_node[:, :, :].rearrange("p i c -> p (i c)"), **one)
                    m.then_inc(S("table_ps"), 1)

            run(pe, step)

        @block.scalar
        def _(act):
            copy = lambda o, i: act.activation(o, i, ACT.Copy)
            act.wait_ge(S("bias_sb"), 1)

            def gelu(k, C):
                m, i = k // 2, k % 2
                act.wait_ge(S(f"hid_ps{k}"), C + 1)
                act.activation(hid[:, m, i, :], B01[:, 512 * i:512 * i + 512], ACT.Gelu, bias=hid_b[:, m:m + 1])\
                   .then_inc(S("gelu" if k == 3 else f"gelu_chunk{k}"), 1)

            def step(s, par, a, b_, c):
                A, B, C = s, s - 1, s - 2
                if c:
                    act.wait_ge(S("cenC"), 2 * C + 1)
                    act.activation(sqC[:, :, :], cenC[:, :, :], ACT.Square).then_inc(S("sqC"), 1)
                if b_:
                    act.wait_ge(S("kvT_ps"), B + 1)
                    act.activation(kvT[:, :], B5[:, :], ACT.Identity, bias=qk_bc[:, 1:2]).then_inc(S("kvT_sb"), 1)
                if a:
                    act.wait_ge(S("resT_ps"), A + 1)
                    copy(resT[:, :], B01[:, :]).then_inc(S("resT_sb"), 1)
                if b_:
                    act.wait_ge(S("nkmax"), B + 1)
                    act.wait_ge(S("kvT_sb"), B + 1)
                    for p in range(P2):
                        m = act.activation(ET[:, 128 * p:128 * p + 128], kvT[:, 128 * p:128 * p + 128], ACT.Exp,
                                           bias=nkmax[:, p:p + 1], accum_out=ksum[:, p:p + 1])
                    m.then_inc(S("ET"), 1)
                if c:
                    act.wait_ge(S("n2T_ps"), C + 1)
                    copy(n2T[:, :], B7[:, :]).then_inc(S("n2T_sb"), 1)
                if b_:
                    act.wait_ge(S("E_ps"), B + 1)
                    copy(E[:, :], B5[:, :]).then_inc(S("E_sb"), 1)
                    act.wait_ge(S("qT_ps"), B + 1)
                    act.activation(qT[:, :], B6[:, :], ACT.Identity, bias=qk_bc[:, 0:1]).then_inc(S("qT_sb"), 1)
                if c:
                    gelu(0, C)
                    gelu(1, C)
                if a:
                    act.wait_ge(S("cenA"), A + 1)
                    act.activation(sqA[:, :, :], cenA[:, :, :], ACT.Square).then_inc(S("sqA"), 1)
                if c:
                    gelu(2, C)
                    gelu(3, C)
                if b_:
                    act.wait_ge(S("qc"), B + 1)
                    act.activation(qexp[:, :, :, :], qexp[:, :, :, :], ACT.Exp).then_inc(S("qexp"), 1)
                    act.wait_ge(S("ndmax"), B + 1)
                    for b in range(GB):
                        m = act.activation(prob[:, b, :], B34[:, 128 * b:128 * b + 128], ACT.Exp, scale=SCALE,
                                           bias=ndmax[:, 1, b:b + 1], accum_out=psm[:, 0, b:b + 1])
                    m.then_inc(S("prob"), 1)
                    act.wait_ge(S("qsT_ps"), B + 1)
                    copy(qsT[:, :], B5[:, :]).then_inc(S("qsT_sb"), 1)
                if c:
                    act.wait_ge(S("cenC"), 2 * C + 2)
                    act.activation(sqC[:, :, :], cenC[:, :, :], ACT.Square).then_inc(S("sqZ"), 1)
                if b_:
                    act.wait_ge(S("probT_ps"), B + 1)
                    copy(probT[:, :], B34[:, :]).then_inc(S("probT_sb"), 1)
                if a:
                    act.wait_ge(S("nT_ps"), A + 1)
                    copy(nT[par][:, :], B2[:, :]).then_inc(S("nT"), 1)
                if b_:
                    act.wait_ge(S("OT_ps"), B + 1)
                    copy(OT[:, :], B6[:, :]).then_inc(S("OT_sb"), 1)
                if c:
                    act.wait_ge(S("zT_ps"), C + 1)
                    after(act, S("zT_out"), 16 * C)
                    copy(zTg[:, :], B7[:, :]).then_inc(S("zT"), 1)

            run(act, step)

        @block.gpsimd
        def _(pool):
            tt = nc.gpsimd.tensor_tensor
            pool.memset(con[:, :, :].rearrange("p k b -> p (k b)"), -0.5).then_inc(S("pool_ready"), 1)
            pool.memset(qs[:, :, :].rearrange("p b c -> p (b c)"), 0.0).then_inc(S("pool_ready"), 1)
            pool.wait_ge(S("w_in"), 16 * 14)
            pool.wait_ge(S("pool_ready"), 2)
            half = con[:, 0, :]

            def step(s, par, a, b_, c):
                A, B, C = s, s - 1, s - 2
                if c:
                    pool.wait_ge(S("x1"), C + 1)
                    after(pool, S("hnew"), C)
                    tt(hx[:, :, :], h[par][:, :, :], x1[par][:, :, :], ALU.add).then_inc(S("hx0"), 1)
                    pool.wait_ge(S("varC"), C + 1)
                    tt(stC[:, 4, :], stC[:, 2, :], half, ALU.pow).then_inc(S("rstdC"), 1)
                    pool.wait_ge(S("rstdC"), C + 1)
                    tt(cenC[:, :, :], cenC[:, :, :], wide(stC[:, 4, :]), ALU.mult).then_inc(S("n2"), 1)
                if b_:
                    pool.wait_ge(S("qmax"), B + 1)
                    q = qkv[:, 0, :, 8:LAT].rearrange("p b (h d) -> p b h d", d=8)
                    tt(qexp[:, :, :, :], q, qmax[:, :, :].unsqueeze(3).broadcast_to([128, GB, 7, 8]), ALU.subtract).then_inc(S("qc"), 1)
                if a:
                    pool.wait_ge(S("varA"), 2 * A + 2)
                    tt(stA[:, 4, :], stA[:, 2, :], half, ALU.pow).then_inc(S("rstdA1"), 1)
                    pool.wait_ge(S("varA"), 2 * A + 2)
                    tt(stA[:, 5, :], stA[:, 3, :], half, ALU.pow).then_inc(S("rstdA"), 1)
                    pool.wait_ge(S("rstdA"), A + 1)
                    after(pool, S("nT_ps"), A)
                    tt(nA[:, :, :], cenA[:, :, :], wide(stA[:, 5, :]), ALU.mult).then_inc(S("nA"), 1)
                if c:
                    pool.wait_ge(S("hx0"), C + 1)
                    tt(hx[:, :, :], hx[:, :, :], over(mlp_b[:, :]), ALU.add).then_inc(S("hx"), 1)
                if b_:
                    pool.wait_ge(S("qrec"), B + 1)
                    o = qs[:, :, 8:LAT].rearrange("p b (h d) -> p b h d", d=8)
                    tt(o, qexp[:, :, :, :], qsum[:, :, :].unsqueeze(3).broadcast_to([128, GB, 7, 8]), ALU.mult).then_inc(S("qs"), 1)
                if a:
                    pool.wait_ge(S("rstdA1"), A + 1)
                    tt(ub[par][:, :, :], cenA[:, :, :], wide(stA[:, 4, :]), ALU.mult).then_inc(S("u"), 1)
                if c:
                    pool.wait_ge(S("varZ"), C + 1)
                    tt(stC[:, 4, :], stC[:, 2, :], half, ALU.pow).then_inc(S("rstdZ"), 1)
                    pool.wait_ge(S("rstdZ"), C + 1)
                    tt(cenC[:, :, :], cenC[:, :, :], wide(stC[:, 4, :]), ALU.mult).then_inc(S("z"), 1)
                if a:
                    pool.wait_ge(S("u"), A + 1)
                    tt(ub[par][:, :, :], ub[par][:, :, :], over(proj_b[:, :]), ALU.add).then_inc(S("ub"), 1)

            run(pool, step)

        @block.vector
        def _(dve):
            v = nc.vector
            dve.wait_ge(S("w_in"), 16 * 14)
            dve.wait_ge(S("pool_ready"), 2)
            v.tensor_scalar(w_qkv_g[:, :, :], w_qkv[:, :, :], cols[:, 0:1], None, ALU.mult).then_inc(S("prep"), 1)
            v.tensor_scalar(w_1g[:, :], w_1[:, :], cols[:, 2:3], None, ALU.mult).then_inc(S("prep"), 1)
            v.tensor_copy(shift1[:, :], cols[:, 1:2].broadcast_to([128, 128])).then_inc(S("prep"), 1)
            v.memset(w_node[:, :, :].rearrange("p i c -> p (i c)"), 0.0).then_inc(S("cleared"), 1)
            dve.wait_ge(S("cleared"), 1)
            for i in range(2):
                half = slice(LAT * i, LAT * (i + 1))
                v.tensor_copy(w_node[half, i, 4:20], w_gat[half, :]).then_inc(S("prep"), 1)
            for k in range(2):
                v.tensor_tensor(att_tmp[:, k, :], w_gat[:, :], w_att[:, k, :], ALU.mult).then_inc(S("prep"), 1)
            dve.wait_ge(S("prep"), 7)
            for k in range(2):
                for i in range(2):
                    half = slice(LAT * i, LAT * (i + 1))
                    v.tensor_reduce(w_node[half, i, 20 * k:20 * k + 4], att_tmp[half, k, :].rearrange("p (h e) -> p h e", e=4), AX.X, ALU.add).then_inc(S("prep"), 1)
            dve.wait_ge(S("prep"), 11)
            v.tensor_copy(hid_b[:, :], cols[:, 4:6]).then_inc(S("w_ready"), 1)
            dve.wait_ge(S("w_ready"), 1)
            dve.wait_ge(S("bias_ps"), 1)
            v.tensor_copy(qkv_b[:, :, :].rearrange("p k c -> p (k c)"), B7[:, 0:256]).then_inc(S("prep"), 1)
            v.tensor_copy(qk_bc[:, :], B7[:, 256:258]).then_inc(S("prep"), 1)
            v.tensor_tensor(hid_b[:, :], B6[:, 0:2], hid_b[:, :], ALU.add).then_inc(S("prep"), 1)
            dve.wait_ge(S("prep"), 14)
            v.tensor_copy(stA[:, 0, :], con[:, 0, :]).then_inc(S("bias_sb"), 1)

            def center(name, g, src, st, cen, done):
                v.tensor_reduce(st[:, 0, :], src, AX.X, ALU.add).then_inc(S(f"{name}_sum"), 1)
                dve.wait_ge(S(f"{name}_sum"), g + 1)
                v.tensor_scalar(st[:, 0, :], st[:, 0, :], 1.0 / LAT, None, ALU.mult).then_inc(S(f"{name}_mean"), 1)
                dve.wait_ge(S(f"{name}_mean"), g + 1)
                v.tensor_tensor(cen, src, wide(st[:, 0, :]), ALU.subtract).then_inc(done, 1)

            def variance(name, g, sq, st, maps):
                v.tensor_reduce(st[:, 1, :], sq[:, :, :], AX.X, ALU.add).then_inc(S(f"ssq{name}"), 1)
                dve.wait_ge(S(f"ssq{name}"), g + 1)
                for k, (scale, shift) in enumerate(maps):
                    v.tensor_scalar(st[:, 2 + k, :], st[:, 1, :], scale, shift, ALU.mult, ALU.add).then_inc(S(f"var{name}"), 1)

            def step(s, par, a, b_, c):
                A, B, C = s, s - 1, s - 2
                if c:
                    dve.wait_ge(S("x1"), C + 1)
                    after(dve, S("zT_ps"), C)
                    center("x1c", C, x1[par][:, :, :], stC, cenC[:, :, :], S("cenC"))
                    dve.wait_ge(S("sqC"), C + 1)
                    variance("C", C, sqC, stC, ((1.0 / LAT, EPS),))
                if b_:
                    dve.wait_ge(S("kvT_sb"), B + 1)
                    v.tensor_reduce(nkmax[:, :], kvT[:, :].rearrange("p (q t) -> p q t", t=128), AX.X, ALU.max, negate=True).then_inc(S("nkmax"), 1)
                if a:
                    dve.wait_ge(S("h_ps"), A + 1)
                    after(dve, S("hx0"), C + 1)
                    v.tensor_tensor(h[par][:, :, :], group(B2[:, :]), over(out_b[:, :]), ALU.add).then_inc(S("h"), 1)
                if b_:
                    dve.wait_ge(S("qkv_ps"), B + 1)
                    after(dve, S("local_ps"), B)
                    v.tensor_tensor(qkv[:, :, :, :].rearrange("p k (q i) c -> p k q (i c)", i=2), B34[:, :].rearrange("p (k q c) -> p k q c", k=2, c=128),
                                    qkv_b[:, :, :].unsqueeze(2).broadcast_to([128, 2, P2, 128]), ALU.add).then_inc(S("qkv_sb"), 1)
                    dve.wait_ge(S("qkv_sb"), B + 1)
                    q = qkv[:, 0, :, 8:LAT].rearrange("p b (h d) -> p b h d", d=8)
                    v.tensor_reduce(qmax[:, :, :], q, AX.X, ALU.max).then_inc(S("qmax"), 1)
                if a:
                    dve.wait_ge(S("h"), A + 1)
                    after(dve, S("u"), A)
                    after(dve, S("nA"), A)
                    center("hc", A, h[par][:, :, :], stA, cenA[:, :, :], S("cenA"))
                if b_:
                    dve.wait_ge(S("ET"), B + 1)
                    v.reciprocal(rks[:, :], ksum[:, :]).then_inc(S("rks"), 1)
                if a:
                    dve.wait_ge(S("sqA"), A + 1)
                    variance("A", A, sqA, stA, ((1.0 / LAT, EPS), ((1.0 + EPS) / LAT, EPS * EPS)))
                if b_:
                    dve.wait_ge(S("dots"), B + 1)
                    v.tensor_reduce(ndmax[:, 0, :], B34[:, :].rearrange("p (b k) -> p b k", k=128), AX.X, ALU.max, negate=True).then_inc(S("dmax"), 1)
                    dve.wait_ge(S("dmax"), B + 1)
                    v.tensor_scalar(ndmax[:, 1, :], ndmax[:, 0, :], SCALE, None, ALU.mult).then_inc(S("ndmax"), 1)
                    dve.wait_ge(S("qexp"), B + 1)
                    v.tensor_reduce(qsum[:, :, :], qexp[:, :, :, :], AX.X, ALU.add).then_inc(S("qsum"), 1)
                    dve.wait_ge(S("qsum"), B + 1)
                    v.reciprocal(qsum[:, :, :], qsum[:, :, :]).then_inc(S("qrec0"), 1)
                    dve.wait_ge(S("qrec0"), B + 1)
                    v.tensor_scalar(qsum[:, :, :], qsum[:, :, :], SCALE, None, ALU.mult).then_inc(S("qrec"), 1)
                    dve.wait_ge(S("rks"), B + 1)
                    dve.wait_ge(S("ctx_ps"), B + 1)
                    for p in range(P2):
                        m = v.scalar_tensor_tensor(ctx2[:, p, :], B5[:, 128 * p:128 * p + 128], rks[:, p:p + 1], headmask[:, :], ALU.mult, ALU.mult)
                    m.then_inc(S("ctx_sb"), 1)
                if c:
                    dve.wait_ge(S("mlp_ps"), C + 1)
                    dve.wait_ge(S("hx"), C + 1)
                    after(dve, S(f"h_out{par}"), 8 * (C - par))
                    v.tensor_tensor(hnew[par][:, :, :], group(B7[:, :]), hx[:, :, :], ALU.add).then_inc(S("hnew"), 1)
                    dve.wait_ge(S("hnew"), C + 1)
                    center("zc", C, hnew[par][:, :, :], stC, cenC[:, :, :], S("cenC"))
                    dve.wait_ge(S("sqZ"), C + 1)
                    variance("Z", C, sqC, stC, ((1.0 / LAT, EPS),))
                if b_:
                    dve.wait_ge(S("prob"), B + 1)
                    v.reciprocal(psm[:, 1, :], psm[:, 0, :]).then_inc(S("rprob"), 1)
                    dve.wait_ge(S("rprob"), B + 1)
                    dve.wait_ge(S("global_ps"), B + 1)
                    after(dve, S("OT_ps"), B)
                    v.tensor_copy(O[:, :, 8:LAT], group(B5[:, :])[:, :, 8:LAT]).then_inc(S("O_global"), 1)
                    dve.wait_ge(S("local_ps"), B + 1)
                    v.tensor_tensor(O[:, :, 0:8].rearrange("p (q i) c -> p i q c", i=2), B6[:, 0:8 * GB].rearrange("p (i q c) -> p i q c", i=2, c=8),
                                    psm[:, 1, :].rearrange("p (i q) -> p i q", i=2).unsqueeze(3).broadcast_to([128, 2, P2, 8]), ALU.mult).then_inc(S("O"), 1)
                    dve.wait_ge(S("proj_ps"), B + 1)
                    dve.wait_ge(S("ub"), B + 1)
                    after(dve, S("hx"), B - 1)
                    v.tensor_tensor(x1[1 - par][:, :, :], group(B5[:, :]), ub[1 - par][:, :, :], ALU.add).then_inc(S("x1"), 1)
                if c:
                    dve.wait_ge(S("table_ps"), C + 1)
                    after(dve, S(f"table_out{par}"), 16 * (C - par))
                    v.tensor_copy(tabg[par][:, :, :], B7[:, 0:24 * GB].rearrange("p (b c) -> p b c", c=24)).then_inc(S("table"), 1)

            run(dve, step)
    n.release()


CW = 64
CHUNKS = EP // CW
RING = 8
CH = 20
EXPERTS, HEADS = 4, 4


def graph(nc, d, keys, cur, seg, count):
    ctx = ExitStack()
    with ctx:
        n = Names(nc, ctx, "graph")
        S = n.sem
        PC = GB // 2 * 128
        SUB = 16
        ident = n.sb("ident3", [128, 128])
        upto = n.sb("upto", [128, 128])
        ones = n.sb("ones", [128, 128])
        ramp = n.sb("ramp", [128, 128])
        ramps = n.sb("ramps", [128, 128, SUB], BF16)
        rowpos = n.sb("first_position", [128, 1])
        dsti = keys[cur][:, :].bitcast(I32)
        srci = keys[1 - cur][:, :].bitcast(I32)
        dlo = n.sb("dst_frame", [128, EP], BF16)
        dhi = n.sb("dst_sample", [128, EP], BF16)
        keep = n.sb("same_segment", [128, EP])
        idx = [n.sb(f"gather_index{i}", [128, CW], U32) for i in range(2)]
        stage = [n.sb(f"gathered{i}", [128, CW, CH]) for i in range(2)]
        ring = n.sb("ring", [128, RING * CW, CH])
        hot = [n.sb(f"one_hot{i}", [128, 2, 128, SUB], BF16) for i in range(2)]
        zero_b = n.sb("zero_bf16", [128, 128], BF16)
        zg = [n.sb(f"zT_in{i}", [128, PC]) for i in range(2)]
        w1e = n.sb("w_expert1", [128, EXPERTS, 128])
        w2e = n.sb("w_expert2", [128, EXPERTS, LAT])
        b1e = n.sb("b_expert1", [128, EXPERTS])
        b2e = n.sb("b_expert2", [128, EXPERTS * LAT])
        hid = n.sb("expert_hidden", [128, 2 * EXPERTS, PC])
        ye = [n.sb(f"expert_out{i}", [128, GB, EXPERTS * LAT]) for i in range(2)]
        cnt = n.sb("count_copy", [128, 128])
        tot = n.sb("sample_total", [128, 128])
        scan_tot = n.sb("sample_total_upto", [128, 128])
        endf = n.sb("end_float", [128, 128])
        startf = n.sb("start_float", [128, 128])
        none = n.sb("no_edges", [128, 128])
        start_i = n.sb("start_index", [128, 128], U32)
        end_i = n.sb("end_index", [128, 128], U32)
        dst_first = n.sb("first_destination", [128, 1], U32)
        nd = n.sb("node_dst_scores", [128, 128, HEADS])
        first4 = n.sb("first_dst_scores", [128, HEADS])
        adc = [n.sb(f"dst_scores_at_starts{i}", [128, CW, HEADS]) for i in range(2)]
        adb = [n.sb(f"dst_scores{i}", [128, HEADS, CW]) for i in range(2)]
        pre = n.sb("score_sum", [128, HEADS, CW])
        e = n.sb("score", [128, HEADS, CW])
        pen = n.sb("reset", [128, CW])
        M = [n.sb(f"running_max{i}", [128, HEADS, CW + 1]) for i in range(2)]
        X = n.sb("exponents", [128, 2 * HEADS, CW])
        RW = n.sb("rescale_and_weight", [128, 2 * HEADS, CW])
        wv = n.sb("weighted", [128, 16, CW])
        st = [n.sb(f"state{i}", [128, CW, CH + HEADS]) for i in range(2)]
        eq = hid[:, 5:7, :].rearrange("p a b -> p (a b)").bitcast(BF16)
        first_len = n.sb("first_segment_length", [128, 1])
        e1f = n.sb("first_end_float", [128, 1])
        e1 = n.sb("first_end", [128, 1], U32)
        jt = n.sb("join_in", [128, 4, CH])
        jT = hid[0:CH, 0, :].rearrange("c (k p) -> c k p", p=128)
        js = hid[0:CH, 1:3, :].rearrange("c a (k p) -> c (a k) p", p=128)
        jm = hid[0:CH, 3, 0:129]
        jx = hid[0:CH, 4, 0:129]
        primed = n.sb("primed", [128, 16])
        token = n.sb("pool_token", [128, 2])
        jc = n.sb("carry", [128, 2, CH])
        row = n.sb("end_row", [128, CH + HEADS])
        jr = n.sb("join_row", [128, 6, CH])
        rowo = n.sb("end_row_joined", [128, CH + HEADS])

        hist = n.ps("histogram", [128, 512])
        hps = [n.ps(f"expert_hidden_ps{i}", [128, PC]) for i in range(2)]
        yps = n.ps("expert_out_ps", [128, GB, EXPERTS * LAT])
        sps = n.ps("small_ps", [128, 512])
        block = ctx.enter_context(nc.Block())
        OOB = 2 * EDGES

        AHEAD = [("adb", 2), ("max_copied", 2), ("RW", 1), ("sums", 1), ("y_ps", 1)]
        AHEAD += [(f"{name}{par}", 16) for name in ("ring", "stored", "y_out") for par in range(2)]

        @block.sync
        def _(sp):
            for t, name in ((ident, "c_ident"), (upto, "c_upto"), (ones, "c_ones"), (ramp, "c_ramp"), (rowpos, "c_rowpos"), (b1e, "b_expert1")):
                sp.dma_start(t[:, :], d[name]).then_inc(S("consts"), 16)
            sp.dma_start(w1e[:, :, :], d["w_expert1"]).then_inc(S("consts"), 16)
            sp.dma_start(w2e[:, :, :], d["w_expert2"]).then_inc(S("consts"), 16)
            sp.dma_start(b2e[:, :], d["b_expert2"].partition_broadcast(128)).then_inc(S("consts"), 16)
            sp.dma_start(nd[:, :, :], d["node_dst"].rearrange("(b t) c -> t b c", t=128)).then_inc(S("nd_in"), 16)
            sp.wait_ge(S("srci"), 1)

            def index(c, par):
                sp.dma_start(idx[par][:, :].bitcast(I32), srci[:, bass.ds(c * CW, CW)]).then_inc(S(f"idx_in{par}"), 16)

            index(0, 0)
            index(1, 1)

            def serve(c, slot, par, more=True):
                sp.wait_ge(S(f"gathered{par}"), (c - par) * (8 * CW) + 16 * CW)
                if more:
                    index(c + 2, par)
                sp.wait_ge(S("chunk_used"), c - RING + 1)
                sp.dma_start(ring[:, bass.ds(slot * CW, CW), :], stage[par][:, :, :]).then_inc(S(f"ring{par}"), 16)

            with sp.Fori(0, RING // 2) as i:
                for par in range(2):
                    c = 2 * i + par
                    sp.wait_ge(S(f"gathered{par}"), (c - par) * (8 * CW) + 16 * CW)
                    sp.dma_start(ring[:, bass.ds(c * CW, CW), :], stage[par][:, :, :]).then_inc(S(f"ring{par}"), 16)
                    index(c + 2, par)
            sp.wait_ge(S("scattered"), 16 * 128)
            sp.wait_ge(S("first4"), 16)
            sp.dma_start(d["dst_at_start"].rearrange("(p f) c -> p f c", p=128)[:, 0, :], first4[:, :]).then_inc(S("starts_set"), 16)
            with sp.Fori(1, CHUNKS // RING - 1) as o:
                with sp.Fori(0, RING // 2) as i:
                    for par in range(2):
                        serve(RING * o + 2 * i + par, 2 * i + par, par)
            with sp.Fori(0, RING // 2 - 1) as i:
                for par in range(2):
                    serve(2 * i + (CHUNKS - RING + par), 2 * i + par, par)
            for par in range(2):
                serve(CHUNKS - 2 + par, RING - 2 + par, par, more=False)

        @block.gpsimd
        def _(pool):
            off = bass.IndirectOffsetOnAxis

            def gather(c, par):
                pool.wait_ge(S(f"idx_in{par}"), 8 * (c - par) + 16)
                pool.wait_ge(S(f"ring{par}"), 8 * (c - par) + 16)
                pool.wait_ge(S("gather_go"), c + 1)
                nc.gpsimd.tensor_tensor(token[:, 0:1], token[:, 1:2], token[:, 1:2], ALU.add).then_inc(S("gather_go"), 1)
                for f in range(CW):
                    pool.indirect_dma_start(stage[par][:, f, :], None, d["node_src"], off(ap=idx[par][:, f:f + 1], axis=0))\
                        .then_inc(S(f"gathered{par}"), 16)

            pool.memset(token[:, :], 0.0).then_inc(S("gather_go"), 1)
            with pool.Fori(0, RING // 2) as i:
                for par in range(2):
                    gather(2 * i + par, par)
            pool.wait_ge(S("indices"), 2)
            pool.wait_ge(S("nd_in"), 16)
            pool.wait_ge(S("starts_cleared"), 64)
            for b in range(B):
                pool.indirect_dma_start(d["dst_at_start"], off(ap=start_i[:, b:b + 1], axis=0), nd[:, b, :], None,
                                        bounds_check=EDGES - 1, oob_is_err=False).then_inc(S("scattered"), 16)
            pool.wait_ge(S("dst_first"), 1)
            pool.indirect_dma_start(first4[:, :], None, d["node_dst"], off(ap=dst_first[:, 0:1], axis=0)).then_inc(S("first4"), 16)
            with pool.Fori(RING // 2, CHUNKS // 2) as i:
                for par in range(2):
                    gather(2 * i + par, par)
            for par in range(2):
                pool.wait_ge(S(f"stored{par}"), 16 * (CHUNKS // 2) + 16)
            pool.wait_ge(S("e1"), 1)
            pool.indirect_dma_start(row[:, :], None, d["edge_state"], off(ap=e1[:, 0:1], axis=0)).then_inc(S("row_in"), 16)
            pool.wait_ge(S("row_joined"), 2)
            pool.indirect_dma_start(d["edge_state"], off(ap=e1[:, 0:1], axis=0), rowo[:, :], None).then_inc(S("row_out"), 16)
            pool.wait_ge(S("row_out"), 16)
            for b in range(B):
                pool.indirect_dma_start(seg[:, b, :], None, d["edge_state"], off(ap=end_i[:, b:b + 1], axis=0)).then_inc(S("ends"), 16)
            pool.wait_ge(S("ends"), 16 * B)

        @block.tensor
        def _(pe):
            mm = nc.tensor.matmul
            one = dict(start=True, stop=True)
            pe.wait_ge(S("consts"), 16 * 9)
            pe.wait_ge(S("zero"), 2)
            mm(hist[:, 0:128], zero_b[:, :], zero_b[:, :], start=True, stop=False).then_inc(S("hist_done"), 2)

            with pe.Fori(0, EP // SUB // 2) as i:
                for par in range(2):
                    pe.wait_ge(S("hot"), 2 * i + (par + 1))
                    for j in range(SUB):
                        m = mm(hist[:, 0:128], hot[par][:, 0, :, j], hot[par][:, 1, :, j], start=False, stop=False)
                    m.then_inc(S("hist_done"), 1)
            mm(hist[:, 0:128], zero_b[:, :], zero_b[:, :], start=False, stop=True).then_inc(S("hist_full"), 1)
            pe.wait_ge(S("count_sb"), 1)
            mm(sps[:, 0:128], upto[:, :], cnt[:, :], **one)
            mm(sps[:, 128:256], ones[:, :], cnt[:, :], **one).then_inc(S("upto_ps"), 1)

            def experts(g, par):
                pe.wait_ge(S(f"z_in{par}"), 8 * (g - par) + 16)
                for k in range(2 * EXPERTS):
                    ex, i = k // 2, k % 2
                    half = slice(LAT * i, LAT * (i + 1))
                    pe.wait_ge(S(f"hid_free{i}"), EXPERTS * g + ex + 1)
                    mm(hps[i][:, :], w1e[half, ex, :], zg[par][half, :], **one).then_inc(S(f"hid_ps{i}"), 1)
                pe.wait_ge(S("gelu_done"), g + 1)
                pe.wait_ge(S("y_free"), g + 1)
                for b in range(GB):
                    for ex in range(EXPERTS):
                        m = mm(yps[:, b, LAT * ex:LAT * ex + LAT], hid[:, 2 * ex + b % 2, 128 * (b // 2):128 * (b // 2) + 128], w2e[:, ex, :], **one)
                m.then_inc(S("y_ps"), 1)

            with pe.Fori(0, G // 2) as i:
                for par in range(2):
                    experts(2 * i + par, par)
            pe.wait_ge(S("join_in"), 4)
            for k in range(4):
                m = nc.tensor.transpose(sps[0:CH, 128 * k:128 * k + 128], jt[:, k, :], ident[:, :])
            m.then_inc(S("join_ps"), 1)
            pe.wait_ge(S("carry_rows"), 2)
            for k, t in ((0, jm), (1, jx)):
                m = nc.tensor.transpose(hps[0][:, CH * k:CH * k + CH], t[:, 0:128], ident[0:CH, 0:CH])
            m.then_inc(S("carry_ps"), 1)

        @block.scalar
        def _(act):
            def load_z(g, par):
                act.dma_start(zg[par][:, :], d["zT"][:, bass.ds(g * PC, PC)]).then_inc(S(f"z_in{par}"), 16)

            def store_y(g, par):
                act.dma_start(d["expert_out"][:, bass.ds(g * GB, GB), :], ye[par][:, :, :]).then_inc(S(f"y_out{par}"), 16)

            load_z(0, 0)
            load_z(1, 1)
            act.wait_ge(S("zero"), 2)
            for k in range(4):
                w = EDGES * HEADS // 128 // 4
                act.dma_start(d["dst_at_start"].rearrange("(p f) c -> p (f c)", p=128)[:, k * w:(k + 1) * w], ye[0][:, :, :].rearrange("p b c -> p (b c)"))\
                   .then_inc(S("starts_cleared"), 16)
            act.wait_ge(S("starts_cleared"), 64)
            act.wait_ge(S("consts"), 16 * 9)
            act.activation(b1e[:, :], b1e[:, :], ACT.Copy).then_inc(S("hid_free0"), 1)
            act.wait_ge(S("hid_free0"), 1)
            act.activation(b1e[:, :], b1e[:, :], ACT.Copy).then_inc(S("hid_free1"), 1)
            act.wait_ge(S("hid_free1"), 1)

            def experts(g, par, more=True):
                for k in range(2 * EXPERTS):
                    ex, i = k // 2, k % 2
                    act.wait_ge(S(f"hid_ps{i}"), EXPERTS * g + ex + 1)
                    if k == 0:
                        act.wait_ge(S("y_ps"), g + 1)
                    m = act.activation(hid[:, k, :], hps[i][:, :], ACT.Gelu, bias=b1e[:, ex:ex + 1])
                    m.then_inc(S(f"hid_free{i}"), 1)
                act.wait_ge(S("hid_free1"), EXPERTS * g + EXPERTS + 1)
                act.activation(b1e[:, :], b1e[:, :], ACT.Copy).then_inc(S("gelu_done"), 1)
                if more:
                    load_z(g + 2, par)
                act.wait_ge(S("y_sb"), g + 1)
                store_y(g, par)

            with act.Fori(0, G // 2 - 1) as i:
                for par in range(2):
                    experts(2 * i + par, par)
            for g in (G - 2, G - 1):
                experts(g, g % 2, more=False)
            for par in range(2):
                act.wait_ge(S(f"y_out{par}"), 16 * (G // 2) + 16)
            act.wait_ge(S("starts_set"), 16)

            def chunk(c, par):
                act.wait_ge(S("adb"), c + 1)
                act.dma_start(adc[par][:, :, :], d["dst_at_start"].rearrange("(p f) c -> p f c", p=128)[:, bass.ds(c * CW, CW), :]).then_inc(S(f"adc_in{par}"), 16)
                act.wait_ge(S("X"), c + 1)
                act.activation(RW[:, :, :], X[:, :, :], ACT.Exp).then_inc(S("RW"), 1)
                act.wait_ge(S(f"stored{par}"), 8 * (c - par) + 16)
                act.activation(st[par][:, :, CH:].rearrange("p f h -> p h f"), M[par][:, :, 1:], ACT.Copy).then_inc(S("max_copied"), 1)
                act.wait_ge(S("sums"), c + 2)
                act.wait_ge(S("max_copied"), c + 3)
                act.dma_start(d["edge_state"].rearrange("(p f) c -> p f c", p=128)[:, bass.ds(c * CW, CW), :], st[par][:, :, :]).then_inc(S(f"stored{par}"), 16)

            with act.Fori(0, CHUNKS // 2) as i:
                for par in range(2):
                    chunk(2 * i + par, par)
            act.wait_ge(S("join_x"), 1)
            act.activation(js[:, 4:6, :], js[:, 2:4, :], ACT.Exp).then_inc(S("join_e"), 1)
            act.wait_ge(S("row_x"), 2)
            act.activation(jr[:, 3:5, :], jr[:, 1:3, :], ACT.Exp).then_inc(S("row_e"), 1)

        @block.vector
        def _(dve):
            v = nc.vector
            for k, (name, ahead) in enumerate(AHEAD):
                v.memset(primed[:, k:k + 1], 0.0).then_inc(S(name), ahead)
            v.memset(ye[0][:, :, :].rearrange("p b c -> p (b c)"), 0.0).then_inc(S("zero"), 1)
            v.memset(zero_b[:, :], 0.0).then_inc(S("zero"), 1)
            v.tensor_scalar(srci, dsti, NODES - 1, None, ALU.bitwise_and).then_inc(S("srci"), 1)
            dve.wait_ge(S("srci"), 1)
            v.tensor_scalar(dsti, dsti, NODE_BITS, NODES - 1, ALU.logical_shift_right, ALU.bitwise_and).then_inc(S("dsti"), 1)
            dve.wait_ge(S("dsti"), 1)
            whole = keep[:, :].bitcast(I32)
            v.tensor_scalar(whole, dsti, T - 1, None, ALU.bitwise_and).then_inc(S("split"), 1)
            dve.wait_ge(S("split"), 1)
            v.tensor_copy(dlo[:, :], whole).then_inc(S("split"), 1)
            dve.wait_ge(S("split"), 2)
            v.tensor_scalar(whole, dsti, T.bit_length() - 1, None, ALU.logical_shift_right).then_inc(S("split"), 1)
            dve.wait_ge(S("split"), 3)
            v.tensor_copy(dhi[:, :], whole).then_inc(S("split"), 1)
            dve.wait_ge(S("split"), 4)
            v.tensor_copy(dst_first[:, :].bitcast(I32), dsti[:, 0:1]).then_inc(S("dst_first"), 1)
            v.memset(keep[:, 0:1], 0.0).then_inc(S("keep0"), 1)
            v.tensor_tensor(keep[:, 1:EP], dsti[:, 1:EP], dsti[:, 0:EP - 1], ALU.is_equal).then_inc(S("keep0"), 1)
            dve.wait_ge(S("consts"), 16 * 9)
            v.tensor_copy(ramps[:, :, :], ramp[:, :].unsqueeze(2).broadcast_to([128, 128, SUB])).then_inc(S("split"), 1)
            dve.wait_ge(S("split"), 5)
            for par in range(2):
                for t in (M[par][:, :, :], adb[par][:, :, :], st[par][:, :, :]):
                    v.memset(t.rearrange("p a b -> p (a b)"), 0.0).then_inc(S("cleared"), 1)
            dve.wait_ge(S("cleared"), 6)
            v.tensor_copy(e1f[:, :], rowpos[:, :]).then_inc(S("y_free"), 1)
            with dve.Fori(0, EP // SUB // 2) as i:
                for par in range(2):
                    dve.wait_ge(S("hist_done"), 2 * i + (par + 1))
                    cols = bass.ds(i * (2 * SUB) + par * SUB, SUB)
                    for k, value in enumerate((dlo, dhi)):
                        m = v.tensor_tensor(hot[par][:, k, :, :], ramps[:, :, :], value[:, cols].unsqueeze(1).broadcast_to([128, 128, SUB]), ALU.is_equal)
                    m.then_inc(S("hot"), 1)

            dve.wait_ge(S("hist_full"), 1)
            v.tensor_copy(cnt[:, :], hist[:, 0:128]).then_inc(S("count_sb"), 1)
            dve.wait_ge(S("count_sb"), 1)
            v.tensor_copy(count[:, :], cnt[:, :]).then_inc(S("f"), 1)
            v.tensor_scalar(none[:, :], cnt[:, :], 0.0, float(OOB), ALU.is_equal, ALU.mult).then_inc(S("f"), 1)
            dve.wait_ge(S("upto_ps"), 1)
            v.tensor_copy(tot[:, :], sps[:, 128:256]).then_inc(S("f"), 1)
            dve.wait_ge(S("f"), 3)
            v.tensor_tensor_scan(scan_tot[:, :], ones[:, :], tot[:, :], 0.0, ALU.mult, ALU.add).then_inc(S("f"), 1)
            dve.wait_ge(S("f"), 4)
            v.tensor_tensor(tot[:, :], scan_tot[:, :], tot[:, :], ALU.subtract).then_inc(S("f"), 1)
            dve.wait_ge(S("f"), 5)
            v.tensor_tensor(endf[:, :], sps[:, 0:128], tot[:, :], ALU.add).then_inc(S("f"), 1)
            dve.wait_ge(S("f"), 6)
            v.tensor_tensor(startf[:, :], endf[:, :], cnt[:, :], ALU.subtract).then_inc(S("f"), 1)
            dve.wait_ge(S("f"), 7)
            v.tensor_tensor(start_i[:, :], startf[:, :], none[:, :], ALU.add).then_inc(S("indices"), 1)
            v.tensor_scalar(end_i[:, :], endf[:, :], -1.0, 0.0, ALU.add, ALU.max).then_inc(S("indices"), 1)

            def experts(g, par):
                dve.wait_ge(S("y_ps"), g + 2)
                dve.wait_ge(S(f"y_out{par}"), 8 * (g - par) + 16)
                v.tensor_tensor(ye[par][:, :, :], yps[:, :, :], b2e[:, :].unsqueeze(1).broadcast_to([128, GB, EXPERTS * LAT]), ALU.add).then_inc(S("y_sb"), 1)
                dve.wait_ge(S("y_sb"), g + 1)
                v.tensor_copy(e1f[:, :], rowpos[:, :]).then_inc(S("y_free"), 1)

            dve.wait_ge(S("starts_cleared"), 64)
            with dve.Fori(0, G // 2) as i:
                for par in range(2):
                    experts(2 * i + par, par)

            def chunk(c, slot, par):
                cols = bass.ds(c * CW, CW)
                g = ring[:, bass.ds(slot * CW, CW), :]
                dve.wait_ge(S(f"adc_in{par}"), 8 * (c - par) + 16)
                dve.wait_ge(S("adb"), c + 2)
                for h in range(HEADS):
                    m = v.tensor_tensor_scan(adb[par][:, h, :], keep[:, cols], adc[par][:, :, h], adb[1 - par][:, h, CW - 1:CW], ALU.mult, ALU.add)
                m.then_inc(S("adb"), 1)
                v.tensor_scalar(pen[:, :], keep[:, cols], -NEG, NEG, ALU.mult, ALU.add).then_inc(S("pen"), 1)
                dve.wait_ge(S(f"ring{par}"), 8 * (c - par) + 32)
                dve.wait_ge(S("adb"), c + 3)
                v.tensor_tensor(pre[:, :, :], g[:, :, 0:HEADS].rearrange("p f h -> p h f"), adb[par][:, :, :], ALU.add).then_inc(S("pre"), 1)
                dve.wait_ge(S("pre"), c + 1)
                v.scalar_tensor_tensor(e[:, :, :], pre[:, :, :], 0.2, pre[:, :, :], ALU.mult, ALU.max).then_inc(S("e"), 1)
                dve.wait_ge(S("max_copied"), c + 1)
                v.tensor_copy(M[par][:, :, 0:1], M[1 - par][:, :, CW:CW + 1]).then_inc(S("M0"), 1)
                dve.wait_ge(S("e"), c + 1)
                dve.wait_ge(S("M0"), c + 1)
                dve.wait_ge(S("pen"), c + 1)
                for h in range(HEADS):
                    m = v.tensor_tensor_scan(M[par][:, h, 1:], pen[:, :], e[:, h, :], M[par][:, h, 0:1], ALU.add, ALU.max)
                m.then_inc(S("M"), 1)
                dve.wait_ge(S("M"), c + 1)
                dve.wait_ge(S("RW"), c + 1)
                v.tensor_tensor(X[:, 0:HEADS, :], M[par][:, :, 0:CW], M[par][:, :, 1:], ALU.subtract).then_inc(S("X0"), 1)
                dve.wait_ge(S("X0"), c + 1)
                v.tensor_tensor(X[:, 0:HEADS, :], X[:, 0:HEADS, :], pen[:, :].unsqueeze(1).broadcast_to([128, HEADS, CW]), ALU.add).then_inc(S("X1"), 1)
                v.tensor_tensor(X[:, HEADS:, :], e[:, :, :], M[par][:, :, 1:], ALU.subtract).then_inc(S("X2"), 1)
                dve.wait_ge(S("X1"), c + 1)
                dve.wait_ge(S("X2"), c + 1)
                v.tensor_copy(first_len[:, :], rowpos[:, :]).then_inc(S("X"), 1)
                dve.wait_ge(S("RW"), c + 2)
                for h in range(HEADS):
                    m = v.tensor_tensor(wv[:, 4 * h:4 * h + 4, :], g[:, :, 4 + 4 * h:8 + 4 * h].rearrange("p f e -> p e f"),
                                        RW[:, HEADS + h, :].unsqueeze(1).broadcast_to([128, 4, CW]), ALU.mult)
                m.then_inc(S("wv"), 1)
                dve.wait_ge(S("wv"), c + 1)
                v.tensor_copy(first_len[:, :], rowpos[:, :]).then_inc(S("chunk_used"), 1)
                dve.wait_ge(S(f"stored{par}"), 8 * (c - par) + 16)
                dve.wait_ge(S("sums"), c + 1)
                for k in range(CH):
                    h = k // 4 if k < 16 else k - 16
                    src = wv[:, k, :] if k < 16 else RW[:, HEADS + h, :]
                    m = v.tensor_tensor_scan(st[par][:, :, k], RW[:, h, :], src, st[1 - par][:, CW - 1, k:k + 1], ALU.mult, ALU.add)
                m.then_inc(S("sums"), 1)

            with dve.Fori(0, CHUNKS // RING) as o:
                with dve.Fori(0, RING // 2) as i:
                    for par in range(2):
                        chunk(RING * o + 2 * i + par, 2 * i + par, par)

            dve.wait_ge(S("sums"), CHUNKS + 1)
            dve.wait_ge(S("max_copied"), CHUNKS + 2)
            last = st[1][:, CW - 1, :]
            dstf = keys[cur]
            v.tensor_copy(dstf[:, :], dsti).then_inc(S("u"), 1)
            dve.wait_ge(S("u"), 1)
            v.tensor_scalar(eq[:, :], dstf[:, :], dstf[:, 0:1], None, ALU.is_equal, ALU.add, accum_out=first_len[:, :]).then_inc(S("u"), 1)
            dve.wait_ge(S("u"), 2)
            v.tensor_scalar(e1f[:, :], first_len[:, :], rowpos[:, :], -1.0, ALU.add, ALU.add).then_inc(S("u"), 1)
            dve.wait_ge(S("u"), 3)
            v.tensor_copy(e1[:, :], e1f[:, :]).then_inc(S("e1"), 1)
            v.tensor_copy(jt[:, 0, :], last[:, 0:CH]).then_inc(S("join_in"), 1)
            v.tensor_copy(jt[:, 1, 0:16].rearrange("p (h e) -> p h e", e=4), last[:, CH:].unsqueeze(2).broadcast_to([128, HEADS, 4])).then_inc(S("join_m"), 1)
            v.tensor_copy(jt[:, 1, 16:CH], last[:, CH:]).then_inc(S("join_in"), 1)
            v.tensor_copy(jt[:, 2, :], dstf[:, 0:1].broadcast_to([128, CH])).then_inc(S("join_in"), 1)
            v.tensor_copy(jt[:, 3, :], dstf[:, EP - 1:EP].broadcast_to([128, CH])).then_inc(S("join_in"), 1)
            dve.wait_ge(S("join_ps"), 1)
            v.tensor_copy(jT[:, :, :].rearrange("c k p -> c (k p)"), sps[0:CH, :]).then_inc(S("u"), 1)
            v.memset(jm[:, 0:1], NEG).then_inc(S("u"), 1)
            v.memset(jx[:, 0:1], 0.0).then_inc(S("u"), 1)
            v.memset(js[:, 0, 0:1], 0.0).then_inc(S("u"), 1)
            dve.wait_ge(S("u"), 7)
            Ss, Mm, first, lastd = (jT[:, k, :] for k in range(4))
            v.tensor_tensor(js[:, 0, 1:128], first[:, 1:128], lastd[:, 0:127], ALU.is_equal).then_inc(S("u"), 1)
            v.tensor_tensor(js[:, 1, :], first, lastd, ALU.is_equal).then_inc(S("u"), 1)
            dve.wait_ge(S("u"), 9)
            v.tensor_tensor(js[:, 1, :], js[:, 1, :], js[:, 0, :], ALU.mult).then_inc(S("u"), 1)
            dve.wait_ge(S("u"), 10)
            v.tensor_scalar(js[:, 1, :], js[:, 1, :], -NEG, NEG, ALU.mult, ALU.add).then_inc(S("u"), 1)
            v.tensor_scalar(js[:, 0, :], js[:, 0, :], -NEG, NEG, ALU.mult, ALU.add).then_inc(S("u"), 1)
            dve.wait_ge(S("u"), 12)
            v.tensor_tensor_scan(jm[:, 1:], js[:, 1, :], Mm, jm[:, 0:1], ALU.add, ALU.max).then_inc(S("u"), 1)
            dve.wait_ge(S("u"), 13)
            v.tensor_tensor(js[:, 2, :], jm[:, 0:128], jm[:, 1:], ALU.subtract).then_inc(S("u"), 1)
            v.tensor_tensor(js[:, 3, :], Mm, jm[:, 1:], ALU.subtract).then_inc(S("u"), 1)
            dve.wait_ge(S("u"), 15)
            v.tensor_tensor(js[:, 2, :], js[:, 2, :], js[:, 1, :], ALU.add).then_inc(S("join_x"), 1)
            dve.wait_ge(S("join_e"), 1)
            v.tensor_tensor(js[:, 6, :], js[:, 5, :], Ss, ALU.mult).then_inc(S("u"), 1)
            dve.wait_ge(S("u"), 16)
            v.tensor_tensor_scan(jx[:, 1:], js[:, 4, :], js[:, 6, :], jx[:, 0:1], ALU.mult, ALU.add).then_inc(S("carry_rows"), 1)
            v.tensor_tensor(jm[:, 0:128], jm[:, 0:128], js[:, 0, :], ALU.add).then_inc(S("carry_rows"), 1)
            dve.wait_ge(S("carry_ps"), 1)
            v.tensor_copy(jc[:, :, :].rearrange("p k c -> p (k c)"), hps[0][:, 0:2 * CH]).then_inc(S("u"), 1)
            dve.wait_ge(S("row_in"), 16)
            v.tensor_copy(jr[:, 5, 0:16].rearrange("p (h e) -> p h e", e=4), row[:, CH:].unsqueeze(2).broadcast_to([128, HEADS, 4])).then_inc(S("u"), 1)
            v.tensor_copy(jr[:, 5, 16:CH], row[:, CH:]).then_inc(S("u"), 1)
            dve.wait_ge(S("u"), 19)
            v.tensor_tensor(jr[:, 0, :], jr[:, 5, :], jc[:, 0, :], ALU.max).then_inc(S("u"), 1)
            dve.wait_ge(S("u"), 20)
            v.tensor_tensor(jr[:, 1, :], jr[:, 5, :], jr[:, 0, :], ALU.subtract).then_inc(S("row_x"), 1)
            v.tensor_tensor(jr[:, 2, :], jc[:, 0, :], jr[:, 0, :], ALU.subtract).then_inc(S("row_x"), 1)
            dve.wait_ge(S("row_e"), 1)
            v.tensor_tensor(jr[:, 3, :], jr[:, 3, :], row[:, 0:CH], ALU.mult).then_inc(S("u"), 1)
            v.tensor_tensor(jr[:, 4, :], jr[:, 4, :], jc[:, 1, :], ALU.mult).then_inc(S("u"), 1)
            dve.wait_ge(S("u"), 22)
            v.tensor_tensor(rowo[:, 0:CH], jr[:, 3, :], jr[:, 4, :], ALU.add).then_inc(S("row_joined"), 1)
            v.tensor_copy(rowo[:, CH:], jr[:, 0, 16:CH]).then_inc(S("row_joined"), 1)
    n.release()


def mix_experts(nc, d, seg, count):
    ctx = ExitStack()
    with ctx:
        n = Names(nc, ctx, "mix")
        S = n.sem
        y = n.sb("expert_outputs", [128, B, EXPERTS, LAT])
        h = n.sb("tokens", [128, B, LAT])
        own = n.sb("own_row", [128, B, CH])
        dst = n.sb("own_dst_scores", [128, B, HEADS])
        vec = n.sb("gain_shift_bias", [128, 3, 16])
        loop = n.sb("loop_score", [128, B, HEADS])
        top = n.sb("max_score", [128, B, HEADS])
        w = n.sb("edge_and_loop_weight", [128, 2, B, HEADS])
        one = n.sb("of_each_node", [128, 4, B])
        con = n.sb("pow_constants", [128, 2, B])
        block = ctx.enter_context(nc.Block())
        wide16 = lambda a: a.unsqueeze(2).broadcast_to([128, B, 16])
        wide4 = lambda a: a.unsqueeze(2).broadcast_to([128, B, EXPERTS])
        each = lambda a: a.unsqueeze(1).broadcast_to([128, B, 16])
        by_head = lambda a: a.rearrange("p b (h e) -> p b h e", e=EXPERTS)
        over_experts = lambda a: a.unsqueeze(3).broadcast_to([128, B, HEADS, EXPERTS])

        @block.sync
        def _(sp):
            sp.dma_start(own[:, :, :], d["node_src"].rearrange("(b t) c -> t b c", t=128)).then_inc(S("rows_in"), 16)
            sp.dma_start(dst[:, :, :], d["node_dst"].rearrange("(b t) c -> t b c", t=128)).then_inc(S("rows_in"), 16)
            for k, name in enumerate(("score_gain", "score_shift", "score_bias")):
                sp.dma_start(vec[:, k, :], d[name].partition_broadcast(128)).then_inc(S("rows_in"), 16)
            for q in range(4):
                b = slice(q * B // 4, (q + 1) * B // 4)
                sp.dma_start(h[:, b, :], d["h2"].rearrange("t (b c) -> t b c", c=LAT)[:, b, :]).then_inc(S("h_in"), 16)
                sp.dma_start(y[:, b, :, :].rearrange("t b e c -> t b (e c)"), d["expert_out"][:, b, :]).then_inc(S("y_in"), 16)
            for k in range(G // 2):
                for i, name in enumerate(("mixed_even", "mixed_odd")):
                    g = 2 * k + i
                    sp.wait_ge(S(name), 4 * (k + 1))
                    sp.dma_start(d["out"][g * GB:(g + 1) * GB].rearrange("b t c -> t b c"), h[:, g * GB:(g + 1) * GB, :]).then_inc(S("out"), 16)
            sp.wait_ge(S("out"), 16 * G)

        def mix(engine, ops, par, name):
            for k in range(G // 2):
                g = 2 * k + par
                b = slice(g * GB, (g + 1) * GB)
                ops.tensor_tensor(y[:, b], y[:, b], top[:, b, :].unsqueeze(3).broadcast_to([128, GB, EXPERTS, LAT]), ALU.mult).then_inc(S(name), 1)
                engine.wait_ge(S(name), 4 * k + 1)
                ops.tensor_tensor(y[:, b, 0:2], y[:, b, 0:2], y[:, b, 2:4], ALU.add).then_inc(S(name), 1)
                engine.wait_ge(S(name), 4 * k + 2)
                ops.tensor_tensor(y[:, b, 0], y[:, b, 0], y[:, b, 1], ALU.add).then_inc(S(name), 1)
                engine.wait_ge(S(name), 4 * k + 3)
                ops.tensor_tensor(h[:, b, :], h[:, b, :], y[:, b, 0], ALU.add).then_inc(S(name), 1)

        @block.vector
        def _(dve):
            v = nc.vector
            count_ops = [0]

            def did(i):
                i.then_inc(S("node"), 1)
                count_ops[0] += 1

            def ready():
                dve.wait_ge(S("node"), count_ops[0])

            sums, total, seg_max = seg[:, :, 0:16], seg[:, :, 16:20], seg[:, :, 20:24]
            pen, mean, var, rstd = (one[:, k, :] for k in range(4))
            did(v.tensor_scalar(pen, count[:, :], 0.0, NEG, ALU.is_equal, ALU.mult))
            dve.wait_ge(S("rows_in"), 16 * 5)
            did(v.tensor_tensor(loop[:, :, :], own[:, :, 0:4], dst[:, :, :], ALU.add))
            ready()
            did(v.scalar_tensor_tensor(loop[:, :, :], loop[:, :, :], 0.2, loop[:, :, :], ALU.mult, ALU.max))
            did(v.tensor_tensor(w[:, 0, :, :], seg_max, wide4(pen), ALU.add))
            ready()
            did(v.tensor_tensor(top[:, :, :], w[:, 0, :, :], loop[:, :, :], ALU.max))
            ready()
            did(v.tensor_tensor(w[:, 0, :, :], w[:, 0, :, :], top[:, :, :], ALU.subtract))
            v.tensor_tensor(w[:, 1, :, :], loop[:, :, :], top[:, :, :], ALU.subtract).then_inc(S("exponents"), 1)
            ready()
            v.tensor_copy(mean, pen).then_inc(S("exponents"), 1)
            dve.wait_ge(S("weights"), 1)
            did(v.tensor_tensor(by_head(sums), by_head(sums), over_experts(w[:, 0, :, :]), ALU.mult))
            did(v.tensor_tensor(by_head(own[:, :, 4:20]), by_head(own[:, :, 4:20]), over_experts(w[:, 1, :, :]), ALU.mult))
            did(v.tensor_tensor(loop[:, :, :], total, w[:, 0, :, :], ALU.mult))
            ready()
            did(v.tensor_tensor(loop[:, :, :], loop[:, :, :], w[:, 1, :, :], ALU.add))
            did(v.tensor_tensor(sums, sums, own[:, :, 4:20], ALU.add))
            ready()
            did(v.tensor_scalar(loop[:, :, :], loop[:, :, :], 1e-16, None, ALU.add))
            ready()
            did(v.reciprocal(loop[:, :, :], loop[:, :, :]))
            ready()
            did(v.tensor_tensor(by_head(sums), by_head(sums), over_experts(loop[:, :, :]), ALU.mult))
            ready()
            did(v.tensor_tensor(sums, sums, each(vec[:, 2, :]), ALU.add))
            ready()
            did(v.tensor_reduce(mean, sums, AX.X, ALU.add))
            ready()
            did(v.tensor_scalar(mean, mean, 1.0 / 16, None, ALU.mult))
            ready()
            did(v.tensor_tensor(sums, sums, wide16(mean), ALU.subtract))
            ready()
            did(v.tensor_tensor(own[:, :, 4:20], sums, sums, ALU.mult))
            ready()
            did(v.tensor_reduce(var, own[:, :, 4:20], AX.X, ALU.add))
            ready()
            v.tensor_scalar(var, var, 1.0 / 16, EPS, ALU.mult, ALU.add).then_inc(S("variance"), 1)
            dve.wait_ge(S("rstd"), 1)
            did(v.tensor_tensor(sums, sums, wide16(rstd), ALU.mult))
            ready()
            did(v.tensor_tensor(sums, sums, each(vec[:, 0, :]), ALU.mult))
            ready()
            did(v.tensor_tensor(sums, sums, each(vec[:, 1, :]), ALU.add))
            ready()
            score = loop
            did(v.tensor_reduce(score[:, :, :], sums.rearrange("p b (h e) -> p b e h", e=EXPERTS), AX.X, ALU.add))
            ready()
            did(v.tensor_scalar(score[:, :, :], score[:, :, :], 1.0 / HEADS, None, ALU.mult))
            ready()
            beats = own[:, :, 4:20].rearrange("p b (i j) -> p b i j", j=EXPERTS)
            for i in range(EXPERTS):
                for j in range(EXPERTS):
                    op = ALU.is_gt if j <= i else ALU.is_ge
                    did(v.tensor_tensor(beats[:, :, i, j], score[:, :, i], score[:, :, j], op))
            did(v.tensor_reduce(mean, score[:, :, :], AX.X, ALU.max))
            ready()
            did(v.tensor_reduce(dst[:, :, :], beats, AX.X, ALU.add))
            v.tensor_tensor(w[:, 0, :, :], score[:, :, :], wide4(mean), ALU.subtract).then_inc(S("exponents"), 1)
            ready()
            did(v.tensor_scalar(dst[:, :, :], dst[:, :, :], 2.0, None, ALU.is_ge))
            dve.wait_ge(S("weights"), 2)
            ready()
            did(v.tensor_tensor(w[:, 0, :, :], w[:, 0, :, :], dst[:, :, :], ALU.mult))
            ready()
            did(v.tensor_reduce(var, w[:, 0, :, :], AX.X, ALU.add))
            ready()
            did(v.reciprocal(var, var))
            ready()
            did(v.tensor_tensor(top[:, :, :], w[:, 0, :, :], wide4(var), ALU.mult))
            dve.wait_ge(S("h_in"), 64)
            dve.wait_ge(S("y_in"), 64)
            ready()
            v.tensor_copy(mean, var).then_inc(S("mix_weights"), 1)
            mix(dve, v, 0, "mixed_even")

        @block.scalar
        def _(act):
            act.wait_ge(S("exponents"), 2)
            act.activation(w[:, :, :, :], w[:, :, :, :], ACT.Exp).then_inc(S("weights"), 1)
            act.wait_ge(S("exponents"), 3)
            act.activation(w[:, 0, :, :], w[:, 0, :, :], ACT.Exp).then_inc(S("weights"), 1)

        @block.gpsimd
        def _(pool):
            pool.memset(con[:, 0, :], -0.5).then_inc(S("pow_constant"), 1)
            pool.wait_ge(S("pow_constant"), 1)
            pool.wait_ge(S("variance"), 1)
            nc.gpsimd.tensor_tensor(one[:, 3, :], one[:, 2, :], con[:, 0, :], ALU.pow).then_inc(S("rstd"), 1)
            pool.wait_ge(S("mix_weights"), 1)
            pool.wait_ge(S("h_in"), 64)
            pool.wait_ge(S("y_in"), 64)
            mix(pool, nc.gpsimd, 1, "mixed_odd")


def program(nc, d):
    for name, shape in (("h2", (128, B * LAT)), ("zT", (128, G * GB // 2 * 128)), ("node_src", (NODES, CH)), ("node_dst", (NODES, HEADS)),
                        ("dst_at_start", (EDGES, HEADS)), ("edge_state", (EDGES, CH + HEADS)), ("expert_out", (128, B, EXPERTS * LAT))):
        d[name] = nc.dram_tensor(f"scratch_{name}", shape, F32, kind="Internal").ap()
    with ExitStack() as outer:
        seg = outer.enter_context(nc.sbuf_tensor("segment_rows", [128, B, CH + HEADS], F32))
        count = outer.enter_context(nc.sbuf_tensor("edge_count", [128, B], F32))
        with ExitStack() as ctx:
            keys = [ctx.enter_context(nc.sbuf_tensor(f"keys{i}", [128, EP], F32)) for i in range(2)]
            with ExitStack() as inner:
                res = inner.enter_context(nc.sbuf_tensor("res", [128, B, 2 * J], F32))
                cur = tokenizer_and_sort(nc, d, keys, res)
                attention(nc, d, res)
            graph(nc, d, keys, cur, seg, count)
        mix_experts(nc, d, seg, count)


def kernel(**inputs):
    from concourse import bacc
    from concourse.bass_utils import run_bass_kernel_spmd

    def tok(name):
        return inputs["L0_tok_" + name]

    def att(name):
        return inputs["L0_attn_" + name]

    def ffn(name):
        return inputs["L0_ffn_" + name]

    def twice(a):
        return np.concatenate([a, a], 0)

    def diagonal(a):
        z = np.zeros_like(a)
        return np.block([[a, z], [z, a]])

    arrays = constants()
    arrays["x"] = inputs["x"].transpose(1, 0, 3, 2).reshape(T, B, D * J)
    arrays["edges"] = ffn("edge_index")
    arrays["conv1_w"] = tok("conv1_w").transpose(1, 2, 3, 0)
    arrays["conv2_w"] = tok("conv2_w").transpose(1, 2, 3, 0)
    arrays["conv3_w"] = tok("conv3_w").reshape(2, T, T, KH, 2).transpose(2, 3, 4, 0, 1)
    arrays["conv_b"] = np.concatenate([tok("conv1_b"), tok("conv2_b"), tok("conv3_b")]).reshape(4, T).T
    for v in "gb":
        arrays[f"ln0_{v}"] = tok(f"ln0_{v}").reshape(J, D).T.reshape(-1)
        arrays[f"ln1_{v}0"] = tok(f"ln1_{v}").reshape(J, 2).T.reshape(-1)
        arrays[f"ln1_{v}1"] = tok(f"ln1_{v}")
    arrays["out_w"], arrays["out_b"] = tok("out_w"), tok("out_b")
    arrays["w_qkv"] = np.stack([diagonal(att("Wq").T), diagonal(att("Wkv").T)], 1)
    arrays["w_proj"] = diagonal(att("Wproj").T)
    arrays["w_mlp1"] = twice(att("W1").T)
    arrays["w_mlp2"] = att("W2").T.reshape(2, 128, LAT).transpose(1, 0, 2)
    arrays["w_gat"] = twice(ffn("W_gat"))
    arrays["norm_cols"] = np.stack([twice(att(v)) for v in ("norm1_g", "norm1_b", "norm2_g", "norm2_b")] + list(att("b1").reshape(2, 128)), 1)
    arrays["proj_b"], arrays["mlp_b"] = att("bproj"), att("b2")
    arrays["att0"], arrays["att1"] = ffn("att_src").reshape(-1), ffn("att_dst").reshape(-1)
    arrays["w_expert1"] = twice(ffn("W1").transpose(1, 0, 2))
    arrays["w_expert2"] = ffn("W2").transpose(1, 0, 2)
    arrays["b_expert1"], arrays["b_expert2"] = ffn("b1").T, ffn("b2").reshape(-1)
    arrays["score_gain"], arrays["score_shift"], arrays["score_bias"] = ffn("ln_gamma"), ffn("ln_beta"), ffn("b_gat")

    nc = bacc.Bacc("TRN2", target_bir_lowering=False, num_devices=1)
    given, d = {}, {}
    for name, a in arrays.items():
        a = np.ascontiguousarray(a)
        given[f"in_{name}_dram"] = a
        d[name] = nc.dram_tensor(f"in_{name}_dram", a.shape, mybir.dt.from_np(a.dtype), kind="ExternalInput").ap()
    d["out"] = nc.dram_tensor("out_0_dram", (B, T, LAT), F32, kind="ExternalOutput").ap()
    program(nc, d)
    result = run_bass_kernel_spmd(nc, [given], core_ids=[0])
    return result.results[0]["out_0_dram"]
```

```python
import numpy as np
import concourse.bass as bass
from concourse import mybir
from contextlib import ExitStack

F32 = mybir.dt.float32
I32 = mybir.dt.int32
U32 = mybir.dt.uint32
BF16 = mybir.dt.bfloat16
F32R = mybir.dt.float32r
ALU = mybir.AluOpType
ACT = mybir.ActivationFunctionType
AX = mybir.AxisListType


B, T, J, D = 128, 128, 64, 3
LAT = 64
NODES = B * T
EDGES = 262144
KH = 5
JP = J + KH - 1
GB = 8
G = B // GB
EP = EDGES // 128
EPS = 1e-5
NEG = -1.0e30
LOG_EP = EP.bit_length() - 1
LOG_E = EDGES.bit_length() - 1
NODE_BITS = NODES.bit_length() - 1
KEY_TOP = 1 << (2 * NODE_BITS)


class Names:

    def __init__(self, nc, ctx, stage):
        self.nc, self.ctx, self.stage, self.sems = nc, ctx, stage, {}

    def sem(self, name):
        if name not in self.sems:
            self.sems[name] = self.nc.alloc_semaphore(f"{self.stage}_{name}")
        return self.sems[name]

    def release(self):
        self.nc.all_engine_barrier()
        self.nc.clear_and_free_semaphores(list(self.sems.values()))
        self.nc.all_engine_barrier()

    def sb(self, name, shape, dtype=F32):
        return self.ctx.enter_context(self.nc.sbuf_tensor(name, shape, dtype))

    def ps(self, name, shape, dtype=F32):
        return self.ctx.enter_context(self.nc.psum_tensor(name, shape, dtype))


def after(engine, sem, value):
    if not isinstance(value, int) or value > 0:
        engine.wait_ge(sem, value)


def sign_of_level(k):
    p = np.arange(128)
    if k < LOG_EP or k == LOG_E:
        return np.ones(128)
    return 1.0 - 2.0 * ((p >> (k - LOG_EP)) & 1)


def constants():
    p = np.arange(128)
    head = (p % LAT) // 8
    same = (p[:, None] // LAT == p[None, :] // LAT) & (head[:, None] == head[None, :]) & (head[:, None] > 0)
    return {
        "c_ident": np.eye(128, dtype=np.float32),
        "c_sign": np.stack([sign_of_level(k - 1) * sign_of_level(k) for k in range(LOG_EP, LOG_E + 1)], 1).astype(np.float32),
        "c_headmask": same.astype(np.float32),
        "c_upto": (p[:, None] <= p[None, :]).astype(np.float32),
        "c_rowpos": (p * EP).astype(np.float32)[:, None],
        "c_ones": np.ones((128, 128), np.float32),
        "c_ramp": np.tile(p.astype(np.float32), (128, 1)),
    }


def tokenizer_and_sort(nc, d, keys):
    ctx = ExitStack()
    with ctx:
        n = Names(nc, ctx, "tok")
        S = n.sem
        w1 = n.sb("w_conv1", [128, 2, KH, 3, 128], F32R)
        w2 = n.sb("w_conv2", [128, 2, KH, 2, 128], F32R)
        w3 = n.sb("w_conv3", [128, 2, KH, 2, 2, 128], F32R)
        cb = n.sb("conv_bias", [128, 4])
        g0 = n.sb("ln0_gain", [128, D * J])
        b0 = n.sb("ln0_shift", [128, D * J])
        g1 = n.sb("ln1_gain", [128, 2, 2 * J])
        b1 = n.sb("ln1_shift", [128, 2, 2 * J])
        sgn = n.sb("sort_signs", [128, LOG_E - LOG_EP + 1])
        xraw = [n.sb(f"x_raw{i}", [128, GB, D * J]) for i in range(2)]
        y0 = [n.sb(f"conv1_in{i}", [128, 2, GB, D, JP], F32R) for i in range(2)]
        y1 = [n.sb(f"conv2_in{i}", [128, 2, GB, D, JP], F32R) for i in range(2)]
        y2 = [n.sb(f"conv3_in{i}", [128, 2, GB, 2, JP], F32R) for i in range(2)]
        normed = [n.sb(f"normed{i}", [128, GB, 2 * J]) for i in range(2)]
        r = [xraw, n.sb("relu1", [128, GB, D * J]), n.sb("relu2", [128, GB, 2 * J]), n.sb("relu3", [128, GB, 2 * J])]
        dump = [n.sb(f"act_dump{k}", [128, GB, w], BF16) for k, w in enumerate((D * J, D * J, 2 * J, 2 * J))]
        dump_x = n.sb("act_dump_x", [128, GB, D * J], BF16)
        stat = [n.sb(f"stat{k}", [128, 6, GB]) for k in range(4)]
        sum3 = n.sb("sum3_half", [128, GB])
        zeros = n.sb("zeros", [128, 2 * GB * D, KH // 2])
        half = n.sb("minus_half", [128, GB])
        eps = n.sb("eps", [128, GB])
        inv = n.sb("inverse_width", [128, 4, GB])
        minus_inv = n.sb("minus_inverse_width", [128, 4, GB])
        c1 = n.ps("conv1_out", [128, D, GB * J])
        c2 = n.ps("conv2_out", [128, 2, GB * J])
        c3 = n.ps("conv3_out", [128, 2, GB * J])
        block = ctx.enter_context(nc.Block())

        widths = (D * J, D * J, 2 * J, 2 * J)

        FIRST, LOOP0, PAIRS, LAST0, END = -1, 4, (G - 6) // 2, G - 2, G + 2
        PASSES_A_SPLIT = 4
        ZEROED = 1 + 2 + 8

        flat = [w1[...].rearrange("p i a b c -> p i (a b c)"), w2[...].rearrange("p i a b c -> p i (a b c)"),
                w3[...].rearrange("p i a b c e -> p i (a b c e)")]
        given = [d["conv1_w"].rearrange("p a b c -> p (a b c)"), d["conv2_w"].rearrange("p a b c -> p (a b c)"),
                 d["conv3_w"].rearrange("p a b c e -> p (a b c e)")]
        cut = KH * 2 * 128
        weight_pieces = [(keys[k % 2][:, 0:hi - lo], flat[m][:, :, lo:hi], given[m][:, lo:hi])
                         for k, (m, lo, hi) in enumerate(((0, 0, KH * 3 * 128), (1, 0, cut), (2, 0, cut), (2, cut, 2 * cut)))]
        PIECES = (1, 2, 4)

        def in_turn(s, turns):
            return sorted(turns, key=lambda t: t[1]) if isinstance(s, int) and s < 1 else turns

        exchanges = []
        count = [0]
        cur = [0]

        @block.vector
        def _(dve):
            def split_layer(k, g):
                y = (y0, y1, y2)[k][g % 2]
                whole = (xraw[g % 2] if k == 0 else r[k])[:, :, :].rearrange("p b (d j) -> p b d j", j=J)
                dve.wait_ge(S(f"shifted{k}"), g + 1)
                after(dve, S(f"conv{k}_done"), g - 1)
                upper, rest = (y[:, i, :, :, KH // 2:KH // 2 + J] for i in range(2))
                nc.vector.tensor_copy(upper, whole).then_inc(S(f"upper{k}"), 1)
                dve.wait_ge(S(f"upper{k}"), g + 1)
                nc.vector.tensor_tensor(rest, whole, upper.bitcast(F32), ALU.subtract).then_inc(S(f"y{k}_ready"), 1)

            splits = [(k, s + 1 - k) for s in range(FIRST, END) for k in range(3) if 0 <= s + 1 - k < G]
            passes = [0]

            def between():
                passes[0] += 1
                at, rest = divmod(passes[0], PASSES_A_SPLIT)
                if rest == 0 and at < len(splits):
                    split_layer(*splits[at])

            def did(i):
                i.then_inc(S("sort"), 1)
                count[0] += 1

            def stage(level, j):
                dve.wait_ge(S("sort"), count[0])
                A, Bk = keys[cur[0]], keys[1 - cur[0]]
                if level < LOG_EP:
                    pat, kw = "p (g r m h d) -> p r h g m d", dict(r=2, m=2 ** (level - 1 - j), h=2, d=2 ** j)
                    a, b = A[:, :].rearrange(pat, **kw), Bk[:, :].rearrange(pat, **kw)
                    for up in range(2):
                        for h in range(2):
                            did(nc.vector.tensor_tensor(b[:, up, h], a[:, up, 0], a[:, up, 1], ALU.min if up == h else ALU.max))
                else:
                    pat, kw = "p (m h d) -> p h m d", dict(h=2, d=2 ** j)
                    a, b = A[:, :].rearrange(pat, **kw), Bk[:, :].rearrange(pat, **kw)
                    for h in range(2):
                        did(nc.vector.tensor_tensor(b[:, h], a[:, 0], a[:, 1], ALU.max if h else ALU.min))
                cur[0] ^= 1
                between()

            def transpose():
                dve.wait_ge(S("sort"), count[0])
                did(nc.vector.transpose(keys[1 - cur[0]][:, :], keys[cur[0]][:, :]))
                cur[0] ^= 1
                between()

            def turn(col):
                dve.wait_ge(S("sort"), count[0])
                did(nc.vector.tensor_scalar(keys[1 - cur[0]][:, :], keys[cur[0]][:, :], sgn[:, col:col + 1], None, ALU.mult))
                cur[0] ^= 1
                between()

            def exchange(bits):
                exchanges.append((count[0], cur[0], bits))
                dve.wait_ge(S("exchanged"), 16 * sum((4 >> b) << (2 * b) for _, _, b in exchanges))
                cur[0] ^= 1

            for k, (raw, w, _) in enumerate(weight_pieces):
                dve.wait_ge(S(f"w_in{k}"), 16)
                nc.vector.tensor_copy(w[:, 0, :], raw).then_inc(S("w_upper"), 1)
                dve.wait_ge(S("w_upper"), k + 1)
                nc.vector.tensor_tensor(w[:, 1, :], raw, w[:, 0, :].bitcast(F32), ALU.subtract).then_inc(S("w_split"), 1)
            dve.wait_ge(S("zeroed"), ZEROED)
            for y in (*y0, *y1, *y2):
                rows = y[...].rearrange("p i b d j -> p (i b d) j")
                for side in (slice(0, KH // 2), slice(KH // 2 + J, JP)):
                    nc.vector.tensor_copy(rows[:, :, side], zeros[:, 0:rows.shape[1], :]).then_inc(S("padded"), 1)
            dve.wait_ge(S("padded"), 12)
            split_layer(*splits[0])
            dve.wait_ge(S("keys_in"), 48)
            dst, src = keys[0][:, :].bitcast(I32), keys[1][:, :].bitcast(I32)
            did(nc.vector.tensor_scalar(dst, dst, NODE_BITS, None, ALU.logical_shift_left))
            dve.wait_ge(S("sort"), count[0])
            did(nc.vector.tensor_tensor(src, dst, src, ALU.bitwise_or))
            dve.wait_ge(S("sort"), count[0])
            did(nc.vector.tensor_scalar(src, src, KEY_TOP, None, ALU.bitwise_or))
            cur[0] = 1
            for level in range(1, LOG_E + 1):
                if level >= LOG_EP:
                    turn(level - LOG_EP)
                quadrant_bits = max(0, level - 16)
                if quadrant_bits:
                    exchange(quadrant_bits)
                    for j in range(quadrant_bits - 1, -1, -1):
                        stage(level + LOG_EP, LOG_EP - quadrant_bits + j)
                if level > LOG_EP:
                    transpose()
                    for j in range(min(level, 16) - LOG_EP - 1, -1, -1):
                        stage(level + LOG_EP, j)
                    transpose()
                if quadrant_bits:
                    exchange(quadrant_bits)
                for j in range(min(level, LOG_EP) - 1, -1, -1):
                    stage(level, j)
            for k, g in splits[passes[0] // PASSES_A_SPLIT + 1:]:
                split_layer(k, g)

        @block.sync
        def _(sp):
            for k, (raw, _, given) in enumerate(weight_pieces):
                after(sp, S("w_split"), k - 1)
                sp.dma_start(raw, given).then_inc(S(f"w_in{k}"), 16)
            sp.wait_ge(S("w_split"), len(weight_pieces))
            sp.dma_start(keys[0][:, :].bitcast(I32), d["edges"][1].rearrange("(p f) -> p f", p=128)).then_inc(S("keys_in"), 16)
            sp.dma_start(keys[1][:, :].bitcast(I32), d["edges"][0].rearrange("(p f) -> p f", p=128)).then_inc(S("keys_in"), 16)
            sp.dma_start(sgn[:, :], d["c_sign"]).then_inc(S("keys_in"), 16)
            for count, src, bits in exchanges:
                sp.wait_ge(S("sort"), count)
                A, Bk = keys[src], keys[1 - src]
                w = EP >> bits
                for top in range(4 >> bits):
                    for f in range(1 << bits):
                        for p in range(1 << bits):
                            to, at = 32 * ((top << bits) + f), 32 * ((top << bits) + p)
                            sp.dma_start(Bk[to:to + 32, p * w:(p + 1) * w], A[at:at + 32, f * w:(f + 1) * w]).then_inc(S("exchanged"), 16)


        @block.tensor
        def _(pe):
            def conv(k, g, par, src, w, out, taps):
                if isinstance(g, int):
                    pe.wait_ge(S("w_split"), PIECES[k])
                pe.wait_ge(S(f"y{k}_ready"), g + 1)
                after(pe, S(f"sum{k + 1}"), g)
                for bank, cols in taps:
                    for i, (dd, kh, wt) in enumerate(cols):
                        for q, (a, b) in enumerate(((0, 0), (0, 1), (1, 0))):
                            m = nc.tensor.matmul(out[:, bank, :].rearrange("p (b j) -> p b j", j=J), wt(a),
                                                 src[par][:, b, :, dd, kh:kh + J], start=(i == 0 and q == 0), stop=(i == len(cols) - 1 and q == 2))
                m.then_inc(S(f"conv{k}_done"), 1)

            taps0 = [(o, [(o + kw - 1, kh, (lambda a, kh=kh, kw=kw: w1[:, a, kh, kw, :])) for kw in range(3) if 0 <= o + kw - 1 < D for kh in range(KH)]) for o in range(D)]
            taps1 = [(o, [(o + kw, kh, (lambda a, kh=kh, kw=kw: w2[:, a, kh, kw, :])) for kw in range(2) for kh in range(KH)]) for o in range(2)]
            taps2 = [(h, [(kw, kh, (lambda a, kh=kh, kw=kw, h=h: w3[:, a, kh, kw, h, :])) for kw in range(2) for kh in range(KH)]) for h in range(2)]

            def step(s, par, a, b, c):
                if a:
                    conv(0, s, par, y0, w1, c1, taps0)
                if b:
                    conv(1, s - 1, 1 - par, y1, w2, c2, taps1)
                if c:
                    conv(2, s - 2, par, y2, w3, c3, taps2)

            for s in range(0, LOOP0):
                step(s, s % 2, True, s >= 1, s >= 2)
            with pe.Fori(0, PAIRS) as i:
                for par in range(2):
                    step(2 * i + (LOOP0 + par), par, True, True, True)
            for s in range(LAST0, END):
                step(s, s % 2, s < G, s - 1 < G, True)

        @block.scalar
        def _(act):
            act.dma_start(cb[:, :], d["conv_b"]).then_inc(S("act_w_in"), 16)

            def load(g, par):
                act.dma_start(xraw[par][:, :, :], d["x"][:, bass.ds(g * GB, GB), :]).then_inc(S(f"x_in{par}"), 16)

            def store(g, par):
                act.dma_start(d["res"][:, bass.ds(g * GB, GB), :], normed[par][:, :, :]).then_inc(S(f"res_out{par}"), 16)

            def sums(k, g, par):
                after(act, S("res_ready" if k == 3 else f"y{k}_ready"), g)
                if k == 3 and (not isinstance(g, int) or g > 0):
                    store(g - 1, 1 - par)
                if k == 0:
                    act.wait_ge(S(f"x_in{par}"), 8 * (g - par) + 16)
                else:
                    act.wait_ge(S(f"conv{k - 1}_done"), g + 1)
                for b in range(GB):
                    if k == 0:
                        o = act.activation(dump_x[:, b, :], xraw[par][:, b, :], ACT.Identity, accum_out=stat[0][:, 0, b:b + 1])
                    elif k < 3:
                        c = (None, c1, c2)[k]
                        w = widths[k] // J
                        o = act.activation(r[k][:, b, :].rearrange("p (d j) -> p d j", j=J), c[:, 0:w, b * J:(b + 1) * J],
                                           ACT.Relu, bias=cb[:, k - 1:k], accum_out=stat[k][:, 0, b:b + 1])
                    else:
                        for h in range(2):
                            o = act.activation(r[3][:, b, h * J:(h + 1) * J], c3[:, h, b * J:(b + 1) * J], ACT.Relu,
                                               bias=cb[:, 2 + h:3 + h], accum_out=(sum3 if h else stat[3][:, 0])[:, b:b + 1])
                o.then_inc(S(f"sum{k}"), 1)

            def squares(k, g, par):
                act.wait_ge(S(f"mean{k}"), g + 1)
                src = r[0][par] if k == 0 else r[k]
                for b in range(GB):
                    o = act.activation(dump[k][:, b, :], src[:, b, :], ACT.Square, bias=stat[k][:, 1, b:b + 1],
                                       accum_out=stat[k][:, 2, b:b + 1])
                o.then_inc(S(f"sq{k}"), 1)

            def normalise(k, g, par):
                act.wait_ge(S(f"scaled_mean{k}"), g + 1)
                src = r[0][par] if k == 0 else r[k]
                for b in range(GB):
                    o = act.activation(src[:, b, :], src[:, b, :], ACT.Identity, scale=stat[k][:, 4, b:b + 1], bias=stat[k][:, 5, b:b + 1])
                o.then_inc(S(f"norm{k}"), 1)

            def step(s, par, *on):
                turns = ((sums, 0), (sums, 1), (squares, 0), (normalise, 0), (squares, 1), (sums, 2), (normalise, 1),
                         (squares, 2), (sums, 3), (squares, 3), (normalise, 2), (normalise, 3))
                for what, k in in_turn(s, turns):
                    if on[k]:
                        what(k, s + 1 - k, par if k % 2 else 1 - par)

            load(0, 0)
            load(1, 1)
            act.wait_ge(S("act_w_in"), 16)

            def load_ahead(s, par):
                act.wait_ge(S("y0_ready"), s + 2)
                load(s + 3, 1 - par)

            for s in range(FIRST, LOOP0):
                step(s, s % 2, True, s >= 0, s >= 1, s >= 2)
                load_ahead(s, s % 2)
            with act.Fori(0, PAIRS - 1) as i:
                for par in range(2):
                    step(2 * i + (LOOP0 + par), par, True, True, True, True)
                    load_ahead(2 * i + (LOOP0 + par), par)
            for s in range(LAST0 - 2, END):
                step(s, s % 2, s + 1 < G, s < G, s - 1 < G, True)
                if s + 3 < G:
                    load_ahead(s, s % 2)
            act.wait_ge(S("res_ready"), G)
            store(G - 1, 1)
            for par in range(2):
                act.wait_ge(S(f"res_out{par}"), 16 * (G // 2))

        @block.gpsimd
        def _(pool):
            pool.dma_start(g0[:, :], d["ln0_g"].partition_broadcast(128)).then_inc(S("pool_in"), 16)
            pool.dma_start(b0[:, :], d["ln0_b"].partition_broadcast(128)).then_inc(S("pool_in"), 16)
            for v in range(2):
                pool.dma_start(g1[:, v, :], d[f"ln1_g{v}"].partition_broadcast(128)).then_inc(S("pool_in"), 16)
                pool.dma_start(b1[:, v, :], d[f"ln1_b{v}"].partition_broadcast(128)).then_inc(S("pool_in"), 16)
            pool.memset(zeros[:, :, :].rearrange("p r j -> p (r j)"), 0.0).then_inc(S("zeroed"), 1)
            pool.memset(half[:, :], -0.5).then_inc(S("zeroed"), 1)
            pool.memset(eps[:, :], EPS).then_inc(S("zeroed"), 1)
            for k in range(4):
                pool.memset(inv[:, k, :], 1.0 / widths[k]).then_inc(S("zeroed"), 1)
                pool.memset(minus_inv[:, k, :], -1.0 / widths[k]).then_inc(S("zeroed"), 1)
            pool.wait_ge(S("zeroed"), ZEROED)
            pool.wait_ge(S("pool_in"), 96)

            def mean(k, g, par):
                pool.wait_ge(S(f"sum{k}"), g + 1)
                total = stat[k][:, 0, :]
                if k == 3:
                    nc.gpsimd.tensor_tensor(stat[3][:, 3, :], total, sum3[:, :], ALU.add).then_inc(S("sum3_both"), 1)
                    pool.wait_ge(S("sum3_both"), g + 1)
                    total = stat[3][:, 3, :]
                nc.gpsimd.tensor_tensor(stat[k][:, 1, :], total, minus_inv[:, k, :], ALU.mult).then_inc(S(f"mean{k}"), 1)

            def deviation(k, g, par):
                pool.wait_ge(S(f"sq{k}"), g + 1)
                st = stat[k]
                nc.gpsimd.tensor_tensor(st[:, 3, :], st[:, 2, :], inv[:, k, :], ALU.mult).then_inc(S(f"var{k}"), 1)
                pool.wait_ge(S(f"var{k}"), g + 1)
                nc.gpsimd.tensor_tensor(st[:, 3, :], st[:, 3, :], eps[:, :], ALU.add).then_inc(S(f"vareps{k}"), 1)
                pool.wait_ge(S(f"vareps{k}"), g + 1)
                nc.gpsimd.tensor_tensor(st[:, 4, :], st[:, 3, :], half[:, :], ALU.pow).then_inc(S(f"std{k}"), 1)
                pool.wait_ge(S(f"std{k}"), g + 1)
                nc.gpsimd.tensor_tensor(st[:, 5, :], st[:, 1, :], st[:, 4, :], ALU.mult).then_inc(S(f"scaled_mean{k}"), 1)

            def wide(k, v):
                return v.unsqueeze(1).broadcast_to([128, GB, widths[k]])

            gains = (g0[:, :], g0[:, :], g1[:, 0, :], g1[:, 1, :])
            shifts = (b0[:, :], b0[:, :], b1[:, 0, :], b1[:, 1, :])

            def gain(k, g, par):
                pool.wait_ge(S(f"norm{k}"), g + 1)
                src = r[0][par] if k == 0 else r[k]
                nc.gpsimd.tensor_tensor(src[:, :, :], src[:, :, :], wide(k, gains[k]), ALU.mult).then_inc(S(f"gain{k}"), 1)

            def shift(k, g, par):
                pool.wait_ge(S(f"gain{k}"), g + 1)
                src = r[0][par] if k == 0 else r[k]
                if k < 3:
                    nc.gpsimd.tensor_tensor(src[:, :, :], src[:, :, :], wide(k, shifts[k]), ALU.add).then_inc(S(f"shifted{k}"), 1)
                else:
                    after(pool, S(f"res_out{par}"), 8 * (g - par))
                    nc.gpsimd.tensor_tensor(normed[par][:, :, :], src[:, :, :], wide(k, shifts[k]), ALU.add).then_inc(S("res_ready"), 1)

            def step(s, par, *on):
                turns = ((mean, 0), (deviation, 0), (mean, 1), (gain, 0), (deviation, 1), (shift, 0), (mean, 2), (gain, 1),
                         (shift, 1), (mean, 3), (deviation, 3), (deviation, 2), (gain, 2), (shift, 2), (gain, 3), (shift, 3))
                for what, k in in_turn(s, turns):
                    if on[k]:
                        what(k, s + 1 - k, par if k % 2 else 1 - par)

            for s in range(FIRST, LOOP0):
                step(s, s % 2, True, s >= 0, s >= 1, s >= 2)
            with pool.Fori(0, PAIRS) as i:
                for par in range(2):
                    step(2 * i + (LOOP0 + par), par, True, True, True, True)
            for s in range(LAST0, END):
                step(s, s % 2, s + 1 < G, s < G, s - 1 < G, True)
    n.release()
    return cur[0]


def attention(nc, d):
    ctx = ExitStack()
    with ctx:
        n = Names(nc, ctx, "attn")
        S = n.sem
        P2, PC = GB // 2, GB // 2 * 128
        ident = n.sb("ident", [128, 128])
        headmask = n.sb("headmask", [128, 128])
        w_out = n.sb("w_out", [128, LAT])
        w_qkv = n.sb("w_qkv", [128, 2, 128])
        w_qkv_g = n.sb("w_qkv_g", [128, 2, 128])
        w_proj = n.sb("w_proj", [128, 128])
        w_1 = n.sb("w_mlp1", [128, 256])
        w_1g = n.sb("w_mlp1_g", [128, 256])
        w_2 = n.sb("w_mlp2", [128, 2, LAT])
        w_gat = n.sb("w_gat", [128, 16])
        w_att = n.sb("w_att", [128, 2, 16])
        w_node = n.sb("w_node", [128, 2, 24])
        att_tmp = n.sb("att_tmp", [128, 2, 16])
        cols = n.sb("norm_cols", [128, 6])
        out_b = n.sb("out_b", [128, LAT])
        proj_b = n.sb("proj_b", [128, LAT])
        mlp_b = n.sb("mlp_b", [128, LAT])
        qkv_b = n.sb("qkv_bias", [128, 2, 128])
        qk_bc = n.sb("qk_bias_cols", [128, 2])
        hid_b = n.sb("hidden_bias", [128, 2])
        shift1 = n.sb("shift1_wide", [128, 128])
        con = n.sb("minus_one_half", [128, 1, GB])
        resg = [n.sb(f"res_group{i}", [128, GB, 128]) for i in range(2)]
        resT = n.sb("resT", [128, GB * 128])
        cenA = n.sb("cenA", [128, GB, LAT])
        sqA = n.sb("sqA", [128, GB, LAT])
        nA = n.sb("nA", [128, GB, LAT])
        ub = [n.sb(f"u_plus_bias{i}", [128, GB, LAT]) for i in range(2)]
        nT = [n.sb(f"nT{i}", [128, PC]) for i in range(2)]
        stA = n.sb("statA", [128, 6, GB])
        qkv = n.sb("qkv", [128, 2, GB, LAT])
        kvT = n.sb("kvT", [128, PC])
        qT = n.sb("qT", [128, PC])
        nkmax = n.sb("minus_kmax", [128, P2])
        ET = n.sb("expkT", [128, PC])
        ksum = n.sb("ksum", [128, P2])
        rks = n.sb("one_over_ksum", [128, P2])
        E = n.sb("expk", [128, PC])
        ctx2 = n.sb("context", [128, P2, 128])
        qmax = n.sb("qmax", [128, GB, 7])
        qexp = n.sb("qexp", [128, GB, 7, 8])
        qsum = n.sb("qsum", [128, GB, 7])
        qs = n.sb("qsoft", [128, GB, LAT])
        qsT = n.sb("qsoftT", [128, PC])
        ndmax = n.sb("minus_dots_max", [128, 2, GB])
        prob = n.sb("prob", [128, GB, 128])
        psm = n.sb("prob_sum", [128, 2, GB])
        probT = n.sb("probT", [128, GB * 128])
        O = n.sb("attn_out", [128, GB, LAT])
        OT = n.sb("attn_outT", [128, PC])
        x1 = [n.sb(f"x1_{i}", [128, GB, LAT]) for i in range(2)]
        cenC = n.sb("cenC", [128, GB, LAT])
        sqC = n.sb("sqC", [128, GB, LAT])
        n2T = n.sb("n2T", [128, PC])
        stC = n.sb("statC", [128, 5, GB])
        hx = n.sb("h_plus_x1", [128, GB, LAT])
        h = [n.sb(f"h_{i}", [128, GB, LAT]) for i in range(2)]
        hnew = [n.sb(f"h_new{i}", [128, GB, LAT]) for i in range(2)]
        hid = n.sb("hidden", [128, 2, 2, PC])
        zTg = n.sb("zT_group", [128, PC])
        tabg = [n.sb(f"table_group{i}", [128, GB, 24]) for i in range(2)]

        B01 = n.ps("bank01", [128, 1024])
        B2 = n.ps("bank2", [128, 512])
        B34 = n.ps("bank34", [128, 1024])
        B5 = n.ps("bank5", [128, 512])
        B6 = n.ps("bank6", [128, 512])
        B7 = n.ps("bank7", [128, 512])
        block = ctx.enter_context(nc.Block())
        SCALE = 8 ** -0.5

        def group(ap):
            return ap.rearrange("p (b c) -> p b c", c=LAT)

        def wide(stat):
            return stat.unsqueeze(2).broadcast_to([128, GB, LAT])

        def over(row):
            return row.unsqueeze(1).broadcast_to([128, GB, LAT])

        def rows(ap, g):
            return ap[:, bass.ds(g * GB, GB), :]

        FIRST, LOOP0, PAIRS, LAST0, END = 0, 4, (G - 4) // 2, G, G + 2

        def run(engine, step):
            for s in range(FIRST, LOOP0):
                step(s, s % 2, True, s >= 1, s >= 2)
            with engine.Fori(0, PAIRS) as i:
                for par in range(2):
                    step(2 * i + (LOOP0 + par), par, True, True, True)
            for s in range(LAST0, END):
                step(s, s % 2, False, s - 1 < G, True)

        @block.sync
        def _(sp):
            for t, name in ((ident, "c_ident"), (headmask, "c_headmask"), (w_out, "out_w"), (w_proj, "w_proj"),
                            (w_1, "w_mlp1"), (w_gat, "w_gat"), (cols, "norm_cols")):
                sp.dma_start(t[:, :], d[name]).then_inc(S("w_in"), 16)
            sp.dma_start(w_2[:, :, :], d["w_mlp2"]).then_inc(S("w_in"), 16)
            sp.dma_start(w_qkv[:, :, :], d["w_qkv"]).then_inc(S("w_in"), 16)
            for t, name in ((out_b, "out_b"), (proj_b, "proj_b"), (mlp_b, "mlp_b")):
                sp.dma_start(t[:, :], d[name].partition_broadcast(128)).then_inc(S("w_in"), 16)
            for k in range(2):
                sp.dma_start(w_att[:, k, :], d[f"att{k}"].partition_broadcast(128)).then_inc(S("w_in"), 16)

            def fetch(g, par):
                sp.dma_start(resg[par][:, :, :], rows(d["res"], g)).then_inc(S(f"res_in{par}"), 16)

            fetch(0, 0)
            fetch(1, 1)

            def step(s, par, a, b, c):
                if a:
                    sp.wait_ge(S("resT_ps"), s + 1)
                    if not isinstance(s, int) or s + 2 < G:
                        fetch(s + 2, par)
                if c:
                    g = s - 2
                    sp.wait_ge(S("hnew"), g + 1)
                    sp.dma_start(d["h2"][:, bass.ds(g * GB * LAT, GB * LAT)], hnew[par][:, :, :].rearrange("p b c -> p (b c)")).then_inc(S(f"h_out{par}"), 16)
                    sp.wait_ge(S("zT"), g + 1)
                    sp.dma_start(d["zT"][:, bass.ds(g * PC, PC)], zTg[:, :]).then_inc(S("zT_out"), 16)
                    sp.wait_ge(S("table"), g + 1)
                    for name, cut in (("node_src", slice(0, 20)), ("node_dst", slice(20, 24))):
                        sp.dma_start(d[name].rearrange("(b t) c -> t b c", t=128)[:, bass.ds(g * GB, GB), :], tabg[par][:, :, cut])\
                          .then_inc(S(f"table_out{par}"), 16)

            for s in range(FIRST, LOOP0):
                step(s, s % 2, True, s >= 1, s >= 2)
            with sp.Fori(0, PAIRS - 1) as i:
                for par in range(2):
                    step(2 * i + (LOOP0 + par), par, True, True, True)
            for s in range(LAST0 - 2, END):
                step(s, s % 2, s < G, s - 1 < G, True)
            sp.wait_ge(S("zT_out"), 16 * G)
            for par in range(2):
                sp.wait_ge(S(f"table_out{par}"), 32 * (G // 2))
                sp.wait_ge(S(f"h_out{par}"), 16 * (G // 2))

        @block.tensor
        def _(pe):
            mm, tr = nc.tensor.matmul, nc.tensor.transpose
            one = dict(start=True, stop=True)
            pe.wait_ge(S("w_in"), 16 * 14)
            pe.wait_ge(S("w_ready"), 1)
            for k in range(2):
                mm(B7[:, 128 * k:128 * k + 128], shift1[:, :], w_qkv[:, k, :], **one)
                mm(B7[:, 256 + k:257 + k], w_qkv[:, k, :], cols[:, 1:2], **one)
            for m in range(2):
                last = mm(B6[:, m:m + 1], w_1[0:LAT, 128 * m:128 * (m + 1)], cols[0:LAT, 3:4], **one)
            last.then_inc(S("bias_ps"), 1)
            pe.wait_ge(S("bias_sb"), 1)

            def sample(b):
                return slice(LAT * (b % 2), LAT * (b % 2) + LAT), slice(128 * (b // 2), 128 * (b // 2) + 128)

            def slot(b):
                k = GB // 2 * (b % 2) + b // 2
                return slice(128 * k, 128 * k + 128)

            def pair_columns(p):
                return slice(128 * p, 128 * p + 128)

            def hidden_layer(k):
                m, i = k // 2, k % 2
                half = slice(LAT * i, LAT * (i + 1))
                return mm(B01[:, 512 * i:512 * i + 512], w_1g[half, 128 * m:128 * m + 128], n2T[half, :], **one)

            def step(s, par, a, b_, c):
                A, B, C = s, s - 1, s - 2
                if a:
                    pe.wait_ge(S(f"res_in{par}"), 8 * (A - par) + 16)
                    after(pe, S("gelu"), A - 2)
                    after(pe, S("resT_sb"), A)
                    for b in range(GB):
                        m = tr(B01[:, 128 * b:128 * b + 128], resg[par][:, b, :], ident[:, :])
                    m.then_inc(S("resT_ps"), 1)
                if b_:
                    pe.wait_ge(S("nT"), B + 1)
                    after(pe, S("x1"), B)
                    mm(B5[:, :], w_qkv_g[:, 1, :], nT[1 - par][:, :], **one).then_inc(S("kvT_ps"), 1)
                    pe.wait_ge(S("nT"), B + 1)
                    after(pe, S("probT_sb"), B)
                    for k in range(2):
                        for p in range(P2):
                            m = mm(B34[:, 512 * k + 128 * p:512 * k + 128 * p + 128], nT[1 - par][:, pair_columns(p)], w_qkv_g[:, k, :], **one)
                    m.then_inc(S("qkv_ps"), 1)
                if a:
                    pe.wait_ge(S("resT_sb"), A + 1)
                    after(pe, S("nT"), A)
                    for b in range(GB):
                        m = mm(B2[:, LAT * b:LAT * b + LAT], resT[:, 128 * b:128 * b + 128], w_out[:, :], **one)
                    m.then_inc(S("h_ps"), 1)
                if b_:
                    pe.wait_ge(S("ET"), B + 1)
                    for p in range(P2):
                        m = tr(B5[:, pair_columns(p)], ET[:, pair_columns(p)], ident[:, :])
                    m.then_inc(S("E_ps"), 1)
                if c:
                    pe.wait_ge(S("n2"), C + 1)
                    after(pe, S("table"), C)
                    for p in range(P2):
                        m = tr(B7[:, pair_columns(p)], cenC[:, 2 * p:2 * p + 2, :].rearrange("t b c -> t (b c)"), ident[:, :])
                    m.then_inc(S("n2T_ps"), 1)
                if b_:
                    after(pe, S("OT_sb"), B)
                    mm(B6[:, :], w_qkv_g[:, 0, :], nT[1 - par][:, :], **one).then_inc(S("qT_ps"), 1)
                if c:
                    pe.wait_ge(S("n2T_sb"), C + 1)
                    after(pe, S("resT_sb"), A + 1 if a else 0)
                    hidden_layer(1).then_inc(S("hid_ps1"), 1)
                    pe.wait_ge(S("n2T_sb"), C + 1)
                    after(pe, S("resT_sb"), A + 1 if a else 0)
                    hidden_layer(0).then_inc(S("hid_ps0"), 1)
                    pe.wait_ge(S("gelu_chunk1"), C + 1)
                    hidden_layer(3).then_inc(S("hid_ps3"), 1)
                    pe.wait_ge(S("gelu_chunk0"), C + 1)
                    hidden_layer(2).then_inc(S("hid_ps2"), 1)
                if b_:
                    pe.wait_ge(S("E_sb"), B + 1)
                    pe.wait_ge(S("qkv_sb"), B + 1)
                    for p in range(P2):
                        m = mm(B5[:, pair_columns(p)].rearrange("p (i c) -> p i c", i=2), E[:, pair_columns(p)], qkv[:, 1, 2 * p:2 * p + 2, :], **one)
                    m.then_inc(S("ctx_ps"), 1)
                    pe.wait_ge(S("qT_sb"), B + 1)
                    pe.wait_ge(S("kvT_sb"), B + 1)
                    pe.wait_ge(S("qkv_sb"), B + 1)
                    for b in range(GB):
                        half, pc = sample(b)
                        head0 = slice(half.start, half.start + 8)
                        m = mm(B34[:, slot(b)], qT[head0, pc], kvT[head0, pc], **one)
                    m.then_inc(S("dots"), 1)
                if c:
                    for k in (2, 3):
                        pe.wait_ge(S("gelu" if k == 2 else f"gelu_chunk{k}"), C + 1)
                    for b in range(GB):
                        _, pc = sample(b)
                        for m_ in range(2):
                            m = mm(B7[:, LAT * b:LAT * b + LAT], hid[:, m_, b % 2, pc], w_2[:, m_, :], start=m_ == 0, stop=m_ == 1)
                    m.then_inc(S("mlp_ps"), 1)
                if b_:
                    pe.wait_ge(S("qs"), B + 1)
                    pe.wait_ge(S("ctx_sb"), B + 1)
                    for p in range(P2):
                        m = tr(B5[:, pair_columns(p)], qs[:, 2 * p:2 * p + 2, :].rearrange("t b c -> t (b c)"), ident[:, :])
                    m.then_inc(S("qsT_ps"), 1)
                    pe.wait_ge(S("prob"), B + 1)
                    for b in range(GB):
                        m = tr(B34[:, slot(b)], prob[:, slot(b).start // 128, :], ident[:, :])
                    m.then_inc(S("probT_ps"), 1)
                    pe.wait_ge(S("qsT_sb"), B + 1)
                    for p in range(P2):
                        m = mm(B5[:, pair_columns(p)], qsT[:, pair_columns(p)], ctx2[:, p, :], **one)
                    m.then_inc(S("global_ps"), 1)
                    pe.wait_ge(S("probT_sb"), B + 1)
                    for b in range(GB):
                        k = slot(b).start // 128
                        m = mm(B6[:, 8 * k:8 * k + 8], probT[:, slot(b)], qkv[:, 1, b, 0:8], **one)
                    m.then_inc(S("local_ps"), 1)
                if a:
                    pe.wait_ge(S("nA"), A + 1)
                    for p in range(P2):
                        m = tr(B2[:, pair_columns(p)], nA[:, 2 * p:2 * p + 2, :].rearrange("t b c -> t (b c)"), ident[:, :])
                    m.then_inc(S("nT_ps"), 1)
                if b_:
                    pe.wait_ge(S("O"), B + 1)
                    for p in range(P2):
                        m = tr(B6[:, pair_columns(p)], O[:, 2 * p:2 * p + 2, :].rearrange("t b c -> t (b c)"), ident[:, :])
                    m.then_inc(S("OT_ps"), 1)
                if c:
                    pe.wait_ge(S("z"), C + 1)
                    for p in range(P2):
                        m = tr(B7[:, pair_columns(p)], cenC[:, 2 * p:2 * p + 2, :].rearrange("t b c -> t (b c)"), ident[:, :])
                    m.then_inc(S("zT_ps"), 1)
                if b_:
                    pe.wait_ge(S("OT_sb"), B + 1)
                    for p in range(P2):
                        m = mm(B5[:, pair_columns(p)], OT[:, pair_columns(p)], w_proj[:, :], **one)
                    m.then_inc(S("proj_ps"), 1)
                if c:
                    pe.wait_ge(S("zT"), C + 1)
                    for p in range(P2):
                        m = mm(B7[:, 48 * p:48 * p + 48], zTg[:, pair_columns(p)], w_node[:, :, :].rearrange("p i c -> p (i c)"), **one)
                    m.then_inc(S("table_ps"), 1)

            run(pe, step)

        @block.scalar
        def _(act):
            copy = lambda o, i: act.activation(o, i, ACT.Copy)
            act.wait_ge(S("bias_sb"), 1)

            def gelu(k, C):
                m, i = k // 2, k % 2
                act.wait_ge(S(f"hid_ps{k}"), C + 1)
                act.activation(hid[:, m, i, :], B01[:, 512 * i:512 * i + 512], ACT.Gelu, bias=hid_b[:, m:m + 1])\
                   .then_inc(S("gelu" if k == 2 else f"gelu_chunk{k}"), 1)

            def step(s, par, a, b_, c):
                A, B, C = s, s - 1, s - 2
                if a:
                    act.wait_ge(S("resT_ps"), A + 1)
                    copy(resT[:, :], B01[:, :]).then_inc(S("resT_sb"), 1)
                if c:
                    act.wait_ge(S("cenC"), 2 * C + 1)
                    act.activation(sqC[:, :, :], cenC[:, :, :], ACT.Square).then_inc(S("sqC"), 1)
                if b_:
                    act.wait_ge(S("kvT_ps"), B + 1)
                    act.activation(kvT[:, :], B5[:, :], ACT.Identity, bias=qk_bc[:, 1:2]).then_inc(S("kvT_sb"), 1)
                    act.wait_ge(S("nkmax"), B + 1)
                    act.wait_ge(S("kvT_sb"), B + 1)
                    for p in range(P2):
                        m = act.activation(ET[:, 128 * p:128 * p + 128], kvT[:, 128 * p:128 * p + 128], ACT.Exp,
                                           bias=nkmax[:, p:p + 1], accum_out=ksum[:, p:p + 1])
                    m.then_inc(S("ET"), 1)
                if c:
                    act.wait_ge(S("n2T_ps"), C + 1)
                    copy(n2T[:, :], B7[:, :]).then_inc(S("n2T_sb"), 1)
                    gelu(1, C)
                if b_:
                    act.wait_ge(S("E_ps"), B + 1)
                    copy(E[:, :], B5[:, :]).then_inc(S("E_sb"), 1)
                if c:
                    gelu(0, C)
                if b_:
                    act.wait_ge(S("qT_ps"), B + 1)
                    act.activation(qT[:, :], B6[:, :], ACT.Identity, bias=qk_bc[:, 0:1]).then_inc(S("qT_sb"), 1)
                if a:
                    act.wait_ge(S("cenA"), A + 1)
                    act.activation(sqA[:, :, :], cenA[:, :, :], ACT.Square).then_inc(S("sqA"), 1)
                if c:
                    gelu(3, C)
                    gelu(2, C)
                if b_:
                    act.wait_ge(S("qc"), B + 1)
                    act.activation(qexp[:, :, :, :], qexp[:, :, :, :], ACT.Exp).then_inc(S("qexp"), 1)
                    act.wait_ge(S("ndmax"), B + 1)
                    for b in range(GB):
                        m = act.activation(prob[:, b, :], B34[:, 128 * b:128 * b + 128], ACT.Exp, scale=SCALE,
                                           bias=ndmax[:, 1, b:b + 1], accum_out=psm[:, 0, b:b + 1])
                    m.then_inc(S("prob"), 1)
                    act.wait_ge(S("qsT_ps"), B + 1)
                    copy(qsT[:, :], B5[:, :]).then_inc(S("qsT_sb"), 1)
                if c:
                    act.wait_ge(S("cenC"), 2 * C + 2)
                    act.activation(sqC[:, :, :], cenC[:, :, :], ACT.Square).then_inc(S("sqZ"), 1)
                if b_:
                    act.wait_ge(S("probT_ps"), B + 1)
                    copy(probT[:, :], B34[:, :]).then_inc(S("probT_sb"), 1)
                    act.wait_ge(S("OT_ps"), B + 1)
                    copy(OT[:, :], B6[:, :]).then_inc(S("OT_sb"), 1)
                if c:
                    act.wait_ge(S("zT_ps"), C + 1)
                    after(act, S("zT_out"), 16 * C)
                    copy(zTg[:, :], B7[:, :]).then_inc(S("zT"), 1)
                if a:
                    act.wait_ge(S("nT_ps"), A + 1)
                    copy(nT[par][:, :], B2[:, :]).then_inc(S("nT"), 1)

            run(act, step)

        @block.gpsimd
        def _(pool):
            tt = nc.gpsimd.tensor_tensor
            pool.memset(con[:, :, :].rearrange("p k b -> p (k b)"), -0.5).then_inc(S("pool_ready"), 1)
            pool.memset(qs[:, :, :].rearrange("p b c -> p (b c)"), 0.0).then_inc(S("pool_ready"), 1)
            pool.wait_ge(S("w_in"), 16 * 14)
            pool.wait_ge(S("pool_ready"), 2)
            half = con[:, 0, :]

            def step(s, par, a, b_, c):
                A, B, C = s, s - 1, s - 2
                if c:
                    pool.wait_ge(S("x1"), C + 1)
                    after(pool, S("hnew"), C)
                    tt(hx[:, :, :], h[par][:, :, :], x1[par][:, :, :], ALU.add).then_inc(S("hx0"), 1)
                    pool.wait_ge(S("hx0"), C + 1)
                    tt(hx[:, :, :], hx[:, :, :], over(mlp_b[:, :]), ALU.add).then_inc(S("hx"), 1)
                    pool.wait_ge(S("varC"), C + 1)
                    tt(stC[:, 4, :], stC[:, 2, :], half, ALU.pow).then_inc(S("rstdC"), 1)
                    pool.wait_ge(S("rstdC"), C + 1)
                    tt(cenC[:, :, :], cenC[:, :, :], wide(stC[:, 4, :]), ALU.mult).then_inc(S("n2"), 1)
                if b_:
                    pool.wait_ge(S("qmax"), B + 1)
                    q = qkv[:, 0, :, 8:LAT].rearrange("p b (h d) -> p b h d", d=8)
                    tt(qexp[:, :, :, :], q, qmax[:, :, :].unsqueeze(3).broadcast_to([128, GB, 7, 8]), ALU.subtract).then_inc(S("qc"), 1)
                if a:
                    pool.wait_ge(S("varA"), 2 * A + 2)
                    tt(stA[:, 5, :], stA[:, 3, :], half, ALU.pow).then_inc(S("rstdA"), 1)
                    pool.wait_ge(S("varA"), 2 * A + 2)
                    tt(stA[:, 4, :], stA[:, 2, :], half, ALU.pow).then_inc(S("rstdA1"), 1)
                    pool.wait_ge(S("rstdA1"), A + 1)
                    tt(ub[par][:, :, :], cenA[:, :, :], wide(stA[:, 4, :]), ALU.mult).then_inc(S("u"), 1)
                if b_:
                    pool.wait_ge(S("qrec"), B + 1)
                    o = qs[:, :, 8:LAT].rearrange("p b (h d) -> p b h d", d=8)
                    tt(o, qexp[:, :, :, :], qsum[:, :, :].unsqueeze(3).broadcast_to([128, GB, 7, 8]), ALU.mult).then_inc(S("qs"), 1)
                if a:
                    pool.wait_ge(S("rstdA"), A + 1)
                    after(pool, S("nT_ps"), A)
                    tt(nA[:, :, :], cenA[:, :, :], wide(stA[:, 5, :]), ALU.mult).then_inc(S("nA"), 1)
                if c:
                    pool.wait_ge(S("varZ"), C + 1)
                    tt(stC[:, 4, :], stC[:, 2, :], half, ALU.pow).then_inc(S("rstdZ"), 1)
                    pool.wait_ge(S("rstdZ"), C + 1)
                    tt(cenC[:, :, :], cenC[:, :, :], wide(stC[:, 4, :]), ALU.mult).then_inc(S("z"), 1)
                if a:
                    pool.wait_ge(S("u"), A + 1)
                    tt(ub[par][:, :, :], ub[par][:, :, :], over(proj_b[:, :]), ALU.add).then_inc(S("ub"), 1)

            run(pool, step)

        @block.vector
        def _(dve):
            v = nc.vector
            dve.wait_ge(S("w_in"), 16 * 14)
            dve.wait_ge(S("pool_ready"), 2)
            v.tensor_scalar(w_qkv_g[:, :, :], w_qkv[:, :, :], cols[:, 0:1], None, ALU.mult).then_inc(S("prep"), 1)
            v.tensor_scalar(w_1g[:, :], w_1[:, :], cols[:, 2:3], None, ALU.mult).then_inc(S("prep"), 1)
            v.tensor_copy(shift1[:, :], cols[:, 1:2].broadcast_to([128, 128])).then_inc(S("prep"), 1)
            v.memset(w_node[:, :, :].rearrange("p i c -> p (i c)"), 0.0).then_inc(S("cleared"), 1)
            dve.wait_ge(S("cleared"), 1)
            for i in range(2):
                half = slice(LAT * i, LAT * (i + 1))
                v.tensor_copy(w_node[half, i, 4:20], w_gat[half, :]).then_inc(S("prep"), 1)
            for k in range(2):
                v.tensor_tensor(att_tmp[:, k, :], w_gat[:, :], w_att[:, k, :], ALU.mult).then_inc(S("prep"), 1)
            dve.wait_ge(S("prep"), 7)
            for k in range(2):
                for i in range(2):
                    half = slice(LAT * i, LAT * (i + 1))
                    v.tensor_reduce(w_node[half, i, 20 * k:20 * k + 4], att_tmp[half, k, :].rearrange("p (h e) -> p h e", e=4), AX.X, ALU.add).then_inc(S("prep"), 1)
            dve.wait_ge(S("prep"), 11)
            v.tensor_copy(hid_b[:, :], cols[:, 4:6]).then_inc(S("w_ready"), 1)
            dve.wait_ge(S("w_ready"), 1)
            dve.wait_ge(S("bias_ps"), 1)
            v.tensor_copy(qkv_b[:, :, :].rearrange("p k c -> p (k c)"), B7[:, 0:256]).then_inc(S("prep"), 1)
            v.tensor_copy(qk_bc[:, :], B7[:, 256:258]).then_inc(S("prep"), 1)
            v.tensor_tensor(hid_b[:, :], B6[:, 0:2], hid_b[:, :], ALU.add).then_inc(S("prep"), 1)
            dve.wait_ge(S("prep"), 14)
            v.tensor_copy(stA[:, 0, :], con[:, 0, :]).then_inc(S("bias_sb"), 1)

            def center(name, g, src, st, cen, done):
                v.tensor_reduce(st[:, 0, :], src, AX.X, ALU.add).then_inc(S(f"{name}_sum"), 1)
                dve.wait_ge(S(f"{name}_sum"), g + 1)
                v.tensor_scalar(st[:, 0, :], st[:, 0, :], 1.0 / LAT, None, ALU.mult).then_inc(S(f"{name}_mean"), 1)
                dve.wait_ge(S(f"{name}_mean"), g + 1)
                v.tensor_tensor(cen, src, wide(st[:, 0, :]), ALU.subtract).then_inc(done, 1)

            def variance(name, g, sq, st, maps):
                v.tensor_reduce(st[:, 1, :], sq[:, :, :], AX.X, ALU.add).then_inc(S(f"ssq{name}"), 1)
                dve.wait_ge(S(f"ssq{name}"), g + 1)
                for k, (scale, shift) in enumerate(maps):
                    v.tensor_scalar(st[:, 2 + k, :], st[:, 1, :], scale, shift, ALU.mult, ALU.add).then_inc(S(f"var{name}"), 1)

            def step(s, par, a, b_, c):
                A, B, C = s, s - 1, s - 2
                if c:
                    dve.wait_ge(S("x1"), C + 1)
                    after(dve, S("zT_ps"), C)
                    center("x1c", C, x1[par][:, :, :], stC, cenC[:, :, :], S("cenC"))
                    dve.wait_ge(S("sqC"), C + 1)
                    variance("C", C, sqC, stC, ((1.0 / LAT, EPS),))
                if b_:
                    dve.wait_ge(S("kvT_sb"), B + 1)
                    v.tensor_reduce(nkmax[:, :], kvT[:, :].rearrange("p (q t) -> p q t", t=128), AX.X, ALU.max, negate=True).then_inc(S("nkmax"), 1)
                    dve.wait_ge(S("ET"), B + 1)
                    v.reciprocal(rks[:, :], ksum[:, :]).then_inc(S("rks"), 1)
                    dve.wait_ge(S("qkv_ps"), B + 1)
                    after(dve, S("local_ps"), B)
                    v.tensor_tensor(qkv[:, :, :, :].rearrange("p k (q i) c -> p k q (i c)", i=2), B34[:, :].rearrange("p (k q c) -> p k q c", k=2, c=128),
                                    qkv_b[:, :, :].unsqueeze(2).broadcast_to([128, 2, P2, 128]), ALU.add).then_inc(S("qkv_sb"), 1)
                if a:
                    dve.wait_ge(S("h_ps"), A + 1)
                    after(dve, S("hx0"), C + 1)
                    v.tensor_tensor(h[par][:, :, :], group(B2[:, :]), over(out_b[:, :]), ALU.add).then_inc(S("h"), 1)
                if b_:
                    dve.wait_ge(S("qkv_sb"), B + 1)
                    q = qkv[:, 0, :, 8:LAT].rearrange("p b (h d) -> p b h d", d=8)
                    v.tensor_reduce(qmax[:, :, :], q, AX.X, ALU.max).then_inc(S("qmax"), 1)
                if a:
                    dve.wait_ge(S("h"), A + 1)
                    after(dve, S("u"), A)
                    after(dve, S("nA"), A)
                    center("hc", A, h[par][:, :, :], stA, cenA[:, :, :], S("cenA"))
                    dve.wait_ge(S("sqA"), A + 1)
                    variance("A", A, sqA, stA, ((1.0 / LAT, EPS), ((1.0 + EPS) / LAT, EPS * EPS)))
                if b_:
                    dve.wait_ge(S("rks"), B + 1)
                    dve.wait_ge(S("ctx_ps"), B + 1)
                    for p in range(P2):
                        m = v.scalar_tensor_tensor(ctx2[:, p, :], B5[:, 128 * p:128 * p + 128], rks[:, p:p + 1], headmask[:, :], ALU.mult, ALU.mult)
                    m.then_inc(S("ctx_sb"), 1)
                    dve.wait_ge(S("dots"), B + 1)
                    v.tensor_reduce(ndmax[:, 0, :], B34[:, :].rearrange("p (b k) -> p b k", k=128), AX.X, ALU.max, negate=True).then_inc(S("dmax"), 1)
                    dve.wait_ge(S("dmax"), B + 1)
                    v.tensor_scalar(ndmax[:, 1, :], ndmax[:, 0, :], SCALE, None, ALU.mult).then_inc(S("ndmax"), 1)
                    dve.wait_ge(S("qexp"), B + 1)
                    v.tensor_reduce(qsum[:, :, :], qexp[:, :, :, :], AX.X, ALU.add).then_inc(S("qsum"), 1)
                    dve.wait_ge(S("qsum"), B + 1)
                    v.reciprocal(qsum[:, :, :], qsum[:, :, :]).then_inc(S("qrec0"), 1)
                    dve.wait_ge(S("qrec0"), B + 1)
                    v.tensor_scalar(qsum[:, :, :], qsum[:, :, :], SCALE, None, ALU.mult).then_inc(S("qrec"), 1)
                if c:
                    dve.wait_ge(S("mlp_ps"), C + 1)
                    dve.wait_ge(S("hx"), C + 1)
                    after(dve, S(f"h_out{par}"), 8 * (C - par))
                    v.tensor_tensor(hnew[par][:, :, :], group(B7[:, :]), hx[:, :, :], ALU.add).then_inc(S("hnew"), 1)
                    dve.wait_ge(S("hnew"), C + 1)
                    center("zc", C, hnew[par][:, :, :], stC, cenC[:, :, :], S("cenC"))
                    dve.wait_ge(S("sqZ"), C + 1)
                    variance("Z", C, sqC, stC, ((1.0 / LAT, EPS),))
                if b_:
                    dve.wait_ge(S("prob"), B + 1)
                    v.reciprocal(psm[:, 1, :], psm[:, 0, :]).then_inc(S("rprob"), 1)
                    dve.wait_ge(S("rprob"), B + 1)
                    dve.wait_ge(S("global_ps"), B + 1)
                    after(dve, S("OT_ps"), B)
                    v.tensor_copy(O[:, :, 8:LAT], group(B5[:, :])[:, :, 8:LAT]).then_inc(S("O_global"), 1)
                    dve.wait_ge(S("local_ps"), B + 1)
                    v.tensor_tensor(O[:, :, 0:8].rearrange("p (q i) c -> p i q c", i=2), B6[:, 0:8 * GB].rearrange("p (i q c) -> p i q c", i=2, c=8),
                                    psm[:, 1, :].rearrange("p (i q) -> p i q", i=2).unsqueeze(3).broadcast_to([128, 2, P2, 8]), ALU.mult).then_inc(S("O"), 1)
                    dve.wait_ge(S("proj_ps"), B + 1)
                    dve.wait_ge(S("ub"), B + 1)
                    after(dve, S("hx"), B - 1)
                    v.tensor_tensor(x1[1 - par][:, :, :], group(B5[:, :]), ub[1 - par][:, :, :], ALU.add).then_inc(S("x1"), 1)
                if c:
                    dve.wait_ge(S("table_ps"), C + 1)
                    after(dve, S(f"table_out{par}"), 16 * (C - par))
                    v.tensor_copy(tabg[par][:, :, :], B7[:, 0:24 * GB].rearrange("p (b c) -> p b c", c=24)).then_inc(S("table"), 1)

            run(dve, step)
    n.release()


CW = 64
CHUNKS = EP // CW
RING = 8
LATE = 6
EARLY = 3
CH = 20
EXPERTS, HEADS = 4, 4


def graph(nc, d, keys, cur, end_i, count):
    ctx = ExitStack()
    with ctx:
        n = Names(nc, ctx, "graph")
        S = n.sem
        PC = GB // 2 * 128
        SUB = 16
        ident = n.sb("ident3", [128, 128])
        upto = n.sb("upto", [128, 128])
        ones = n.sb("ones", [128, 128])
        ramp = n.sb("ramp", [128, 128])
        ramps = n.sb("ramps", [128, 128, SUB], BF16)
        rowpos = n.sb("first_position", [128, 1])
        dsti = keys[cur][:, :].bitcast(I32)
        srci = keys[1 - cur][:, :].bitcast(I32)
        dlo = n.sb("dst_frame", [128, EP], BF16)
        dhi = n.sb("dst_sample", [128, EP], BF16)
        keep = n.sb("same_segment", [128, EP])
        idx = [n.sb(f"gather_index{i}", [128, CW], U32) for i in range(2)]
        stage = [n.sb(f"gathered{i}", [128, CW, CH]) for i in range(2)]
        ring = n.sb("ring", [128, RING * CW, CH])
        hot = [n.sb(f"one_hot{i}", [128, 2, 128, SUB], BF16) for i in range(2)]
        zero_b = n.sb("zero_bf16", [128, 128], BF16)
        zg = [n.sb(f"zT_in{i}", [128, PC]) for i in range(2)]
        w1e = n.sb("w_expert1", [128, EXPERTS, 128])
        w2e = n.sb("w_expert2", [128, EXPERTS, LAT])
        b1e = n.sb("b_expert1", [128, EXPERTS])
        b2e = n.sb("b_expert2", [128, EXPERTS * LAT])
        hid = n.sb("expert_hidden", [128, 2 * EXPERTS, PC])
        ye = [n.sb(f"expert_out{i}", [128, GB, EXPERTS * LAT]) for i in range(2)]
        cnt = n.sb("count_copy", [128, 128])
        tot = n.sb("sample_total", [128, 128])
        scan_tot = n.sb("sample_total_upto", [128, 128])
        endf = n.sb("end_float", [128, 128])
        startf = n.sb("start_float", [128, 128])
        none = n.sb("no_edges", [128, 128])
        start_i = n.sb("start_index", [128, 128], U32)
        dst_first = n.sb("first_destination", [128, 1], U32)
        nd = n.sb("node_dst_scores", [128, 128, HEADS])
        first4 = n.sb("first_dst_scores", [128, HEADS])
        adc = [n.sb(f"dst_scores_at_starts{i}", [128, CW, HEADS]) for i in range(2)]
        adb = [n.sb(f"dst_scores{i}", [128, HEADS, CW]) for i in range(2)]
        pre = n.sb("score_sum", [128, HEADS, CW])
        e = n.sb("score", [128, HEADS, CW])
        pen = n.sb("reset", [128, CW])
        M = [n.sb(f"running_max{i}", [128, HEADS, CW + 1]) for i in range(2)]
        X = n.sb("exponents", [128, 2 * HEADS, CW])
        RW = n.sb("rescale_and_weight", [128, 2 * HEADS, CW])
        wv = n.sb("weighted", [128, 16, CW])
        st = [n.sb(f"state{i}", [128, CW, CH + HEADS]) for i in range(2)]
        eq = hid[:, 5:7, :].rearrange("p a b -> p (a b)").bitcast(BF16)
        first_len = n.sb("first_segment_length", [128, 1])
        e1f = n.sb("first_end_float", [128, 1])
        e1 = n.sb("first_end", [128, 1], U32)
        jt = n.sb("join_in", [128, 4, CH])
        jT = hid[0:CH, 0, :].rearrange("c (k p) -> c k p", p=128)
        js = hid[0:CH, 1:3, :].rearrange("c a (k p) -> c (a k) p", p=128)
        jm = hid[0:CH, 3, 0:129]
        jx = hid[0:CH, 4, 0:129]
        primed = n.sb("primed", [128, 16])
        token = n.sb("pool_token", [128, 2])
        jc = n.sb("carry", [128, 2, CH])
        row = n.sb("end_row", [128, CH + HEADS])
        jr = n.sb("join_row", [128, 6, CH])
        rowo = n.sb("end_row_joined", [128, CH + HEADS])

        hist = n.ps("histogram", [128, 512])
        hps = [n.ps(f"expert_hidden_ps{i}", [128, PC]) for i in range(2)]
        yps = n.ps("expert_out_ps", [128, GB, EXPERTS * LAT])
        sps = n.ps("small_ps", [128, 512])
        block = ctx.enter_context(nc.Block())
        OOB = 2 * EDGES

        AHEAD = [("adb", 2), ("max_copied", 2), ("RW", 1), ("sums", 1), ("y_ps", 1)]
        AHEAD += [(f"{name}{par}", 16) for name in ("ring", "stored", "y_out") for par in range(2)]

        @block.sync
        def _(sp):
            sp.wait_ge(S("srci"), 1)

            def index(c, par):
                sp.dma_start(idx[par][:, :].bitcast(I32), srci[:, bass.ds(c * CW, CW)]).then_inc(S(f"idx_in{par}"), 16)

            index(0, 0)
            index(1, 1)
            for t, name in ((ident, "c_ident"), (upto, "c_upto"), (ones, "c_ones"), (ramp, "c_ramp"), (rowpos, "c_rowpos"), (b1e, "b_expert1")):
                sp.dma_start(t[:, :], d[name]).then_inc(S("consts"), 16)
            sp.dma_start(w1e[:, :, :], d["w_expert1"]).then_inc(S("consts"), 16)
            sp.dma_start(w2e[:, :, :], d["w_expert2"]).then_inc(S("consts"), 16)
            sp.dma_start(b2e[:, :], d["b_expert2"].partition_broadcast(128)).then_inc(S("consts"), 16)
            sp.dma_start(nd[:, :, :], d["node_dst"].rearrange("(b t) c -> t b c", t=128)).then_inc(S("nd_in"), 16)

            def serve(c, slot, par, more=True):
                sp.wait_ge(S(f"gathered{par}"), (c - par) * (8 * CW) + 16 * CW)
                if more:
                    index(c + 2, par)
                sp.wait_ge(S("chunk_used"), c - RING + 1)
                sp.dma_start(ring[:, bass.ds(slot * CW, CW), :], stage[par][:, :, :]).then_inc(S(f"ring{par}"), 16)

            def serve_first(i):
                for par in range(2):
                    c = 2 * i + par
                    sp.wait_ge(S(f"gathered{par}"), (c - par) * (8 * CW) + 16 * CW)
                    sp.dma_start(ring[:, bass.ds(c * CW, CW), :], stage[par][:, :, :]).then_inc(S(f"ring{par}"), 16)
                    index(c + 2, par)

            with sp.Fori(0, EARLY) as i:
                serve_first(i)
            sp.wait_ge(S("scattered"), 16 * 128)
            sp.wait_ge(S("first4"), 16)
            sp.dma_start(d["dst_at_start"].rearrange("(p f) c -> p f c", p=128)[:, 0, :], first4[:, :]).then_inc(S("starts_set"), 16)
            with sp.Fori(EARLY, RING // 2) as i:
                serve_first(i)
            with sp.Fori(1, CHUNKS // RING - 1) as o:
                with sp.Fori(0, RING // 2) as i:
                    for par in range(2):
                        serve(RING * o + 2 * i + par, 2 * i + par, par)
            with sp.Fori(0, RING // 2 - 1) as i:
                for par in range(2):
                    serve(2 * i + (CHUNKS - RING + par), 2 * i + par, par)
            for par in range(2):
                serve(CHUNKS - 2 + par, RING - 2 + par, par, more=False)

        @block.gpsimd
        def _(pool):
            off = bass.IndirectOffsetOnAxis

            def gather(c, par):
                pool.wait_ge(S(f"idx_in{par}"), 8 * (c - par) + 16)
                pool.wait_ge(S(f"ring{par}"), 8 * (c - par) + 16)
                pool.wait_ge(S("gather_go"), c + 1)
                nc.gpsimd.tensor_tensor(token[:, 0:1], token[:, 1:2], token[:, 1:2], ALU.add).then_inc(S("gather_go"), 1)
                for f in range(CW):
                    pool.indirect_dma_start(stage[par][:, f, :], None, d["node_src"], off(ap=idx[par][:, f:f + 1], axis=0))\
                        .then_inc(S(f"gathered{par}"), 16)

            pool.memset(token[:, :], 0.0).then_inc(S("gather_go"), 1)
            with pool.Fori(0, EARLY) as i:
                for par in range(2):
                    gather(2 * i + par, par)
            pool.wait_ge(S("indices"), 2)
            pool.wait_ge(S("nd_in"), 16)
            pool.wait_ge(S("starts_cleared"), 64)
            for b in range(B):
                pool.indirect_dma_start(d["dst_at_start"], off(ap=start_i[:, b:b + 1], axis=0), nd[:, b, :], None,
                                        bounds_check=EDGES - 1, oob_is_err=False).then_inc(S("scattered"), 16)
            pool.wait_ge(S("dst_first"), 1)
            pool.indirect_dma_start(first4[:, :], None, d["node_dst"], off(ap=dst_first[:, 0:1], axis=0)).then_inc(S("first4"), 16)
            with pool.Fori(EARLY, CHUNKS // 2) as i:
                for par in range(2):
                    gather(2 * i + par, par)
            for par in range(2):
                pool.wait_ge(S(f"stored{par}"), 16 * (CHUNKS // 2) + 16)
            pool.wait_ge(S("e1"), 1)
            pool.indirect_dma_start(row[:, :], None, d["edge_state"], off(ap=e1[:, 0:1], axis=0)).then_inc(S("row_in"), 16)
            pool.wait_ge(S("row_joined"), 2)
            pool.indirect_dma_start(d["edge_state"], off(ap=e1[:, 0:1], axis=0), rowo[:, :], None).then_inc(S("row_out"), 16)
            pool.wait_ge(S("row_out"), 16)

        @block.tensor
        def _(pe):
            mm = nc.tensor.matmul
            one = dict(start=True, stop=True)
            pe.wait_ge(S("consts"), 16 * 9)
            pe.wait_ge(S("zero"), 2)
            mm(hist[:, 0:128], zero_b[:, :], zero_b[:, :], start=True, stop=False).then_inc(S("hist_done"), 2)

            with pe.Fori(0, EP // SUB // 2) as i:
                for par in range(2):
                    pe.wait_ge(S("hot"), 2 * i + (par + 1))
                    for j in range(SUB):
                        m = mm(hist[:, 0:128], hot[par][:, 0, :, j], hot[par][:, 1, :, j], start=False, stop=False)
                    m.then_inc(S("hist_done"), 1)
            mm(hist[:, 0:128], zero_b[:, :], zero_b[:, :], start=False, stop=True).then_inc(S("hist_full"), 1)
            pe.wait_ge(S("count_sb"), 1)
            mm(sps[:, 0:128], upto[:, :], cnt[:, :], **one)
            mm(sps[:, 128:256], ones[:, :], cnt[:, :], **one).then_inc(S("upto_ps"), 1)

            def experts(g, par):
                pe.wait_ge(S(f"z_in{par}"), 8 * (g - par) + 16)
                for k in range(2 * EXPERTS):
                    ex, i = k // 2, k % 2
                    half = slice(LAT * i, LAT * (i + 1))
                    pe.wait_ge(S(f"hid_free{i}"), EXPERTS * g + ex + 1)
                    mm(hps[i][:, :], w1e[half, ex, :], zg[par][half, :], **one).then_inc(S(f"hid_ps{i}"), 1)
                pe.wait_ge(S("gelu_done"), g + 1)
                pe.wait_ge(S("y_free"), g + 1)
                for b in range(GB):
                    for ex in range(EXPERTS):
                        m = mm(yps[:, b, LAT * ex:LAT * ex + LAT], hid[:, 2 * ex + b % 2, 128 * (b // 2):128 * (b // 2) + 128], w2e[:, ex, :], **one)
                m.then_inc(S("y_ps"), 1)

            with pe.Fori(0, G // 2) as i:
                for par in range(2):
                    experts(2 * i + par, par)
            pe.wait_ge(S("join_in"), 4)
            for k in range(4):
                m = nc.tensor.transpose(sps[0:CH, 128 * k:128 * k + 128], jt[:, k, :], ident[:, :])
            m.then_inc(S("join_ps"), 1)
            pe.wait_ge(S("carry_rows"), 2)
            for k, t in ((0, jm), (1, jx)):
                m = nc.tensor.transpose(hps[0][:, CH * k:CH * k + CH], t[:, 0:128], ident[0:CH, 0:CH])
            m.then_inc(S("carry_ps"), 1)

        @block.scalar
        def _(act):
            def load_z(g, par):
                act.dma_start(zg[par][:, :], d["zT"][:, bass.ds(g * PC, PC)]).then_inc(S(f"z_in{par}"), 16)

            def store_y(g, par):
                act.dma_start(d["expert_out"][:, bass.ds(g * GB, GB), :], ye[par][:, :, :]).then_inc(S(f"y_out{par}"), 16)

            load_z(0, 0)
            load_z(1, 1)
            act.wait_ge(S("zero"), 2)
            for k in range(4):
                w = EDGES * HEADS // 128 // 4
                act.dma_start(d["dst_at_start"].rearrange("(p f) c -> p (f c)", p=128)[:, k * w:(k + 1) * w], ye[0][:, :, :].rearrange("p b c -> p (b c)"))\
                   .then_inc(S("starts_cleared"), 16)
            act.wait_ge(S("starts_cleared"), 64)
            act.wait_ge(S("consts"), 16 * 9)
            act.activation(b1e[:, :], b1e[:, :], ACT.Copy).then_inc(S("hid_free0"), 1)
            act.wait_ge(S("hid_free0"), 1)
            act.activation(b1e[:, :], b1e[:, :], ACT.Copy).then_inc(S("hid_free1"), 1)
            act.wait_ge(S("hid_free1"), 1)

            def experts(g, par, more=True):
                for k in range(2 * EXPERTS):
                    ex, i = k // 2, k % 2
                    act.wait_ge(S(f"hid_ps{i}"), EXPERTS * g + ex + 1)
                    if k == 0:
                        act.wait_ge(S("y_ps"), g + 1)
                    m = act.activation(hid[:, k, :], hps[i][:, :], ACT.Gelu, bias=b1e[:, ex:ex + 1])
                    m.then_inc(S(f"hid_free{i}"), 1)
                act.wait_ge(S("hid_free1"), EXPERTS * g + EXPERTS + 1)
                act.activation(b1e[:, :], b1e[:, :], ACT.Copy).then_inc(S("gelu_done"), 1)
                if more:
                    load_z(g + 2, par)
                act.wait_ge(S("y_sb"), g + 1)
                store_y(g, par)

            with act.Fori(0, LATE) as i:
                for par in range(2):
                    experts(2 * i + par, par)
            act.wait_ge(S("starts_set"), 16)

            def chunk(c, par):
                act.wait_ge(S("adb"), c + 1)
                act.dma_start(adc[par][:, :, :], d["dst_at_start"].rearrange("(p f) c -> p f c", p=128)[:, bass.ds(c * CW, CW), :]).then_inc(S(f"adc_in{par}"), 16)
                act.wait_ge(S("X"), c + 1)
                act.activation(RW[:, :, :], X[:, :, :], ACT.Exp).then_inc(S("RW"), 1)
                act.wait_ge(S(f"stored{par}"), 8 * (c - par) + 16)
                act.activation(st[par][:, :, CH:].rearrange("p f h -> p h f"), M[par][:, :, 1:], ACT.Copy).then_inc(S("max_copied"), 1)
                act.wait_ge(S("sums"), c + 2)
                act.wait_ge(S("max_copied"), c + 3)
                act.dma_start(d["edge_state"].rearrange("(p f) c -> p f c", p=128)[:, bass.ds(c * CW, CW), :], st[par][:, :, :]).then_inc(S(f"stored{par}"), 16)

            with act.Fori(0, RING // 2) as i:
                for par in range(2):
                    chunk(2 * i + par, par)
            for g in range(2 * LATE, G):
                experts(g, g % 2, more=g + 2 < G)
            with act.Fori(RING // 2, CHUNKS // 2) as i:
                for par in range(2):
                    chunk(2 * i + par, par)
            for par in range(2):
                act.wait_ge(S(f"y_out{par}"), 16 * (G // 2) + 16)
            act.wait_ge(S("join_x"), 1)
            act.activation(js[:, 4:6, :], js[:, 2:4, :], ACT.Exp).then_inc(S("join_e"), 1)
            act.wait_ge(S("row_x"), 2)
            act.activation(jr[:, 3:5, :], jr[:, 1:3, :], ACT.Exp).then_inc(S("row_e"), 1)

        @block.vector
        def _(dve):
            v = nc.vector
            v.tensor_scalar(srci, dsti, NODES - 1, None, ALU.bitwise_and).then_inc(S("srci"), 1)
            for k, (name, ahead) in enumerate(AHEAD):
                v.memset(primed[:, k:k + 1], 0.0).then_inc(S(name), ahead)
            v.memset(ye[0][:, :, :].rearrange("p b c -> p (b c)"), 0.0).then_inc(S("zero"), 1)
            v.memset(zero_b[:, :], 0.0).then_inc(S("zero"), 1)
            dve.wait_ge(S("srci"), 1)
            v.tensor_scalar(dsti, dsti, NODE_BITS, NODES - 1, ALU.logical_shift_right, ALU.bitwise_and).then_inc(S("dsti"), 1)
            dve.wait_ge(S("dsti"), 1)
            whole = keep[:, :].bitcast(I32)
            v.tensor_scalar(whole, dsti, T - 1, None, ALU.bitwise_and).then_inc(S("split"), 1)
            dve.wait_ge(S("split"), 1)
            v.tensor_copy(dlo[:, :], whole).then_inc(S("split"), 1)
            dve.wait_ge(S("split"), 2)
            v.tensor_scalar(whole, dsti, T.bit_length() - 1, None, ALU.logical_shift_right).then_inc(S("split"), 1)
            dve.wait_ge(S("split"), 3)
            v.tensor_copy(dhi[:, :], whole).then_inc(S("split"), 1)
            dve.wait_ge(S("split"), 4)
            v.tensor_copy(dst_first[:, :].bitcast(I32), dsti[:, 0:1]).then_inc(S("dst_first"), 1)
            v.memset(keep[:, 0:1], 0.0).then_inc(S("keep0"), 1)
            v.tensor_tensor(keep[:, 1:EP], dsti[:, 1:EP], dsti[:, 0:EP - 1], ALU.is_equal).then_inc(S("keep0"), 1)
            dve.wait_ge(S("consts"), 16 * 9)
            v.tensor_copy(ramps[:, :, :], ramp[:, :].unsqueeze(2).broadcast_to([128, 128, SUB])).then_inc(S("split"), 1)
            dve.wait_ge(S("split"), 5)
            for par in range(2):
                for t in (M[par][:, :, :], adb[par][:, :, :], st[par][:, :, :]):
                    v.memset(t.rearrange("p a b -> p (a b)"), 0.0).then_inc(S("cleared"), 1)
            dve.wait_ge(S("cleared"), 6)
            v.tensor_copy(e1f[:, :], rowpos[:, :]).then_inc(S("y_free"), 1)
            with dve.Fori(0, EP // SUB // 2) as i:
                for par in range(2):
                    dve.wait_ge(S("hist_done"), 2 * i + (par + 1))
                    cols = bass.ds(i * (2 * SUB) + par * SUB, SUB)
                    for k, value in enumerate((dlo, dhi)):
                        m = v.tensor_tensor(hot[par][:, k, :, :], ramps[:, :, :], value[:, cols].unsqueeze(1).broadcast_to([128, 128, SUB]), ALU.is_equal)
                    m.then_inc(S("hot"), 1)

            dve.wait_ge(S("hist_full"), 1)
            v.tensor_copy(cnt[:, :], hist[:, 0:128]).then_inc(S("count_sb"), 1)
            dve.wait_ge(S("count_sb"), 1)
            v.tensor_copy(count[:, :], cnt[:, :]).then_inc(S("f"), 1)
            v.tensor_scalar(none[:, :], cnt[:, :], 0.0, float(OOB), ALU.is_equal, ALU.mult).then_inc(S("f"), 1)
            dve.wait_ge(S("upto_ps"), 1)
            v.tensor_copy(tot[:, :], sps[:, 128:256]).then_inc(S("f"), 1)
            dve.wait_ge(S("f"), 3)
            v.tensor_tensor_scan(scan_tot[:, :], ones[:, :], tot[:, :], 0.0, ALU.mult, ALU.add).then_inc(S("f"), 1)
            dve.wait_ge(S("f"), 4)
            v.tensor_tensor(tot[:, :], scan_tot[:, :], tot[:, :], ALU.subtract).then_inc(S("f"), 1)
            dve.wait_ge(S("f"), 5)
            v.tensor_tensor(endf[:, :], sps[:, 0:128], tot[:, :], ALU.add).then_inc(S("f"), 1)
            dve.wait_ge(S("f"), 6)
            v.tensor_tensor(startf[:, :], endf[:, :], cnt[:, :], ALU.subtract).then_inc(S("f"), 1)
            dve.wait_ge(S("f"), 7)
            v.tensor_tensor(start_i[:, :], startf[:, :], none[:, :], ALU.add).then_inc(S("indices"), 1)
            v.tensor_scalar(end_i[:, :], endf[:, :], -1.0, 0.0, ALU.add, ALU.max).then_inc(S("indices"), 1)

            def experts(g, par):
                dve.wait_ge(S("y_ps"), g + 2)
                dve.wait_ge(S(f"y_out{par}"), 8 * (g - par) + 16)
                v.tensor_tensor(ye[par][:, :, :], yps[:, :, :], b2e[:, :].unsqueeze(1).broadcast_to([128, GB, EXPERTS * LAT]), ALU.add).then_inc(S("y_sb"), 1)
                dve.wait_ge(S("y_sb"), g + 1)
                v.tensor_copy(e1f[:, :], rowpos[:, :]).then_inc(S("y_free"), 1)

            dve.wait_ge(S("starts_cleared"), 64)
            with dve.Fori(0, LATE) as i:
                for par in range(2):
                    experts(2 * i + par, par)

            def chunk(c, slot, par):
                cols = bass.ds(c * CW, CW)
                g = ring[:, bass.ds(slot * CW, CW), :]
                dve.wait_ge(S(f"adc_in{par}"), 8 * (c - par) + 16)
                dve.wait_ge(S("adb"), c + 2)
                for h in range(HEADS):
                    m = v.tensor_tensor_scan(adb[par][:, h, :], keep[:, cols], adc[par][:, :, h], adb[1 - par][:, h, CW - 1:CW], ALU.mult, ALU.add)
                m.then_inc(S("adb"), 1)
                v.tensor_scalar(pen[:, :], keep[:, cols], -NEG, NEG, ALU.mult, ALU.add).then_inc(S("pen"), 1)
                dve.wait_ge(S(f"ring{par}"), 8 * (c - par) + 32)
                dve.wait_ge(S("adb"), c + 3)
                v.tensor_tensor(pre[:, :, :], g[:, :, 0:HEADS].rearrange("p f h -> p h f"), adb[par][:, :, :], ALU.add).then_inc(S("pre"), 1)
                dve.wait_ge(S("pre"), c + 1)
                v.scalar_tensor_tensor(e[:, :, :], pre[:, :, :], 0.2, pre[:, :, :], ALU.mult, ALU.max).then_inc(S("e"), 1)
                dve.wait_ge(S("max_copied"), c + 1)
                v.tensor_copy(M[par][:, :, 0:1], M[1 - par][:, :, CW:CW + 1]).then_inc(S("M0"), 1)
                dve.wait_ge(S("e"), c + 1)
                dve.wait_ge(S("M0"), c + 1)
                dve.wait_ge(S("pen"), c + 1)
                for h in range(HEADS):
                    m = v.tensor_tensor_scan(M[par][:, h, 1:], pen[:, :], e[:, h, :], M[par][:, h, 0:1], ALU.add, ALU.max)
                m.then_inc(S("M"), 1)
                dve.wait_ge(S("M"), c + 1)
                dve.wait_ge(S("RW"), c + 1)
                v.tensor_tensor(X[:, 0:HEADS, :], M[par][:, :, 0:CW], M[par][:, :, 1:], ALU.subtract).then_inc(S("X0"), 1)
                dve.wait_ge(S("X0"), c + 1)
                v.tensor_tensor(X[:, 0:HEADS, :], X[:, 0:HEADS, :], pen[:, :].unsqueeze(1).broadcast_to([128, HEADS, CW]), ALU.add).then_inc(S("X1"), 1)
                v.tensor_tensor(X[:, HEADS:, :], e[:, :, :], M[par][:, :, 1:], ALU.subtract).then_inc(S("X2"), 1)
                dve.wait_ge(S("X1"), c + 1)
                dve.wait_ge(S("X2"), c + 1)
                v.tensor_copy(first_len[:, :], rowpos[:, :]).then_inc(S("X"), 1)
                dve.wait_ge(S("RW"), c + 2)
                for h in range(HEADS):
                    m = v.tensor_tensor(wv[:, 4 * h:4 * h + 4, :], g[:, :, 4 + 4 * h:8 + 4 * h].rearrange("p f e -> p e f"),
                                        RW[:, HEADS + h, :].unsqueeze(1).broadcast_to([128, 4, CW]), ALU.mult)
                m.then_inc(S("wv"), 1)
                dve.wait_ge(S("wv"), c + 1)
                v.tensor_copy(first_len[:, :], rowpos[:, :]).then_inc(S("chunk_used"), 1)
                dve.wait_ge(S(f"stored{par}"), 8 * (c - par) + 16)
                dve.wait_ge(S("sums"), c + 1)
                for k in range(CH):
                    h = k // 4 if k < 16 else k - 16
                    src = wv[:, k, :] if k < 16 else RW[:, HEADS + h, :]
                    m = v.tensor_tensor_scan(st[par][:, :, k], RW[:, h, :], src, st[1 - par][:, CW - 1, k:k + 1], ALU.mult, ALU.add)
                m.then_inc(S("sums"), 1)

            with dve.Fori(0, RING // 2) as i:
                for par in range(2):
                    chunk(2 * i + par, 2 * i + par, par)
            with dve.Fori(LATE, G // 2) as i:
                for par in range(2):
                    experts(2 * i + par, par)
            with dve.Fori(1, CHUNKS // RING) as o:
                with dve.Fori(0, RING // 2) as i:
                    for par in range(2):
                        chunk(RING * o + 2 * i + par, 2 * i + par, par)

            dve.wait_ge(S("sums"), CHUNKS + 1)
            dve.wait_ge(S("max_copied"), CHUNKS + 2)
            last = st[1][:, CW - 1, :]
            dstf = keys[cur]
            v.tensor_copy(dstf[:, :], dsti).then_inc(S("u"), 1)
            dve.wait_ge(S("u"), 1)
            v.tensor_scalar(eq[:, :], dstf[:, :], dstf[:, 0:1], None, ALU.is_equal, ALU.add, accum_out=first_len[:, :]).then_inc(S("u"), 1)
            dve.wait_ge(S("u"), 2)
            v.tensor_scalar(e1f[:, :], first_len[:, :], rowpos[:, :], -1.0, ALU.add, ALU.add).then_inc(S("u"), 1)
            dve.wait_ge(S("u"), 3)
            v.tensor_copy(e1[:, :], e1f[:, :]).then_inc(S("e1"), 1)
            v.tensor_copy(jt[:, 0, :], last[:, 0:CH]).then_inc(S("join_in"), 1)
            v.tensor_copy(jt[:, 1, 0:16].rearrange("p (h e) -> p h e", e=4), last[:, CH:].unsqueeze(2).broadcast_to([128, HEADS, 4])).then_inc(S("join_m"), 1)
            v.tensor_copy(jt[:, 1, 16:CH], last[:, CH:]).then_inc(S("join_in"), 1)
            v.tensor_copy(jt[:, 2, :], dstf[:, 0:1].broadcast_to([128, CH])).then_inc(S("join_in"), 1)
            v.tensor_copy(jt[:, 3, :], dstf[:, EP - 1:EP].broadcast_to([128, CH])).then_inc(S("join_in"), 1)
            dve.wait_ge(S("join_ps"), 1)
            v.tensor_copy(jT[:, :, :].rearrange("c k p -> c (k p)"), sps[0:CH, :]).then_inc(S("u"), 1)
            v.memset(jm[:, 0:1], NEG).then_inc(S("u"), 1)
            v.memset(jx[:, 0:1], 0.0).then_inc(S("u"), 1)
            v.memset(js[:, 0, 0:1], 0.0).then_inc(S("u"), 1)
            dve.wait_ge(S("u"), 7)
            Ss, Mm, first, lastd = (jT[:, k, :] for k in range(4))
            v.tensor_tensor(js[:, 0, 1:128], first[:, 1:128], lastd[:, 0:127], ALU.is_equal).then_inc(S("u"), 1)
            v.tensor_tensor(js[:, 1, :], first, lastd, ALU.is_equal).then_inc(S("u"), 1)
            dve.wait_ge(S("u"), 9)
            v.tensor_tensor(js[:, 1, :], js[:, 1, :], js[:, 0, :], ALU.mult).then_inc(S("u"), 1)
            dve.wait_ge(S("u"), 10)
            v.tensor_scalar(js[:, 1, :], js[:, 1, :], -NEG, NEG, ALU.mult, ALU.add).then_inc(S("u"), 1)
            v.tensor_scalar(js[:, 0, :], js[:, 0, :], -NEG, NEG, ALU.mult, ALU.add).then_inc(S("u"), 1)
            dve.wait_ge(S("u"), 12)
            v.tensor_tensor_scan(jm[:, 1:], js[:, 1, :], Mm, jm[:, 0:1], ALU.add, ALU.max).then_inc(S("u"), 1)
            dve.wait_ge(S("u"), 13)
            v.tensor_tensor(js[:, 2, :], jm[:, 0:128], jm[:, 1:], ALU.subtract).then_inc(S("u"), 1)
            v.tensor_tensor(js[:, 3, :], Mm, jm[:, 1:], ALU.subtract).then_inc(S("u"), 1)
            dve.wait_ge(S("u"), 15)
            v.tensor_tensor(js[:, 2, :], js[:, 2, :], js[:, 1, :], ALU.add).then_inc(S("join_x"), 1)
            dve.wait_ge(S("join_e"), 1)
            v.tensor_tensor(js[:, 6, :], js[:, 5, :], Ss, ALU.mult).then_inc(S("u"), 1)
            dve.wait_ge(S("u"), 16)
            v.tensor_tensor_scan(jx[:, 1:], js[:, 4, :], js[:, 6, :], jx[:, 0:1], ALU.mult, ALU.add).then_inc(S("carry_rows"), 1)
            v.tensor_tensor(jm[:, 0:128], jm[:, 0:128], js[:, 0, :], ALU.add).then_inc(S("carry_rows"), 1)
            dve.wait_ge(S("carry_ps"), 1)
            v.tensor_copy(jc[:, :, :].rearrange("p k c -> p (k c)"), hps[0][:, 0:2 * CH]).then_inc(S("u"), 1)
            dve.wait_ge(S("row_in"), 16)
            v.tensor_copy(jr[:, 5, 0:16].rearrange("p (h e) -> p h e", e=4), row[:, CH:].unsqueeze(2).broadcast_to([128, HEADS, 4])).then_inc(S("u"), 1)
            v.tensor_copy(jr[:, 5, 16:CH], row[:, CH:]).then_inc(S("u"), 1)
            dve.wait_ge(S("u"), 19)
            v.tensor_tensor(jr[:, 0, :], jr[:, 5, :], jc[:, 0, :], ALU.max).then_inc(S("u"), 1)
            dve.wait_ge(S("u"), 20)
            v.tensor_tensor(jr[:, 1, :], jr[:, 5, :], jr[:, 0, :], ALU.subtract).then_inc(S("row_x"), 1)
            v.tensor_tensor(jr[:, 2, :], jc[:, 0, :], jr[:, 0, :], ALU.subtract).then_inc(S("row_x"), 1)
            dve.wait_ge(S("row_e"), 1)
            v.tensor_tensor(jr[:, 3, :], jr[:, 3, :], row[:, 0:CH], ALU.mult).then_inc(S("u"), 1)
            v.tensor_tensor(jr[:, 4, :], jr[:, 4, :], jc[:, 1, :], ALU.mult).then_inc(S("u"), 1)
            dve.wait_ge(S("u"), 22)
            v.tensor_tensor(rowo[:, 0:CH], jr[:, 3, :], jr[:, 4, :], ALU.add).then_inc(S("row_joined"), 1)
            v.tensor_copy(rowo[:, CH:], jr[:, 0, 16:CH]).then_inc(S("row_joined"), 1)
    n.release()


def mix_experts(nc, d, end_i, count):
    ctx = ExitStack()
    with ctx:
        n = Names(nc, ctx, "mix")
        S = n.sem
        seg = n.sb("segment_rows", [128, B, CH + HEADS])
        CUTS = [0, 24, 56, 88, 112, B]
        chunks = [slice(CUTS[q], CUTS[q + 1]) for q in range(len(CUTS) - 1)]
        y = n.sb("expert_outputs", [128, B, EXPERTS, LAT])
        h = n.sb("tokens", [128, B, LAT])
        own = n.sb("own_row", [128, B, CH])
        dst = n.sb("own_dst_scores", [128, B, HEADS])
        vec = n.sb("gain_shift_bias", [128, 3, 16])
        loop = n.sb("loop_score", [128, B, HEADS])
        top = n.sb("max_score", [128, B, HEADS])
        w = n.sb("edge_and_loop_weight", [128, 2, B, HEADS])
        one = n.sb("of_each_node", [128, 4, B])
        con = n.sb("minus_half_each", [128, 1, B])
        block = ctx.enter_context(nc.Block())
        by_head = lambda a: a.rearrange("p b (h e) -> p b h e", e=EXPERTS)

        @block.sync
        def _(sp):
            sp.dma_start(own[:, :, :], d["node_src"].rearrange("(b t) c -> t b c", t=128)).then_inc(S("rows_in"), 16)
            sp.dma_start(dst[:, :, :], d["node_dst"].rearrange("(b t) c -> t b c", t=128)).then_inc(S("rows_in"), 16)
            for k, name in enumerate(("score_gain", "score_shift", "score_bias")):
                sp.dma_start(vec[:, k, :], d[name].partition_broadcast(128)).then_inc(S("rows_in"), 16)
            for q, b in enumerate(chunks):
                if q:
                    sp.wait_ge(S(f"ends{q - 1}"), 16 * (chunks[q - 1].stop - chunks[q - 1].start))
                sp.dma_start(h[:, b, :], d["h2"].rearrange("t (b c) -> t b c", c=LAT)[:, b, :]).then_inc(S(f"h_in{q}"), 16)
                sp.dma_start(y[:, b, :, :].rearrange("t b e c -> t b (e c)"), d["expert_out"][:, b, :]).then_inc(S(f"y_in{q}"), 16)
            for g in range(G):
                sp.wait_ge(S(f"mixed{g}"), 4)
                sp.dma_start(d["out"][g * GB:(g + 1) * GB].rearrange("b t c -> t b c"), h[:, g * GB:(g + 1) * GB, :]).then_inc(S("out"), 16)
            sp.wait_ge(S("out"), 16 * G)

        def group(g):
            return slice(g * GB, (g + 1) * GB)

        def last_group(b):
            return b.stop // GB - 1

        @block.vector
        def _(dve):
            v = nc.vector
            count_ops = [0]

            def did(i):
                i.then_inc(S("node"), 1)
                count_ops[0] += 1

            def ready():
                dve.wait_ge(S("node"), count_ops[0])

            def mix(g, weighted=False):
                b, done = group(g), S(f"mixed{g}")
                if weighted:
                    dve.wait_ge(done, 1)
                else:
                    v.tensor_tensor(y[:, b], y[:, b], top[:, b, :].unsqueeze(3).broadcast_to([128, GB, EXPERTS, LAT]), ALU.mult).then_inc(done, 1)
                    dve.wait_ge(done, 1)
                v.tensor_tensor(y[:, b, 0:2], y[:, b, 0:2], y[:, b, 2:4], ALU.add).then_inc(done, 1)
                dve.wait_ge(done, 2)
                v.tensor_tensor(y[:, b, 0], y[:, b, 0], y[:, b, 1], ALU.add).then_inc(done, 1)
                dve.wait_ge(done, 3)
                v.tensor_tensor(h[:, b, :], h[:, b, :], y[:, b, 0], ALU.add).then_inc(done, 1)

            def gates(q, b):
                nb = b.stop - b.start
                wide16 = lambda a: a.unsqueeze(2).broadcast_to([128, nb, 16])
                wide4 = lambda a: a.unsqueeze(2).broadcast_to([128, nb, EXPERTS])
                each = lambda a: a.unsqueeze(1).broadcast_to([128, nb, 16])
                over_experts = lambda a: a.unsqueeze(3).broadcast_to([128, nb, HEADS, EXPERTS])
                sums, total, seg_max = seg[:, b, 0:16], seg[:, b, 16:20], seg[:, b, 20:24]
                pen, mean, var, rstd = (one[:, k, b] for k in range(4))
                did(v.tensor_scalar(pen, count[:, b], 0.0, NEG, ALU.is_equal, ALU.mult))
                dve.wait_ge(S("rows_in"), 16 * 5)
                did(v.tensor_tensor(loop[:, b, :], own[:, b, 0:4], dst[:, b, :], ALU.add))
                ready()
                did(v.scalar_tensor_tensor(loop[:, b, :], loop[:, b, :], 0.2, loop[:, b, :], ALU.mult, ALU.max))
                dve.wait_ge(S(f"ends{q}"), 16 * nb)
                did(v.tensor_tensor(w[:, 0, b, :], seg_max, wide4(pen), ALU.add))
                ready()
                did(v.tensor_tensor(top[:, b, :], w[:, 0, b, :], loop[:, b, :], ALU.max))
                ready()
                did(v.tensor_tensor(w[:, 0, b, :], w[:, 0, b, :], top[:, b, :], ALU.subtract))
                v.tensor_tensor(w[:, 1, b, :], loop[:, b, :], top[:, b, :], ALU.subtract).then_inc(S("exponents"), 1)
                ready()
                v.tensor_copy(mean, pen).then_inc(S("exponents"), 1)
                dve.wait_ge(S("weights"), 2 * q + 1)
                did(v.tensor_tensor(by_head(sums), by_head(sums), over_experts(w[:, 0, b, :]), ALU.mult))
                did(v.tensor_tensor(by_head(own[:, b, 4:20]), by_head(own[:, b, 4:20]), over_experts(w[:, 1, b, :]), ALU.mult))
                did(v.tensor_tensor(loop[:, b, :], total, w[:, 0, b, :], ALU.mult))
                ready()
                did(v.tensor_tensor(loop[:, b, :], loop[:, b, :], w[:, 1, b, :], ALU.add))
                did(v.tensor_tensor(sums, sums, own[:, b, 4:20], ALU.add))
                ready()
                did(v.tensor_scalar(loop[:, b, :], loop[:, b, :], 1e-16, None, ALU.add))
                ready()
                did(v.reciprocal(loop[:, b, :], loop[:, b, :]))
                ready()
                did(v.tensor_tensor(by_head(sums), by_head(sums), over_experts(loop[:, b, :]), ALU.mult))
                ready()
                did(v.tensor_tensor(sums, sums, each(vec[:, 2, :]), ALU.add))
                ready()
                did(v.tensor_reduce(mean, sums, AX.X, ALU.add))
                ready()
                did(v.tensor_scalar(mean, mean, 1.0 / 16, None, ALU.mult))
                ready()
                did(v.tensor_tensor(sums, sums, wide16(mean), ALU.subtract))
                ready()
                did(v.tensor_tensor(own[:, b, 4:20], sums, sums, ALU.mult))
                ready()
                did(v.tensor_reduce(var, own[:, b, 4:20], AX.X, ALU.add))
                ready()
                v.tensor_scalar(var, var, 1.0 / 16, EPS, ALU.mult, ALU.add).then_inc(S("variance"), 1)
                if q:
                    mix(last_group(chunks[q - 1]), weighted=True)
                dve.wait_ge(S("rstd"), q + 1)
                did(v.tensor_tensor(sums, sums, wide16(rstd), ALU.mult))
                ready()
                did(v.tensor_tensor(sums, sums, each(vec[:, 0, :]), ALU.mult))
                ready()
                did(v.tensor_tensor(sums, sums, each(vec[:, 1, :]), ALU.add))
                ready()
                score = loop[:, b, :]
                did(v.tensor_reduce(score, sums.rearrange("p b (h e) -> p b e h", e=EXPERTS), AX.X, ALU.add))
                ready()
                did(v.tensor_scalar(score, score, 1.0 / HEADS, None, ALU.mult))
                ready()
                beats = own[:, b, 4:20].rearrange("p b (i j) -> p b i j", j=EXPERTS)
                for i in range(EXPERTS):
                    for j in range(EXPERTS):
                        op = ALU.is_gt if j <= i else ALU.is_ge
                        did(v.tensor_tensor(beats[:, :, i, j], score[:, :, i], score[:, :, j], op))
                did(v.tensor_reduce(mean, score, AX.X, ALU.max))
                ready()
                did(v.tensor_reduce(dst[:, b, :], beats, AX.X, ALU.add))
                v.tensor_tensor(w[:, 0, b, :], score, wide4(mean), ALU.subtract).then_inc(S("exponents"), 1)
                ready()
                did(v.tensor_scalar(dst[:, b, :], dst[:, b, :], 2.0, None, ALU.is_ge))
                dve.wait_ge(S("weights"), 2 * q + 2)
                ready()
                did(v.tensor_tensor(w[:, 0, b, :], w[:, 0, b, :], dst[:, b, :], ALU.mult))
                ready()
                did(v.tensor_reduce(var, w[:, 0, b, :], AX.X, ALU.add))
                ready()
                did(v.reciprocal(var, var))
                ready()
                did(v.tensor_tensor(top[:, b, :], w[:, 0, b, :], wide4(var), ALU.mult))

            for q, b in enumerate(chunks):
                gates(q, b)
                ready()
                dve.wait_ge(S(f"h_in{q}"), 16)
                dve.wait_ge(S(f"y_in{q}"), 16)
                v.tensor_copy(one[:, 0, b], one[:, 2, b]).then_inc(S("mix_weights"), 1)
                for g in range(b.start // GB, last_group(b)):
                    mix(g)
            mix(last_group(chunks[-1]), weighted=True)

        @block.scalar
        def _(act):
            for q, b in enumerate(chunks):
                act.wait_ge(S("exponents"), 3 * q + 2)
                act.activation(w[:, :, b, :], w[:, :, b, :], ACT.Exp).then_inc(S("weights"), 1)
                act.wait_ge(S("exponents"), 3 * q + 3)
                act.activation(w[:, 0, b, :], w[:, 0, b, :], ACT.Exp).then_inc(S("weights"), 1)
                act.wait_ge(S("mix_weights"), q + 1)
                act.wait_ge(S(f"y_in{q}"), 16)
                for sample in range(last_group(b) * GB, b.stop):
                    for ex in range(EXPERTS):
                        m = act.activation(y[:, sample, ex, :], y[:, sample, ex, :], ACT.Identity, scale=top[:, sample, ex:ex + 1])
                m.then_inc(S(f"mixed{last_group(b)}"), 1)

        @block.gpsimd
        def _(pool):
            pool.memset(con[:, 0, :], -0.5).then_inc(S("pow_constant"), 1)
            pool.wait_ge(S("pow_constant"), 1)

            MEANWHILE = 14

            def fetch(q, first, last=B):
                for b in range(chunks[q].start, chunks[q].stop)[first:last]:
                    pool.indirect_dma_start(seg[:, b, :], None, d["edge_state"], bass.IndirectOffsetOnAxis(ap=end_i[:, b:b + 1], axis=0))\
                        .then_inc(S(f"ends{q}"), 16)

            fetch(0, 0)
            for q, b in enumerate(chunks):
                if q + 1 < len(chunks):
                    fetch(q + 1, 0, MEANWHILE)
                pool.wait_ge(S("variance"), q + 1)
                nc.gpsimd.tensor_tensor(one[:, 3, b], one[:, 2, b], con[:, 0, b], ALU.pow).then_inc(S("rstd"), 1)
                if q + 1 < len(chunks):
                    fetch(q + 1, MEANWHILE)


def program(nc, d):
    for name, shape in (("res", (T, B, 2 * J)), ("h2", (128, B * LAT)), ("zT", (128, G * GB // 2 * 128)), ("node_src", (NODES, CH)), ("node_dst", (NODES, HEADS)),
                        ("dst_at_start", (EDGES, HEADS)), ("edge_state", (EDGES, CH + HEADS)), ("expert_out", (128, B, EXPERTS * LAT))):
        d[name] = nc.dram_tensor(f"scratch_{name}", shape, F32, kind="Internal").ap()
    with ExitStack() as outer:
        end_i = outer.enter_context(nc.sbuf_tensor("end_index", [128, B], U32))
        count = outer.enter_context(nc.sbuf_tensor("edge_count", [128, B], F32))
        with ExitStack() as ctx:
            keys = [ctx.enter_context(nc.sbuf_tensor(f"keys{i}", [128, EP], F32)) for i in range(2)]
            cur = tokenizer_and_sort(nc, d, keys)
            attention(nc, d)
            graph(nc, d, keys, cur, end_i, count)
        mix_experts(nc, d, end_i, count)


def kernel(**inputs):
    from concourse import bacc
    from concourse.bass_utils import run_bass_kernel_spmd

    def tok(name):
        return inputs["L0_tok_" + name]

    def att(name):
        return inputs["L0_attn_" + name]

    def ffn(name):
        return inputs["L0_ffn_" + name]

    def twice(a):
        return np.concatenate([a, a], 0)

    def diagonal(a):
        z = np.zeros_like(a)
        return np.block([[a, z], [z, a]])

    arrays = constants()
    arrays["x"] = inputs["x"].transpose(1, 0, 3, 2).reshape(T, B, D * J)
    arrays["edges"] = ffn("edge_index")
    arrays["conv1_w"] = tok("conv1_w").transpose(1, 2, 3, 0)
    arrays["conv2_w"] = tok("conv2_w").transpose(1, 2, 3, 0)
    arrays["conv3_w"] = tok("conv3_w").reshape(2, T, T, KH, 2).transpose(2, 3, 4, 0, 1)
    arrays["conv_b"] = np.concatenate([tok("conv1_b"), tok("conv2_b"), tok("conv3_b")]).reshape(4, T).T
    for v in "gb":
        arrays[f"ln0_{v}"] = tok(f"ln0_{v}").reshape(J, D).T.reshape(-1)
        arrays[f"ln1_{v}0"] = tok(f"ln1_{v}").reshape(J, 2).T.reshape(-1)
        arrays[f"ln1_{v}1"] = tok(f"ln1_{v}")
    arrays["out_w"], arrays["out_b"] = tok("out_w"), tok("out_b")
    arrays["w_qkv"] = np.stack([diagonal(att("Wq").T), diagonal(att("Wkv").T)], 1)
    arrays["w_proj"] = diagonal(att("Wproj").T)
    arrays["w_mlp1"] = twice(att("W1").T)
    arrays["w_mlp2"] = att("W2").T.reshape(2, 128, LAT).transpose(1, 0, 2)
    arrays["w_gat"] = twice(ffn("W_gat"))
    arrays["norm_cols"] = np.stack([twice(att(v)) for v in ("norm1_g", "norm1_b", "norm2_g", "norm2_b")] + list(att("b1").reshape(2, 128)), 1)
    arrays["proj_b"], arrays["mlp_b"] = att("bproj"), att("b2")
    arrays["att0"], arrays["att1"] = ffn("att_src").reshape(-1), ffn("att_dst").reshape(-1)
    arrays["w_expert1"] = twice(ffn("W1").transpose(1, 0, 2))
    arrays["w_expert2"] = ffn("W2").transpose(1, 0, 2)
    arrays["b_expert1"], arrays["b_expert2"] = ffn("b1").T, ffn("b2").reshape(-1)
    arrays["score_gain"], arrays["score_shift"], arrays["score_bias"] = ffn("ln_gamma"), ffn("ln_beta"), ffn("b_gat")

    nc = bacc.Bacc("TRN2", target_bir_lowering=False, num_devices=1)
    given, d = {}, {}
    for name, a in arrays.items():
        a = np.ascontiguousarray(a)
        given[f"in_{name}_dram"] = a
        d[name] = nc.dram_tensor(f"in_{name}_dram", a.shape, mybir.dt.from_np(a.dtype), kind="ExternalInput").ap()
    d["out"] = nc.dram_tensor("out_0_dram", (B, T, LAT), F32, kind="ExternalOutput").ap()
    program(nc, d)
    result = run_bass_kernel_spmd(nc, [given], core_ids=[0])
    return result.results[0]["out_0_dram"]
```
